# Optimizing a Trainium2 kernel written in Bass

```python
import numpy as np
import jax
import jax.numpy as jnp

def _softmax(x, axis=-1):
    return jax.nn.softmax(x, axis=axis)

def _gelu(x):
    return jax.nn.gelu(x, approximate=True)

def _silu(x):
    return jax.nn.silu(x)

def _sigmoid(x):
    return jax.nn.sigmoid(x)

def _layernorm(x, axis=-1, eps=1e-05):
    m = jnp.mean(x, axis=axis, keepdims=True)
    v = jnp.var(x, axis=axis, keepdims=True)
    return (x - m) / jnp.sqrt(v + eps)

def _scatter_add(tgt, idx, src, axis=0):
    return tgt.at[idx].add(src)

def _segment_sum(src, seg, n):
    return jax.ops.segment_sum(src, seg, n)
kernel_name = 'mk_seq_postln_d1_jaxref_r8_f19701'

def setup_inputs(seed: int=0):
    np.random.seed(seed)
    _w = jnp.asarray

    def _L0_attn_setup():
        import jax, jax.numpy as jnp
        import numpy as np
        B, T, D, N = (4, 128, 128, 16)

        def _depthwise_conv3_same(x, w, b):
            xp = jnp.pad(x, ((0, 0), (1, 1), (0, 0)))
            return xp[:, :-2] * w[:, 0] + xp[:, 1:-1] * w[:, 1] + xp[:, 2:] * w[:, 2] + b

        def _selective_scan(x, A, Wb, bb, Wc, bc, Wdt, bdt):
            dt = jax.nn.softplus(x @ Wdt + bdt)
            Bm = x @ Wb + bb
            Cm = x @ Wc + bc
            dA = jnp.exp(dt[..., None] * A)
            dBx = dt[..., None] * Bm[:, :, None, :] * x[..., None]

            def step(h, ins):
                dA_t, dBx_t, C_t = ins
                h = dA_t * h + dBx_t
                y = jnp.einsum('bdn,bn->bd', h, C_t)
                return (h, y)
            h0 = jnp.zeros((x.shape[0], x.shape[2], A.shape[1]), x.dtype)
            _, ys = jax.lax.scan(step, h0, (dA.transpose(1, 0, 2, 3), dBx.transpose(1, 0, 2, 3), Cm.transpose(1, 0, 2)))
            return ys.transpose(1, 0, 2)
        key = jax.random.key(seed)
        ks = jax.random.split(key, 16)
        s = 1.0 / np.sqrt(D)
        inp = {'u': jax.random.normal(ks[0], (B, T, D), jnp.float32), 'Win': jax.random.normal(ks[1], (D, D), jnp.float32) * s, 'b_in': jnp.zeros((D,), jnp.float32), 'Wg': jax.random.normal(ks[2], (D, D), jnp.float32) * s, 'bg': jnp.zeros((D,), jnp.float32), 'Wout': jax.random.normal(ks[3], (D, D), jnp.float32) * s, 'bout': jnp.zeros((D,), jnp.float32), 'convw': jax.random.normal(ks[4], (D, 3), jnp.float32) * 0.5, 'convb': jnp.zeros((D,), jnp.float32), 'A': -jnp.exp(jax.random.normal(ks[5], (D, N), jnp.float32) * 0.5), 'Wb': jax.random.normal(ks[6], (D, N), jnp.float32) * s, 'bb': jnp.zeros((N,), jnp.float32), 'Wc': jax.random.normal(ks[7], (D, N), jnp.float32) * s, 'bc': jnp.zeros((N,), jnp.float32), 'Wdt': jax.random.normal(ks[8], (D, D), jnp.float32) * s, 'bdt': jnp.full((D,), -2.0, jnp.float32)}
        return inp
    _L0_attn_in = _L0_attn_setup()

    def _L0_ffn_setup():
        import jax, jax.numpy as jnp
        import numpy as np
        EMB_DIM = 128
        HIDDEN = int(2 / 3 * 4 * EMB_DIM)
        NUM_EXPERTS = 8
        TOP_K = 2
        B, S = (4, 128)
        key = jax.random.key(seed)
        ks = jax.random.split(key, 5)
        sc = 1.0 / np.sqrt(EMB_DIM)
        sh = 1.0 / np.sqrt(HIDDEN)
        return {'x': jax.random.normal(ks[0], (B, S, EMB_DIM), dtype=jnp.float32), 'Wg': jax.random.normal(ks[1], (NUM_EXPERTS, EMB_DIM), dtype=jnp.float32) * sc, 'W1': jax.random.normal(ks[2], (NUM_EXPERTS, HIDDEN, EMB_DIM), dtype=jnp.float32) * sc, 'W2': jax.random.normal(ks[3], (NUM_EXPERTS, HIDDEN, EMB_DIM), dtype=jnp.float32) * sc, 'W3': jax.random.normal(ks[4], (NUM_EXPERTS, EMB_DIM, HIDDEN), dtype=jnp.float32) * sh}
    _L0_ffn_in = _L0_ffn_setup()
    _d = {'L0_attn_u': _L0_attn_in['u'], 'L0_attn_Win': _L0_attn_in['Win'], 'L0_attn_b_in': _L0_attn_in['b_in'], 'L0_attn_Wg': _L0_attn_in['Wg'], 'L0_attn_bg': _L0_attn_in['bg'], 'L0_attn_Wout': _L0_attn_in['Wout'], 'L0_attn_bout': _L0_attn_in['bout'], 'L0_attn_convw': _L0_attn_in['convw'], 'L0_attn_convb': _L0_attn_in['convb'], 'L0_attn_A': _L0_attn_in['A'], 'L0_attn_Wb': _L0_attn_in['Wb'], 'L0_attn_bb': _L0_attn_in['bb'], 'L0_attn_Wc': _L0_attn_in['Wc'], 'L0_attn_bc': _L0_attn_in['bc'], 'L0_attn_Wdt': _L0_attn_in['Wdt'], 'L0_attn_bdt': _L0_attn_in['bdt'], 'L0_ffn_Wg': _L0_ffn_in['Wg'], 'L0_ffn_W1': _L0_ffn_in['W1'], 'L0_ffn_W2': _L0_ffn_in['W2'], 'L0_ffn_W3': _L0_ffn_in['W3']}
    _x0 = _d['L0_attn_u']
    _d['L0_attn_u'] = jax.random.normal(jax.random.fold_in(jax.random.key(seed), 1), (8, 1024, 128), dtype=_x0.dtype)
    del _x0
    return _d

def reference(L0_attn_u, L0_attn_Win, L0_attn_b_in, L0_attn_Wg, L0_attn_bg, L0_attn_Wout, L0_attn_bout, L0_attn_convw, L0_attn_convb, L0_attn_A, L0_attn_Wb, L0_attn_bb, L0_attn_Wc, L0_attn_bc, L0_attn_Wdt, L0_attn_bdt, L0_ffn_Wg, L0_ffn_W1, L0_ffn_W2, L0_ffn_W3):

    def _L0_attn_ref(u, Win, b_in, Wg, bg, Wout, bout, convw, convb, A, Wb, bb, Wc, bc, Wdt, bdt):
        import jax, jax.numpy as jnp
        import numpy as np
        B, T, D, N = (4, 128, 128, 16)

        def _depthwise_conv3_same(x, w, b):
            xp = jnp.pad(x, ((0, 0), (1, 1), (0, 0)))
            return xp[:, :-2] * w[:, 0] + xp[:, 1:-1] * w[:, 1] + xp[:, 2:] * w[:, 2] + b

        def _selective_scan(x, A, Wb, bb, Wc, bc, Wdt, bdt):
            dt = jax.nn.softplus(x @ Wdt + bdt)
            Bm = x @ Wb + bb
            Cm = x @ Wc + bc
            dA = jnp.exp(dt[..., None] * A)
            dBx = dt[..., None] * Bm[:, :, None, :] * x[..., None]

            def step(h, ins):
                dA_t, dBx_t, C_t = ins
                h = dA_t * h + dBx_t
                y = jnp.einsum('bdn,bn->bd', h, C_t)
                return (h, y)
            h0 = jnp.zeros((x.shape[0], x.shape[2], A.shape[1]), x.dtype)
            _, ys = jax.lax.scan(step, h0, (dA.transpose(1, 0, 2, 3), dBx.transpose(1, 0, 2, 3), Cm.transpose(1, 0, 2)))
            return ys.transpose(1, 0, 2)
        x = u @ Win + b_in
        x = _depthwise_conv3_same(x, convw, convb)
        x = jax.nn.silu(x)
        x_ssm = _selective_scan(x, A, Wb, bb, Wc, bc, Wdt, bdt)
        z = jax.nn.silu(u @ Wg + bg)
        return x_ssm * z @ Wout + bout

    def _L0_ffn_ref(x, Wg, W1, W2, W3):
        import jax, jax.numpy as jnp
        import numpy as np
        EMB_DIM = 128
        HIDDEN = int(2 / 3 * 4 * EMB_DIM)
        NUM_EXPERTS = 8
        TOP_K = 2
        B, S = (4, 128)
        gate_logits = jnp.einsum('bsd,ed->bse', x, Wg)
        top_v, top_i = jax.lax.top_k(gate_logits, TOP_K)
        mask = jnp.any(top_i[..., :, None] == jnp.arange(NUM_EXPERTS), axis=-2)
        sparse_logits = jnp.where(mask, gate_logits, -jnp.inf)
        gating = jax.nn.softmax(sparse_logits, axis=-1)
        h1 = jnp.einsum('bsd,ehd->bseh', x, W1)
        h2 = jnp.einsum('bsd,ehd->bseh', x, W2)
        hidden = jax.nn.silu(h1) * h2
        expert_out = jnp.einsum('bseh,edh->bsed', hidden, W3)
        return jnp.einsum('bsed,bse->bsd', expert_out, gating)
    x = L0_attn_u
    x = _layernorm(x + _L0_attn_ref(x, L0_attn_Win, L0_attn_b_in, L0_attn_Wg, L0_attn_bg, L0_attn_Wout, L0_attn_bout, L0_attn_convw, L0_attn_convb, L0_attn_A, L0_attn_Wb, L0_attn_bb, L0_attn_Wc, L0_attn_bc, L0_attn_Wdt, L0_attn_bdt), axis=-1)
    x = _layernorm(x + _L0_ffn_ref(x, L0_ffn_Wg, L0_ffn_W1, L0_ffn_W2, L0_ffn_W3), axis=-1)
    return x

_drawn_inputs = setup_inputs


def setup_inputs(seed=0):
    import zlib

    import numpy as np

    out = dict(_drawn_inputs(seed))
    spreads = {'L0_attn_b_in': (0.0, 0.1),
     'L0_attn_bg': (0.0, 0.1),
     'L0_attn_bout': (0.0, 0.1),
     'L0_attn_convb': (0.0, 0.1),
     'L0_attn_bb': (0.0, 0.1),
     'L0_attn_bc': (0.0, 0.1),
     'L0_attn_bdt': (-2.0, 0.2)}
    factors = {}
    for name, (base, spread) in spreads.items():
        noise = np.random.default_rng([zlib.crc32(name.encode()), seed]).standard_normal(out[name].shape)
        drawn = base * np.exp(spread * noise) if base else spread * noise
        out[name] = jnp.asarray(drawn.astype(out[name].dtype))
    for name, factor in factors.items():
        out[name] = (out[name] * factor).astype(out[name].dtype)
    return out
```

```python
from contextlib import ExitStack

import concourse.bass as bass
from concourse import mybir

F32 = mybir.dt.float32
F32R = mybir.dt.float32r
ALU = mybir.AluOpType
ACT = mybir.ActivationFunctionType
AX = mybir.AxisListType

P = 128
EXP_LN = "natural_log_exp_and_others"
HALF = 512
I32 = mybir.dt.int32
U32 = mybir.dt.uint32
LAG = 3
RING = 4
PAIR = 2


def wait(eng, sem, value):
    if not isinstance(value, int) or value > 0:
        eng.wait_ge(sem, value)


def build(nc, u, Win, b_in, Wg, bg, Wout, bout, convw, convb, A, Wb, bb, Wc, bc, Wdt, bdt,
          Wgate, W1, W2, W3, out):
    B, T, D = u.shape
    N = A.shape[1]
    NT = T // P
    E, H, _ = W1.shape
    HC = -(-H // P)
    HP = HC * P
    assert E == NT and E * H % 2 == 0

    group_of = [0] * (B - 2) + [1] * 2
    tokens = [group_of.count(g) * T for g in range(2)]
    region = [t + P for t in tokens]
    first_tile = [0, E * region[0] // P]
    tiles = first_tile[1] + E * region[1] // P
    slots = [-(-((2 * t + E * (P - 1)) // P) // RING) * RING for t in tokens]
    first_slot = [0, slots[0]]
    S = sum(slots)
    assert D == P and T == 2 * HALF and N == 16

    with ExitStack() as ctx:
        def sb(name, shape, dt=F32):
            return ctx.enter_context(nc.sbuf_tensor(name, shape, dt))

        def ps(name, shape, dt=F32):
            return ctx.enter_context(nc.psum_tensor(name, shape, dt))

        def sem(name):
            return ctx.enter_context(nc.semaphore(name))

        ident = sb("ident", [P, P])
        eps_c = sb("eps_c", [P, 1])
        zeros = sb("zeros", [P, P])
        RB = -(-E * H // P)
        raw = sb("raw", [P, 2 * RB + E * HC, D])
        raw1 = raw[:, 0:RB, :]
        raw2 = raw[:, RB:2 * RB, :]
        raw3 = raw[:, 2 * RB:, :].rearrange("p (e c) h -> p e (c h)", e=E)
        x1_row = [sb(f"x1_row{i}", [P, NT, D]) for i in range(2)]
        place = [sb(f"place{i}", [P, 2, NT], U32) for i in range(2)]
        places = sb("places", [P, 2, B * NT])
        gap = sb("gap", [P, B * NT])
        gate1 = sb("gate1", [P, B * NT])
        gate2 = sb("gate2", [P, B * NT])
        base_from = [sb(f"base_from{g}", [P, E]) for g in range(2)]
        base = [sb(f"base{g}", [P, E]) for g in range(2)]
        pad_place = [sb(f"pad_place{g}", [P, E], U32) for g in range(2)]
        slot_expert = sb("slot_expert", [1, S], I32)
        slot_from = sb("slot_from", [1, S], I32)
        skip = [sb(f"skip{g}", [P, E]) for g in range(2)]
        stats = sb("stats", [P, NT, 6])
        mean = sb("mean", [P, NT])
        dif = sb("dif", [P, NT])
        sq = sb("sq", [P, NT])
        var = sb("var", [P, NT])
        lnv = sb("lnv", [P, NT])
        rstd = sb("rstd", [P, NT])

        own = ctx.enter_context(ExitStack())

        def sb(name, shape, dt=F32):
            return own.enter_context(nc.sbuf_tensor(name, shape, dt))

        win = sb("win", [P, D])
        wg = sb("wg", [P, D])
        wdt = sb("wdt", [P, D])
        wout = sb("wout", [P, D])
        wbc = sb("wbc", [P, 4 * N])
        a_dn = sb("a_dn", [P, N])
        b_in_c = sb("b_in_c", [P, 1])
        bg_c = sb("bg_c", [P, 1])
        bdt_c = sb("bdt_c", [P, 1])
        cw = sb("cw", [P, 3])
        cb = sb("cb", [P, 1])
        bbc_c = sb("bbc_c", [4 * N, 1])
        bout_r = sb("bout_r", [1, HALF])
        ones_r = sb("ones_r", [1, P])
        pick = sb("pick", [4 * N, 2 * N, P], F32R)

        u_in = sb("u_in", [P, NT, D])
        u_res = sb("u_res", [P, NT, D])
        u_t = sb("u_t", [P, T])
        x_pad = sb("x_pad", [P, T + 2])
        xs = sb("xs", [P, T])
        z = [sb(f"z{i}", [P, T]) for i in range(2)]
        dt_abs = sb("dt_abs", [P, T])
        dt_relu = sb("dt_relu", [P, T])
        dt = [sb(f"dt{i}", [P, T]) for i in range(2)]
        dtx = [sb(f"dtx{i}", [P, T]) for i in range(2)]
        bc_val = sb("bc_val", [4 * N, T])
        bc_split = [sb(f"bc_split{i}", [4 * N, T], F32R) for i in range(2)]
        decay = sb("decay", [P, PAIR, T])
        drive = sb("drive", [P, PAIR, T])
        state = sb("state", [P, RING, T])
        c_all = sb("c_all", [P, PAIR, T])
        prod = sb("prod", [P, RING, T])
        yz = sb("yz", [P, T])
        res = sb("res", [P, NT, D])
        x1_t = yz
        wgate_t = sb("wgate_t", [P, E])
        wgate = sb("wgate", [E, D])
        before = sb("before", [P, P])
        ones = sb("ones", [P, P])
        first_high = sb("first_high", [P, E, NT])
        logit = sb("logit", [P, E, NT])
        logit2 = sb("logit2", [P, E, NT])
        top1 = sb("top1", [P, E, NT])
        top2 = sb("top2", [P, E, NT])
        chosen = sb("chosen", [P, E, NT])
        rank = sb("rank", [P, E, NT])
        part = sb("part", [P, E, NT])
        best = sb("best", [P, NT])
        place_f = sb("place_f", [P, 2, NT])
        best2 = sb("best2", [P, NT])
        index = sb("index", [P, NT])
        running = sb("running", [P, E * NT + 1])
        count = sb("count", [P, E])
        offset = sb("offset", [P, E])
        lane = sb("lane", [P, 1])
        SM = max(slots)
        slot_no = sb("slot_no", [1, SM])
        n_tiles = sb("n_tiles", [P, E])
        n_tiles_i = sb("n_tiles_i", [P, E], I32)
        done_at = sb("done_at", [P, E])
        passed = sb("passed", [1, SM, E])
        t_expert = sb("t_expert", [1, SM])
        t_tile = sb("t_tile", [1, SM])
        t_used = sb("t_used", [1, SM])
        ones_e = sb("ones_e", [P, E])
        own.close()

        def sb(name, shape, dt=F32):
            return ctx.enter_context(nc.sbuf_tensor(name, shape, dt))

        EH = E * H + 2
        w1 = [sb(f"w1_{i}", [P, EH], F32R) for i in ("hi", "lo")]
        w2 = [sb(f"w2_{i}", [P, EH], F32R) for i in ("hi", "lo")]
        w3 = sb("w3", [P, E * HC, 2, P], F32R)
        x1 = sb("x1", [P, B * NT, D])
        y_got = [sb("y_got", [P, B * NT, D]), raw[:, 0:B * NT, :]]
        x_slot = sb("x_slot", [P, RING, D])
        x_hi = sb("x_hi", [P, 2, P], F32R)
        x_lo = sb("x_lo", [P, 2, P], F32R)
        act1 = sb("act1", [P, 2, H])
        hid = sb("hid", [P, 2, HP])
        hid_hi = sb("hid_hi", [P, HP], F32R)
        hid_lo = sb("hid_lo", [P, HP], F32R)
        y_slot = sb("y_slot", [P, RING, D])
        y_place = sb("y_place", [P, 2, B * NT], U32)
        y_sum = y_slot[:, 0:2, 0:B * NT]

        x1_rows = nc.dram_tensor("x1_rows", (B * T, D), F32, kind="Internal").ap()
        x_sorted = nc.dram_tensor("x_sorted", (tiles * P, D), F32, kind="Internal").ap()
        y_sorted = nc.dram_tensor("y_sorted", (S * P, D), F32, kind="Internal").ap()

        ps_b = ps("ps_b", [P, T])
        ps_c = ps("ps_c", [P, T])
        ps_y = ps("ps_y", [P, T])
        ps_s = ps("ps_s", [P, T])

        w_loaded = sem("w_loaded")
        const_ready = sem("const_ready")
        pick_ready = sem("pick_ready")
        u_loaded, ures_loaded = sem("u_loaded"), sem("ures_loaded")
        raw_loaded = sem("raw_loaded")
        x1_saved = [sem("x1_saved0"), sem("x1_saved1")]
        x1t_in, x1t_ready = sem("x1t_in"), sem("x1t_ready")
        logit_in, logit_ready = sem("logit_in"), sem("logit_ready")
        count_ready, rank_in, rank_drained = sem("count_ready"), sem("rank_in"), sem("rank_drained")
        place_ready, route_step = sem("place_ready"), sem("route_step")
        scattered = [[sem(f"scattered{g}{i}") for i in range(2)] for g in range(2)]
        padded = [sem(f"padded{g}") for g in range(2)]
        table_step, table_ready = sem("table_step"), sem("table_ready")
        wgate_in, wgate_ready = sem("wgate_in"), sem("wgate_ready")
        prep_in, prep_hi, prep_lo = sem("prep_in"), sem("prep_hi"), sem("prep_lo")
        result_step, y_place_ready = sem("result_step"), sem("y_place_ready")
        gap_exp, gate_step = sem("gap_exp"), sem("gate_step")
        xs_loaded = [sem(f"xs_loaded{i}") for i in range(RING)]
        xt_in, xhi_ready, xlo_ready = sem("xt_in"), sem("xhi_ready"), sem("xlo_ready")
        h1_in, h2_in, silu_ready, hid_ready = sem("h1_in"), sem("h2_in"), sem("silu_ready"), sem("hid_ready")
        ht_in, hthi_ready, htlo_ready = sem("ht_in"), sem("hthi_ready"), sem("htlo_ready")
        yo_in, ys_ready = sem("yo_in"), sem("ys_ready")
        y_saved = [sem(f"y_saved{i}") for i in range(RING)]
        x1_loaded = sem("x1_loaded")
        y_gathered = [sem(f"y_gathered{i}") for i in range(B)]
        mix_step, mix_ln, mix_rstd, mix_ready = sem("mix_step"), sem("mix_ln"), sem("mix_rstd"), sem("mix_ready")
        ut_in, ut_ready = sem("ut_in"), sem("ut_ready")
        x_in, xpad_ready = sem("x_in"), sem("xpad_ready")
        conv_part, conv_ready, xs_ready = sem("conv_part"), sem("conv_ready"), sem("xs_ready")
        z_in, z_ready = sem("z_in"), sem("z_ready")
        dt_in, dtabs_ready, dtrelu_ready = sem("dt_in"), sem("dtabs_ready"), sem("dtrelu_ready")
        dtexp_ready, dtln_ready, dt_ready, dtx_ready = sem("dtexp_ready"), sem("dtln_ready"), sem("dt_ready"), sem("dtx_ready")
        bc_in, bcval_ready, bchi_ready, bclo_ready = sem("bc_in"), sem("bcval_ready"), sem("bchi_ready"), sem("bclo_ready")
        bB_ready, bC_ready = sem("bB_ready"), sem("bC_ready")
        decay_ready, drive_ready, state_ready = sem("decay_ready"), sem("drive_ready"), sem("state_ready")
        c_ready, prod_ready, y_added = sem("c_ready"), sem("prod_ready"), sem("y_added")
        yz_ready, out_in, res_ready = sem("yz_ready"), sem("out_in"), sem("res_ready")
        stats_ready, agg_part, lnv_ready, rstd_ready, x1_ready = sem("stats_ready"), sem("agg_part"), sem("lnv_ready"), sem("rstd_ready"), sem("x1_ready")
        out_stored = sem("out_stored")

        u_v = u.rearrange("b (n p) d -> b p n d", p=P)
        out_v = out.rearrange("b (n p) d -> b p n d", p=P)
        x1_v = x1_rows.rearrange("(b n p) d -> b p n d", p=P, n=NT)
        col = lambda v: v.rearrange("(p o) -> p o", o=1)
        row = lambda v: v.rearrange("(o p) -> o p", o=1)
        weight_loads = (
            [(win[:], Win), (b_in_c[:], col(b_in)), (wg[:], Wg), (bg_c[:], col(bg)), (cw[:], convw), (cb[:], col(convb)),
             (wdt[:], Wdt), (bdt_c[:], col(bdt)), (a_dn[:], A), (wout[:], Wout)]
            + [(wbc[:, k * N:(k + 1) * N], (Wb, Wc)[k % 2]) for k in range(4)]
            + [(bbc_c[k * N:(k + 1) * N, :], col((bb, bc)[k % 2])) for k in range(4)]
            + [(wgate[:], Wgate)]
            + [(bout_r[:, k * D:(k + 1) * D], row(bout)) for k in range(4)])
        CONSTANTS = 22
        ROUTE = 21
        TABLE = 16
        MIX = 6
        WEIGHTS = 16 * len(weight_loads)

        block = ctx.enter_context(nc.Block())

        def rows(eng, body):
            body(0, 0, first=True, last=False)
            body(1, 1, first=False, last=False)
            with eng.Fori(0, 2) as pair:
                body(pair * 2 + 2, 0, first=False, last=False)
                body(pair * 2 + 3, 1, first=False, last=False)
            body(6, 0, first=False, last=False)
            body(7, 1, first=False, last=True)

        def all_slots(eng, slot, begin=lambda first, count: None):
            begin(0, RING + 1)
            for s in range(RING + 1):
                slot(s, s % RING, s // RING, s, first=s == 0, last=False)
            with eng.Fori(0, S // RING - 2) as i:
                begin(i * RING + RING, RING + 1)
                for k in range(1, RING + 1):
                    slot(i * RING + (RING + k), k % RING, i + (1 + k // RING), k, first=False, last=False)
            begin(S - RING, RING)
            for s in range(S - RING + 1, S):
                slot(s, s % RING, s // RING, s - (S - RING), first=False, last=s == S - 1)

        preps = ([(1, c, min(HALF, E * H - c), w1) for c in range(0, E * H, HALF)]
                 + [(2, c, min(HALF, E * H - c), w2) for c in range(0, E * H, HALF)]
                 + [(3, c, HALF, None) for c in range(0, E * HP, HALF)])

        def prep_part(i, part):
            kind, cols, width, dst = preps[i]
            if kind == 3:
                return w3[:, cols // P:(cols + width) // P, part, :]
            return dst[part][:, cols:cols + width]

        def prep_shape(i, t):
            return t.rearrange("p (k m) -> p k m", m=P) if preps[i][0] == 3 else t

        def prep_bank(i):
            return ps_y[:, (i % 2) * HALF:(i % 2 + 1) * HALF]

        HE = H + H % 2
        ps_h1 = ps_b[:, 0:HE]
        ps_h2 = ps_b[:, HALF:HALF + HE]
        ps_ht = ps_c[:, 0:HP]
        ps_xt = ps_s[:, 0:P]
        ps_yo = ps_s[:, HALF:HALF + 2 * D]

        def group(b):
            return group_of[b] if isinstance(b, int) else 0

        @block.sync
        def _(sp):
            sp.dma_start(u_in[:], u_v[0]).then_inc(u_loaded, 16)
            for dst, src in weight_loads:
                sp.dma_start(dst, src).then_inc(w_loaded, 16)

            def body(b, par, first, last):
                if not last:
                    wait(sp, ut_in, b + 1)
                    sp.dma_start(u_in[:], u_v[b + 1]).then_inc(u_loaded, 16)
                wait(sp, res_ready, b)
                sp.dma_start(u_res[:], u_v[b]).then_inc(ures_loaded, 16)
                if first:
                    for raw, w in ((raw1, W1), (raw2, W2)):
                        flat = w.rearrange("e h d -> (e h) d")
                        full = E * H // P
                        sp.dma_start(raw[:, 0:full, :], flat[0:full * P].rearrange("(k p) d -> p k d", p=P)).then_inc(raw_loaded, 16)
                        sp.dma_start(raw[0:E * H - full * P, full, :], flat[full * P:]).then_inc(raw_loaded, 16)
                    sp.dma_start(raw3[:, :, 0:H], W3.rearrange("e d h -> d e h")).then_inc(raw_loaded, 16)
                else:
                    if not isinstance(b, int) or b >= 2:
                        wait(sp, x1_saved[par], (b - par) * 8)
                    wait(sp, x1_ready, b)
                    sp.dma_start(x1_v[b - 1], x1_row[1 - par][:]).then_inc(x1_saved[1 - par], 16)

            rows(sp, body)
            sp.wait_ge(x1_ready, B)
            sp.dma_start(x1_v[B - 1], x1_row[1][:]).then_inc(x1_saved[1], 16)

            def load_slot(s, r):
                if not isinstance(s, int) or s >= RING:
                    wait(sp, xt_in, s - RING + 1)
                tile = sp.value_load(slot_from[0:1, bass.ds(s, 1)], min_val=0, max_val=tiles - 1)
                sp.dma_start(x_slot[:, r, :], x_sorted[bass.ds(tile * P, P)]).then_inc(xs_loaded[r], 16)

            sp.wait_ge(table_ready, 1)
            sp.wait_ge(padded[0], 16 * E)
            for i in range(2):
                sp.wait_ge(scattered[0][i], 16 * 2 * NT * (B - 2) // 2)
            sp.wait_ge(prep_lo, 1)
            for r in range(RING):
                load_slot(r, r)
            for i in range(2):
                sp.wait_ge(x1_saved[i], 16 * B // 2)
            sp.dma_start(x1[:], x1_rows.rearrange("(n p) d -> p n d", p=P)).then_inc(x1_loaded, 16)
            with sp.Fori(1, slots[0] // RING) as i:
                for r in range(RING):
                    load_slot(i * RING + r, r)
            sp.wait_ge(table_ready, 2)
            sp.wait_ge(padded[1], 16 * E)
            for i in range(2):
                sp.wait_ge(scattered[1][i], 16 * 2 * NT)
            with sp.Fori(slots[0] // RING, S // RING) as i:
                for r in range(RING):
                    load_slot(i * RING + r, r)
            for b in range(B):
                sp.wait_ge(mix_ready, b + 1)
                sp.dma_start(out_v[b], x1[:, b * NT:(b + 1) * NT, :]).then_inc(out_stored, 16)
            sp.wait_ge(out_stored, 16 * B)

        @block.gpsimd
        def _(pool):
            stage = prod[0:4 * N, :, :].rearrange("q a (r m) -> q (a r) m", m=P)
            nc.gpsimd.memset(stage, 0.0).then_inc(const_ready, 1)
            nc.gpsimd.memset(ident[:], 0.0).then_inc(const_ready, 1)
            nc.gpsimd.memset(ones[:], 1.0).then_inc(const_ready, 1)
            nc.gpsimd.memset(before[:], 1.0).then_inc(const_ready, 1)
            nc.gpsimd.memset(zeros[:], 0.0).then_inc(const_ready, 1)
            nc.gpsimd.memset(running[:, 0:1], 0.0).then_inc(const_ready, 1)
            nc.gpsimd.memset(ones_e[:], 1.0).then_inc(const_ready, 1)
            nc.gpsimd.memset(raw3[:, :, H:HP], 0.0).then_inc(const_ready, 1)
            nc.gpsimd.memset(x_pad[:], 0.0).then_inc(const_ready, 1)
            nc.gpsimd.memset(ones_r[:], 1.0).then_inc(const_ready, 1)
            nc.gpsimd.memset(eps_c[:], 1e-5).then_inc(const_ready, 1)
            pool.wait_ge(const_ready, 11)
            nc.gpsimd.affine_select(out=ident[:], in_=ident[:], compare_op=ALU.not_equal, fill=1.0, base=0,
                                    pattern=[[-1, P]], channel_multiplier=1).then_inc(const_ready, 1)
            for part in range(2):
                nc.gpsimd.affine_select(out=stage, in_=stage, compare_op=ALU.not_equal, fill=1.0,
                                        base=-2 * N * part, pattern=[[-1, 2 * N], [0, P]],
                                        channel_multiplier=1).then_inc(const_ready, 1)
                pool.wait_ge(const_ready, 13 + part)
            nc.gpsimd.affine_select(out=before[:], in_=before[:], compare_op=ALU.is_gt, fill=0.0, base=0,
                                    pattern=[[1, P]], channel_multiplier=-1).then_inc(const_ready, 1)
            exact = dict(allow_small_or_imprecise_dtypes=True)
            nc.gpsimd.iota(first_high[:], pattern=[[-1, E], [0, NT]], base=E, channel_multiplier=0, **exact).then_inc(const_ready, 1)
            nc.gpsimd.iota(lane[:], pattern=[[0, 1]], base=0, channel_multiplier=1, **exact).then_inc(const_ready, 1)
            nc.gpsimd.iota(slot_no[:], pattern=[[1, SM]], base=0, channel_multiplier=0, **exact).then_inc(const_ready, 1)
            for g in range(2):
                for t in (base_from[g], base[g]):
                    nc.gpsimd.iota(t[:], pattern=[[region[g], E]], base=first_tile[g] * P, channel_multiplier=0,
                                   **exact).then_inc(const_ready, 1)

            def scatter(b, par, j):
                for k in range(2):
                    nc.gpsimd.indirect_dma_start(x_sorted[:, :], bass.IndirectOffsetOnAxis(place[par][:, k, j:j + 1], 0),
                                                 x1_row[par][:, j, :], None).then_inc(scattered[group(b)][par], 16)

            def pad(g, e):
                if e == 0:
                    pool.wait_ge(table_ready, g + 1)
                nc.gpsimd.indirect_dma_start(x_sorted[:, :], bass.IndirectOffsetOnAxis(pad_place[g][:, e:e + 1], 0),
                                             zeros[:], None).then_inc(padded[g], 16)

            def body(b, par, first, last):
                past = not isinstance(b, int) or b >= 2
                for n in range(N):
                    g = b * N + n
                    if past and n == 0:
                        wait(pool, place_ready, b - 1)
                    if past and n == N - 1:
                        wait(pool, scattered[0][par], (b - par) * (8 * 2 * NT))
                    wait(pool, state_ready, g + 1)
                    wait(pool, c_ready, g + 1)
                    if first and n == 0:
                        pool.wait_ge(pick_ready, 1)
                    if not first or n >= RING:
                        wait(pool, y_added, g - RING + 1)
                    nc.gpsimd.tensor_tensor(prod[:, n % RING, :], state[:, n % RING, :], c_all[:, n % PAIR, :],
                                            ALU.mult).then_inc(prod_ready, 1)
                    if past and n < NT:
                        scatter(b - 2, par, n)
                    if last and n >= NT:
                        pad(0, n - NT)

            rows(pool, body)
            for b in (B - 2, B - 1):
                pool.wait_ge(place_ready, b + 1)
                for j in range(NT):
                    scatter(b, b % 2, j)
            for e in range(E):
                pad(1, e)

            for b in range(B):
                if b == 0:
                    pool.wait_ge(y_place_ready, 2)
                    pool.wait_ge(ys_ready, slots[0] + RING)
                if b == group_of.count(0):
                    for r in range(RING):
                        pool.wait_ge(y_saved[r], 16 * S // RING)
                done = y_sorted[0:slots[0] * P, :] if group_of[b] == 0 else y_sorted[:, :]
                for j in range(b * NT, (b + 1) * NT):
                    for k in range(2):
                        nc.gpsimd.indirect_dma_start(y_got[k][:, j, :], None, done,
                                                     bass.IndirectOffsetOnAxis(y_place[:, k, j:j + 1], 0)).then_inc(y_gathered[b], 16)

        @block.tensor
        def _(pe):
            def halves(dst, lhs, rhs, start=True, stop=True):
                for h in range(2):
                    s = slice(h * HALF, (h + 1) * HALF)
                    ins = nc.tensor.matmul(dst[:, s], lhs, rhs[:, s], start=start, stop=stop)
                return ins

            def transpose_u(b):
                wait(pe, u_loaded, (b + 1) * 16)
                for j in range(NT):
                    ins = nc.tensor.transpose(ps_s[:, j * P:(j + 1) * P], u_in[:, j, :], ident[:])
                ins.then_inc(ut_in, 1)

            def project_x(b):
                wait(pe, ut_ready, b + 1)
                halves(ps_s, win[:], u_t).then_inc(x_in, 1)

            def project_z(b):
                wait(pe, xpad_ready, b + 1)
                halves(ps_s, wg[:], u_t).then_inc(z_in, 1)

            def project_dt(b):
                wait(pe, xs_ready, b + 1)
                wait(pe, z_ready, b + 1)
                halves(ps_s, wdt[:], xs).then_inc(dt_in, 1)

            def project_bc(b):
                wait(pe, dtabs_ready, b + 1)
                wait(pe, dtrelu_ready, b + 1)
                halves(ps_s[0:4 * N], wbc[:], xs).then_inc(bc_in, 1)

            def project_out(b):
                wait(pe, yz_ready, b + 1)
                for h in range(2):
                    nc.tensor.matmul(ps_s[:, h * HALF:(h + 1) * HALF], ones_r[:], bout_r[:], start=True, stop=True)
                for j in range(NT):
                    ins = nc.tensor.matmul(ps_s[:, j * P:(j + 1) * P], yz[:, j * P:(j + 1) * P], wout[:],
                                           start=False, stop=True, skip_group_check=True)
                ins.then_inc(out_in, 1)

            def add_state(b, n):
                wait(pe, prod_ready, b * N + n + 1)
                if n == 0:
                    wait(pe, yz_ready, b)
                halves(ps_y, ident[:], prod[:, n % RING, :], start=n == 0, stop=n == N - 1).then_inc(y_added, 1)

            def broadcast(b, par, n):
                if n == 0:
                    wait(pe, bchi_ready, b + 1)
                    wait(pe, bclo_ready, b + 1)
                wait(pe, drive_ready, b * N + n)
                halves(ps_b, pick[:, n, :], bc_split[par]).then_inc(bB_ready, 1)
                wait(pe, c_ready, b * N + n)
                halves(ps_c, pick[:, N + n, :], bc_split[par]).then_inc(bC_ready, 1)

            def transpose_x1(b, par):
                wait(pe, x1_ready, b + 1)
                for j in range(NT):
                    ins = nc.tensor.transpose(ps_s[:, j * P:(j + 1) * P], x1_row[par][:, j, :], ident[:])
                ins.then_inc(x1t_in, 1)

            def route_logits(b):
                wait(pe, x1t_ready, b + 1)
                for j in range(NT):
                    ins = nc.tensor.matmul(ps_s[:, j * E:(j + 1) * E], x1_t[:, j * P:(j + 1) * P], wgate_t[:],
                                           start=True, stop=True)
                ins.then_inc(logit_in, 1)

            def rank_tokens(b):
                wait(pe, count_ready, b + 1)
                nc.tensor.matmul(ps_s[:, 0:E], before[:], count[:], start=True, stop=True)
                nc.tensor.matmul(ps_s[:, E:2 * E], ones[:], count[:], start=True, stop=True).then_inc(rank_in, 1)

            pe.wait_ge(const_ready, CONSTANTS)
            transpose_u(0)
            pe.wait_ge(w_loaded, WEIGHTS)
            nc.tensor.transpose(ps_y[:, 0:E], wgate[:], ident[0:E, 0:E]).then_inc(wgate_in, 1)
            project_x(0)
            project_z(0)
            project_dt(0)
            project_bc(0)
            pe.wait_ge(pick_ready, 1)

            def body(b, par, first, last):
                for n in range(N):
                    broadcast(b, par, n)
                    if n >= LAG:
                        add_state(b, n - LAG)
                    elif not first:
                        add_state(b - 1, n - LAG + N)
                    if n == LAG + 1 and not first:
                        if isinstance(b, int) and b == 1:
                            pe.wait_ge(bcval_ready, 2)
                        else:
                            wait(pe, rank_drained, b - 1)
                        project_out(b - 1)
                    if n == LAG + 6 and not first:
                        wait(pe, res_ready, b)
                        if not last:
                            wait(pe, z_ready, b + 2)
                        transpose_x1(b - 1, 1 - par)
                    if n == LAG + 7 and not first:
                        route_logits(b - 1)
                    if n == LAG + 11 and not first:
                        if last:
                            wait(pe, logit_ready, b)
                        else:
                            wait(pe, bcval_ready, b + 2)
                        rank_tokens(b - 1)
                    if not last:
                        if n == LAG + 2:
                            if first:
                                wait(pe, bcval_ready, 1)
                            else:
                                wait(pe, res_ready, b)
                            transpose_u(b + 1)
                        if n == LAG + 3:
                            project_x(b + 1)
                        if n == LAG + 4:
                            project_z(b + 1)
                        if n == LAG + 8:
                            if not first:
                                wait(pe, logit_ready, b)
                            project_dt(b + 1)
                        if n == LAG + 9:
                            project_bc(b + 1)

            rows(pe, body)
            for n in range(N - LAG, N):
                add_state(B - 1, n)
            pe.wait_ge(rank_drained, B - 1)
            project_out(B - 1)
            pe.wait_ge(res_ready, B)
            transpose_x1(B - 1, 1)
            route_logits(B - 1)
            pe.wait_ge(logit_ready, B)
            rank_tokens(B - 1)

            pe.wait_ge(raw_loaded, 16 * 5)
            for i, (kind, cols, width, _) in enumerate(preps):
                if i >= 2:
                    pe.wait_ge(prep_lo, i - 1)
                for c in range(0, width, P):
                    if kind == 3:
                        src, n = raw3.rearrange("d e h -> d (e h)")[:, cols + c:cols + c + P], P
                    else:
                        n = min(P, width - c)
                        src = (raw1, raw2)[kind - 1][0:n, (cols + c) // P, :]
                    ins = nc.tensor.transpose(prep_bank(i)[:, c:c + n], src, ident[0:src.shape[0], 0:src.shape[0]])
                ins.then_inc(prep_in, 1)

            expert = []

            def load_experts(first, count):
                expert[:] = nc.values_load_multi_w_load_instructions(
                    slot_expert[0:1, bass.ds(first, count)], [mybir.EngineType.PE], min_val=0, max_val=E - 1,
                    skip_runtime_bounds_check_because="tables() takes an expert below E or the first")[1]

            def three(dst, a_hi, a_lo, b_hi, b_lo, start=True, stop=True):
                nc.tensor.matmul(dst, a_hi, b_hi, start=start, stop=False)
                nc.tensor.matmul(dst, a_hi, b_lo, start=False, stop=False)
                return nc.tensor.matmul(dst, a_lo, b_hi, start=False, stop=stop)

            def turn_x(s, r, turn):
                wait(pe, xs_loaded[r], (turn + 1) * 16)
                nc.tensor.transpose(ps_xt, x_slot[:, r, :], ident[:]).then_inc(xt_in, 1)

            def hidden(s, p, e, nxt):
                wait(pe, xlo_ready, s + 1)
                cut = bass.ds(e * H, H + H % 2)
                three(ps_h1, x_hi[:, p, :], x_lo[:, p, :], w1[0][:, cut], w1[1][:, cut]).then_inc(h1_in, 1)
                if nxt is not None:
                    turn_x(*nxt)
                three(ps_h2, x_hi[:, p, :], x_lo[:, p, :], w2[0][:, cut], w2[1][:, cut]).then_inc(h2_in, 1)

            def turn_hidden(s, p):
                wait(pe, hid_ready, s + 1)
                for c in range(HC):
                    ins = nc.tensor.transpose(ps_ht[:, c * P:(c + 1) * P], hid[:, p, c * P:(c + 1) * P], ident[:])
                ins.then_inc(ht_in, 1)

            def out_rows(s, e):
                wait(pe, hthi_ready, s + 1)
                wait(pe, ys_ready, s)
                chunk = lambda c, both: w3.rearrange("p k i m -> p (k i m)")[:, bass.ds(e * (2 * HP) + 2 * P * c, P * (1 + both))]
                for c in range(HC):
                    nc.tensor.matmul(ps_yo, hid_hi[:, c * P:(c + 1) * P], chunk(c, True), start=c == 0, stop=c == HC - 1)
                wait(pe, htlo_ready, s + 1)
                for c in range(HC):
                    ins = nc.tensor.matmul(ps_yo[:, 0:D], hid_lo[:, c * P:(c + 1) * P], chunk(c, False), start=False,
                                           stop=c == HC - 1, skip_group_check=True)
                ins.then_inc(yo_in, 1)

            pe.wait_ge(prep_lo, len(preps))
            pe.wait_ge(gate_step, 0 + 3)
            pe.wait_ge(table_ready, 2)
            turn_x(0, 0, 0)

            def slot(s, r, turn, at, first, last):
                if not first:
                    turn_hidden(s - 1, (r - 1) % 2)
                hidden(s, r % 2, expert[at], None if last else (s + 1, (r + 1) % RING, turn + (r + 1) // RING))
                if not first:
                    out_rows(s - 1, expert[at - 1])

            all_slots(pe, slot, load_experts)
            turn_hidden(S - 1, (S - 1) % 2)
            out_rows(S - 1, expert[RING - 1])

        @block.scalar
        def _(act):
            def evacuate_u(b):
                wait(act, ut_in, b + 1)
                wait(act, z_in, b)
                nc.scalar.copy(u_t[:], ps_s[:]).then_inc(ut_ready, 1)

            def evacuate_x(b):
                wait(act, x_in, b + 1)
                wait(act, conv_ready, b)
                nc.scalar.activation(x_pad[:, 1:T + 1], ps_s[:], ACT.Identity, bias=b_in_c[:]).then_inc(xpad_ready, 1)

            def silu_z(b, par):
                wait(act, z_in, b + 1)
                wait(act, yz_ready, b - 1)
                nc.scalar.activation(z[par][:], ps_s[:], ACT.Silu, bias=bg_c[:]).then_inc(z_ready, 1)

            def silu_x(b):
                wait(act, conv_ready, b + 1)
                nc.scalar.activation(xs[:], xs[:], ACT.Silu).then_inc(xs_ready, 1)
                act.preload_act_table_set(EXP_LN)

            def abs_dt(b):
                wait(act, dt_in, b + 1)
                wait(act, dt_ready, b)
                nc.scalar.activation(dt_abs[:], ps_s[:], ACT.Abs, bias=bdt_c[:]).then_inc(dtabs_ready, 1)

            def relu_dt(b):
                wait(act, dt_ready, b)
                nc.scalar.activation(dt_relu[:], ps_s[:], ACT.Relu, bias=bdt_c[:]).then_inc(dtrelu_ready, 1)

            def exp_dt(b):
                wait(act, dtabs_ready, b + 1)
                nc.scalar.activation(dt_abs[:], dt_abs[:], ACT.Exp, scale=-1.0).then_inc(dtexp_ready, 1)

            def ln_dt(b):
                wait(act, dtexp_ready, b + 1)
                nc.scalar.activation(dt_abs[:], dt_abs[:], ACT.Ln, bias=1.0).then_inc(dtln_ready, 1)

            def evacuate_bc(b):
                wait(act, bc_in, b + 1)
                wait(act, bclo_ready, b)
                nc.scalar.activation(bc_val[:], ps_s[0:4 * N, :], ACT.Identity, bias=bbc_c[:]).then_inc(bcval_ready, 1)

            def round_bc(b, par):
                wait(act, bcval_ready, b + 1)
                wait(act, bC_ready, (b - 1) * N)
                nc.scalar.copy(bc_split[par][:], bc_val[:]).then_inc(bchi_ready, 1)

            def row_ln(b):
                wait(act, agg_part, 3 * b + 3)
                nc.scalar.activation(lnv[:], var[:], ACT.Ln, bias=eps_c[:], scale=1.0 / P).then_inc(lnv_ready, 1)

            def row_rstd(b):
                wait(act, lnv_ready, b + 1)
                nc.scalar.activation(rstd[:], lnv[:], ACT.Exp, scale=-0.5).then_inc(rstd_ready, 1)

            def evacuate_x1(b):
                wait(act, x1t_in, b + 1)
                wait(act, logit_in, b)
                nc.scalar.copy(x1_t[:], ps_s[:]).then_inc(x1t_ready, 1)

            act.preload_act_table_set(EXP_LN)
            act.wait_ge(const_ready, CONSTANTS)
            act.wait_ge(w_loaded, WEIGHTS)
            act.wait_ge(wgate_in, 1)
            nc.scalar.copy(wgate_t[:], ps_y[:, 0:E]).then_inc(wgate_ready, 1)
            evacuate_u(0)
            evacuate_x(0)
            silu_z(0, 0)
            silu_x(0)
            nc.scalar.copy(pick[:], prod[0:4 * N, :, :].rearrange("q a (r m) -> q (a r) m", m=P)).then_inc(pick_ready, 1)
            abs_dt(0)
            relu_dt(0)
            evacuate_bc(0)
            exp_dt(0)
            round_bc(0, 0)
            ln_dt(0)

            def body(b, par, first, last):
                for n in range(N):
                    g = b * N + n
                    if n == 0:
                        wait(act, dt_ready, b + 1)
                    if not first or n >= PAIR:
                        wait(act, state_ready, g - PAIR + 1)
                    nc.scalar.activation(decay[:, n % PAIR, :], dt[par][:], ACT.Exp,
                                         scale=a_dn[:, n:n + 1]).then_inc(decay_ready, 1)
                    wait(act, bC_ready, g + 1)
                    if not first or n >= PAIR:
                        wait(act, prod_ready, g - PAIR + 1)
                    nc.scalar.copy(c_all[:, n % PAIR, :], ps_c[:]).then_inc(c_ready, 1)
                    if not first:
                        if n == LAG + 3:
                            row_ln(b - 1)
                        if n == LAG + 4:
                            row_rstd(b - 1)
                        if n == LAG + 6:
                            evacuate_x1(b - 1)
                    if not last:
                        if n == LAG + 2:
                            evacuate_u(b + 1)
                        if n == LAG + 3:
                            evacuate_x(b + 1)
                        if n == LAG + 5:
                            silu_z(b + 1, 1 - par)
                            silu_x(b + 1)
                        if n == LAG + 8:
                            abs_dt(b + 1)
                            relu_dt(b + 1)
                        if n == LAG + 9:
                            evacuate_bc(b + 1)
                            exp_dt(b + 1)
                        if n == LAG + 10:
                            round_bc(b + 1, 1 - par)
                            ln_dt(b + 1)

            rows(act, body)
            row_ln(B - 1)
            row_rstd(B - 1)
            evacuate_x1(B - 1)
            act.wait_ge(route_step, B * ROUTE)
            nc.scalar.activation(gate2[:], gap[:], ACT.Exp).then_inc(gap_exp, 1)

            for i, (kind, cols, width, dst) in enumerate(preps):
                act.wait_ge(prep_in, i + 1)
                nc.scalar.copy(prep_part(i, 0), prep_shape(i, prep_bank(i)[:, 0:width])).then_inc(prep_hi, 1)

            def round_x(s, p):
                wait(act, xt_in, s + 1)
                nc.scalar.copy(x_hi[:, p, :], ps_xt).then_inc(xhi_ready, 1)

            def silu_hidden(s, p):
                wait(act, h1_in, s + 1)
                nc.scalar.activation(act1[:, p, :], ps_h1[:, 0:H], ACT.Silu).then_inc(silu_ready, 1)

            def round_hidden(s):
                wait(act, ht_in, s + 1)
                nc.scalar.copy(hid_hi[:], ps_ht).then_inc(hthi_ready, 1)

            def save_slot(s, r):
                wait(act, ys_ready, s + 1)
                act.dma_start(y_sorted[bass.ds(s * P, P)], y_slot[:, r, :]).then_inc(y_saved[r], 16)

            act.wait_ge(table_ready, 2)
            act.preload_act_table(ACT.Silu)
            round_x(0, 0)

            def slot(s, r, turn, at, first, last):
                if not first:
                    round_hidden(s - 1)
                silu_hidden(s, r % 2)
                if not last:
                    round_x(s + 1, (r + 1) % 2)
                if not isinstance(s, int) or s >= 2:
                    save_slot(s - 2, (r - 2) % RING)

            all_slots(act, slot)
            round_hidden(S - 1)
            for s in (S - 2, S - 1):
                save_slot(s, s % RING)

            act.preload_act_table_set(EXP_LN)
            for b in range(B):
                act.wait_ge(mix_step, MIX * (b + 1))
                nc.scalar.activation(lnv[:], var[:], ACT.Ln, bias=eps_c[:], scale=1.0 / P).then_inc(mix_ln, 1)
                act.wait_ge(mix_ln, b + 1)
                if b:
                    act.wait_ge(mix_ready, b)
                nc.scalar.activation(rstd[:], lnv[:], ACT.Exp, scale=-0.5).then_inc(mix_rstd, 1)

        @block.vector
        def _(dve):
            def conv(b):
                wait(dve, xpad_ready, b + 1)
                wait(dve, dtx_ready, b)
                wait(dve, bc_in, b)
                nc.vector.tensor_scalar(xs[:], x_pad[:, 0:T], cw[:, 0:1], cb[:], ALU.mult, ALU.add).then_inc(conv_part, 1)
                wait(dve, conv_part, 2 * b + 1)
                nc.vector.scalar_tensor_tensor(out=xs[:], in0=x_pad[:, 1:T + 1], scalar=cw[:, 1:2], in1=xs[:],
                                               op0=ALU.mult, op1=ALU.add).then_inc(conv_part, 1)
                wait(dve, conv_part, 2 * b + 2)
                nc.vector.scalar_tensor_tensor(out=xs[:], in0=x_pad[:, 2:T + 2], scalar=cw[:, 2:3], in1=xs[:],
                                               op0=ALU.mult, op1=ALU.add).then_inc(conv_ready, 1)

            def sum_dt(b, par):
                wait(dve, dtln_ready, b + 1)
                wait(dve, dtrelu_ready, b + 1)
                wait(dve, dtx_ready, b - 1)
                wait(dve, decay_ready, (b - 1) * N)
                nc.vector.tensor_tensor(dt[par][:], dt_relu[:], dt_abs[:], ALU.add).then_inc(dt_ready, 1)

            def mul_dtx(b, par):
                wait(dve, dt_ready, b + 1)
                wait(dve, drive_ready, (b - 1) * N)
                nc.vector.tensor_tensor(dtx[par][:], dt[par][:], xs[:], ALU.mult).then_inc(dtx_ready, 1)

            def low_bc(b, par):
                wait(dve, bchi_ready, b + 1)
                lo = slice(2 * N, 4 * N)
                nc.vector.tensor_tensor(bc_split[par][lo, :], bc_val[lo, :], bc_split[par][lo, :].bitcast(F32),
                                        ALU.subtract).then_inc(bclo_ready, 1)

            def drive_of(b, par, n):
                g = b * N + n
                wait(dve, bB_ready, g + 1)
                if n == 0:
                    wait(dve, dtx_ready, b + 1)
                if not isinstance(g, int) or g >= PAIR:
                    wait(dve, state_ready, g - PAIR + 1)
                nc.vector.tensor_tensor(drive[:, n % PAIR, :], dtx[par][:], ps_b[:], ALU.mult).then_inc(drive_ready, 1)

            def scan(b, n):
                g = b * N + n
                wait(dve, drive_ready, g + 1)
                wait(dve, decay_ready, g + 1)
                if not isinstance(g, int) or g >= RING:
                    wait(dve, prod_ready, g - RING + 1)
                nc.vector.tensor_tensor_scan(state[:, n % RING, :], decay[:, n % PAIR, :], drive[:, n % PAIR, :], 0.0,
                                             ALU.mult, ALU.add).then_inc(state_ready, 1)

            def gate_y(b, par):
                wait(dve, y_added, (b + 1) * N)
                wait(dve, z_ready, b + 1)
                wait(dve, logit_in, b)
                nc.vector.tensor_tensor(yz[:], ps_y[:], z[par][:], ALU.mult).then_inc(yz_ready, 1)

            def residual(b, par):
                wait(dve, out_in, b + 1)
                wait(dve, ures_loaded, (b + 1) * 16)
                nc.vector.tensor_tensor(res[:].rearrange("p n d -> p (n d)"), ps_s[:],
                                        u_res[:].rearrange("p n d -> p (n d)"), ALU.add).then_inc(res_ready, 1)
                wait(dve, res_ready, b + 1)
                for j in range(NT):
                    ins = nc.vector.bn_stats(stats[:, j, :], res[:, j, :])
                ins.then_inc(stats_ready, 1)

            def aggregate(b):
                wait(dve, stats_ready, b + 1)
                nc.vector.tensor_tensor(mean[:], stats[:, :, 1], stats[:, :, 4], ALU.add)
                nc.vector.tensor_tensor(dif[:], stats[:, :, 1], stats[:, :, 4], ALU.subtract)
                nc.vector.tensor_tensor(sq[:], stats[:, :, 2], stats[:, :, 5], ALU.add).then_inc(agg_part, 1)
                wait(dve, agg_part, 3 * b + 1)
                nc.vector.tensor_scalar(mean[:], mean[:], 0.5, None, ALU.mult)
                nc.vector.tensor_tensor(dif[:], dif[:], dif[:], ALU.mult).then_inc(agg_part, 1)
                wait(dve, agg_part, 3 * b + 2)
                nc.vector.scalar_tensor_tensor(out=var[:], in0=dif[:], scalar=P / 4.0, in1=sq[:],
                                               op0=ALU.mult, op1=ALU.add).then_inc(agg_part, 1)

            def normalise(b, par):
                wait(dve, rstd_ready, b + 1)
                wait(dve, prod_ready, (b + 1) * N)
                for j in range(NT):
                    ins = nc.vector.tensor_scalar(x1_row[par][:, j, :], res[:, j, :], mean[:, j:j + 1], rstd[:, j:j + 1],
                                                  ALU.subtract, ALU.mult)
                ins.then_inc(x1_ready, 1)

            by_tile = lambda t: t[:].rearrange("p e j -> p j e")
            each_expert = lambda t: t[:].unsqueeze(1).broadcast_to([P, E, NT])
            each_tile = lambda t: t[:].unsqueeze(2).broadcast_to([P, E, NT])
            flat = lambda t: t[:].rearrange("p e j -> p (e j)")

            def choose(b):
                k = [0]

                def link(ins):
                    k[0] += 1
                    ins.then_inc(route_step, 1)
                    wait(dve, route_step, b * ROUTE + k[0])

                wait(dve, logit_in, b + 1)
                ins = nc.vector.tensor_copy(logit[:], ps_s[:, 0:E * NT].rearrange("p (j e) -> p e j", e=E))
                ins.then_inc(logit_ready, 1)
                wait(dve, logit_ready, b + 1)

                def pick_top(values, top, dst):
                    link(nc.vector.tensor_reduce(dst[:], by_tile(values), AX.X, ALU.max))
                    link(nc.vector.tensor_tensor(top[:], values[:], each_expert(dst), ALU.is_equal))
                    link(nc.vector.tensor_tensor(top[:], top[:], first_high[:], ALU.mult))
                    link(nc.vector.tensor_reduce(index[:], by_tile(top), AX.X, ALU.max))
                    link(nc.vector.tensor_tensor(top[:], first_high[:], each_expert(index), ALU.is_equal))

                pick_top(logit, top1, best)
                link(nc.vector.scalar_tensor_tensor(out=flat(logit2), in0=flat(top1), scalar=-3.0e38, in1=flat(logit),
                                                    op0=ALU.mult, op1=ALU.add))
                pick_top(logit2, top2, best2)
                nc.vector.tensor_tensor(gap[:, bass.ds(b * NT, NT)], best2[:], best[:], ALU.subtract)
                link(nc.vector.tensor_tensor(chosen[:], top1[:], top2[:], ALU.add))
                link(nc.vector.tensor_tensor_scan(running[:, 1:], ones[:, 0:E * NT], flat(chosen), 0.0, ALU.mult, ALU.add))
                nc.vector.tensor_tensor(count[:], running[:, NT::NT], running[:, 0:E * NT:NT], ALU.subtract).then_inc(count_ready, 1)
                assert k[0] == ROUTE - 8

            def locate(b, par):
                g = group(b)
                k = [ROUTE - 8]

                def link(ins):
                    k[0] += 1
                    ins.then_inc(route_step, 1)
                    wait(dve, route_step, b * ROUTE + k[0])

                wait(dve, count_ready, b + 1)
                link(nc.vector.tensor_tensor(offset[:], base[g][:], running[:, 0:E * NT:NT], ALU.subtract))
                wait(dve, rank_in, b + 1)
                link(nc.vector.tensor_tensor(offset[:], offset[:], ps_s[:, 0:E], ALU.add))
                nc.vector.tensor_tensor(base[g][:], base[g][:], ps_s[:, E:2 * E], ALU.add).then_inc(rank_drained, 1)
                link(nc.vector.tensor_tensor(flat(rank), running[:, 1:], flat(chosen), ALU.subtract))
                link(nc.vector.tensor_tensor(rank[:], rank[:], each_tile(offset), ALU.add))
                for i, top in enumerate((top1, top2)):
                    link(nc.vector.tensor_tensor(part[:], top[:], rank[:], ALU.mult))
                    link(nc.vector.tensor_reduce(place_f[:, i, :], by_tile(part), AX.X, ALU.add))
                nc.vector.tensor_copy(place[par][:], place_f[:])
                nc.vector.tensor_copy(places[:, :, bass.ds(b * NT, NT)], place_f[:]).then_inc(place_ready, 1)
                assert k[0] == ROUTE

            def tables(g):
                n, o, k = slots[g], first_slot[g], [g * TABLE]

                def link(ins):
                    k[0] += 1
                    ins.then_inc(table_step, 1)
                    dve.wait_ge(table_step, k[0])

                number, one = slot_no[:, 0:n], slice(0, 1)
                by_slot = lambda t: t[one, :].unsqueeze(1).broadcast_to([1, n, E])
                dve.wait_ge(rank_drained, B - 2 if g == 0 else B)
                link(nc.vector.tensor_tensor(pad_place[g][:], base[g][:], lane[:].broadcast_to([P, E]), ALU.add))
                link(nc.vector.tensor_tensor(n_tiles[:], base[g][:], base_from[g][:], ALU.subtract))
                link(nc.vector.tensor_scalar(n_tiles_i[:], n_tiles[:], float(P - 1), None, ALU.add))
                link(nc.vector.tensor_scalar(n_tiles_i[:], n_tiles_i[:], 7, None, ALU.logical_shift_right))
                link(nc.vector.tensor_copy(n_tiles[:], n_tiles_i[:]))
                link(nc.vector.tensor_tensor_scan(done_at[:], ones_e[:], n_tiles[:], 0.0, ALU.mult, ALU.add))
                link(nc.vector.tensor_scalar(skip[g][:], n_tiles[:], -1.0, float(region[g] // P), ALU.mult, ALU.add))
                link(nc.vector.tensor_tensor(passed[:, 0:n, :], number.unsqueeze(2).broadcast_to([1, n, E]), by_slot(done_at), ALU.is_ge))
                link(nc.vector.tensor_reduce(t_expert[:, 0:n], passed[:, 0:n, :], AX.X, ALU.add))
                link(nc.vector.tensor_tensor(passed[:, 0:n, :], passed[:, 0:n, :], by_slot(skip[g]), ALU.mult))
                link(nc.vector.tensor_reduce(t_tile[:, 0:n], passed[:, 0:n, :], AX.X, ALU.add))
                link(nc.vector.tensor_scalar(t_used[:, 0:n], number, done_at[one, E - 1:E], None, ALU.is_lt))
                link(nc.vector.tensor_tensor(slot_expert[:, o:o + n], t_expert[:, 0:n], t_used[:, 0:n], ALU.mult))
                link(nc.vector.scalar_tensor_tensor(out=t_tile[:, 0:n], in0=t_tile[:, 0:n], scalar=float(first_tile[g]), in1=number,
                                                    op0=ALU.add, op1=ALU.add))
                link(nc.vector.scalar_tensor_tensor(out=t_tile[:, 0:n], in0=t_tile[:, 0:n], scalar=-float(first_tile[g]),
                                                    in1=t_used[:, 0:n], op0=ALU.add, op1=ALU.mult))
                link(nc.vector.tensor_scalar(slot_from[:, o:o + n], t_tile[:, 0:n], float(first_tile[g]), None, ALU.add))
                assert k[0] == (g + 1) * TABLE
                nc.vector.tensor_copy(t_tile[:, 0:1], number[:, 0:1]).then_inc(table_ready, 1)

            def find_results():
                step = [0]

                def link(ins):
                    step[0] += 1
                    ins.then_inc(result_step, 1)
                    dve.wait_ge(result_step, step[0])

                dve.wait_ge(table_ready, 2)
                for g in range(2):
                    first = group_of.index(g) * NT
                    n = 2 * tokens[g] // P
                    gaps = hid[:].rearrange("p a h -> p (a h)")[:, 0:n * E].rearrange("p (i t e) -> p i t e", i=2, e=E)
                    total = y_sum[:, :, first:first + n // 2]
                    mine = places[:, :, first:first + n // 2]
                    spread = lambda t: t[:].unsqueeze(1).unsqueeze(1).broadcast_to([P, 2, n // 2, E])
                    link(nc.vector.tensor_scalar(total, mine, -float(region[g]), None, ALU.add))
                    link(nc.vector.tensor_tensor(gaps, total.unsqueeze(3).broadcast_to([P, 2, n // 2, E]), spread(base_from[g]), ALU.is_ge))
                    link(nc.vector.tensor_tensor(gaps, gaps, spread(skip[g]), ALU.mult))
                    link(nc.vector.tensor_reduce(total, gaps, AX.X, ALU.add))
                    link(nc.vector.scalar_tensor_tensor(out=total, in0=total, scalar=-float(P), in1=mine, op0=ALU.mult, op1=ALU.add))
                    nc.vector.tensor_scalar(y_place[:, :, first:first + n // 2], total,
                                            float((first_slot[g] - first_tile[g]) * P), None, ALU.add).then_inc(y_place_ready, 1)

            dve.wait_ge(w_loaded, WEIGHTS)
            dve.wait_ge(const_ready, CONSTANTS)
            conv(0)
            sum_dt(0, 0)
            mul_dtx(0, 0)
            low_bc(0, 0)

            def body(b, par, first, last):
                for n in range(N):
                    drive_of(b, par, n)
                    if n:
                        scan(b, n - 1)
                    elif not first:
                        scan(b - 1, N - 1)
                    if not first:
                        if n == LAG:
                            gate_y(b - 1, 1 - par)
                        if n == LAG + 2:
                            residual(b - 1, 1 - par)
                            aggregate(b - 1)
                        if n == LAG + 5:
                            normalise(b - 1, 1 - par)
                        if n == LAG + 8:
                            choose(b - 1)
                        if n == LAG + 12:
                            locate(b - 1, 1 - par)
                        if last and n == 1:
                            tables(0)
                    if not last:
                        if n == LAG + 4:
                            conv(b + 1)
                        if n == LAG + 11:
                            sum_dt(b + 1, 1 - par)
                            low_bc(b + 1, 1 - par)
                        if n == LAG + 12:
                            mul_dtx(b + 1, 1 - par)

            rows(dve, body)
            scan(B - 1, N - 1)
            gate_y(B - 1, 1)
            residual(B - 1, 1)
            aggregate(B - 1)
            normalise(B - 1, 1)
            choose(B - 1)
            locate(B - 1, 1)
            tables(1)
            find_results()
            dve.wait_ge(gap_exp, 1)
            nc.vector.tensor_scalar(gate1[:], gate2[:], 1.0, None, ALU.add).then_inc(gate_step, 1)
            dve.wait_ge(gate_step, 1)
            nc.vector.reciprocal(gate1[:], gate1[:]).then_inc(gate_step, 1)
            dve.wait_ge(gate_step, 2)
            nc.vector.tensor_tensor(gate2[:], gate2[:], gate1[:], ALU.mult)
            nc.vector.memset(hid[:, :, H:HP], 0.0).then_inc(gate_step, 1)

            for i, (kind, cols, width, dst) in enumerate(preps):
                dve.wait_ge(prep_hi, i + 1)
                nc.vector.tensor_tensor(prep_part(i, 1), prep_shape(i, prep_bank(i)[:, 0:width]), prep_part(i, 0).bitcast(F32),
                                        ALU.subtract).then_inc(prep_lo, 1)
            for w in w1 + w2:
                nc.vector.memset(w[:, E * H:].bitcast(F32), 0.0)

            def low_x(s, p):
                wait(dve, xhi_ready, s + 1)
                nc.vector.tensor_tensor(x_lo[:, p, :], ps_xt, x_hi[:, p, :].bitcast(F32), ALU.subtract).then_inc(xlo_ready, 1)

            def multiply(s, p):
                wait(dve, silu_ready, s + 1)
                wait(dve, h2_in, s + 1)
                nc.vector.tensor_tensor(hid[:, p, 0:H], act1[:, p, :], ps_h2[:, 0:H], ALU.mult).then_inc(hid_ready, 1)

            def low_hidden(s):
                wait(dve, hthi_ready, s + 1)
                nc.vector.tensor_tensor(hid_lo[:], ps_ht, hid_hi[:].bitcast(F32), ALU.subtract).then_inc(htlo_ready, 1)

            def evacuate_y(s, r, turn):
                wait(dve, yo_in, s + 1)
                wait(dve, y_saved[r], turn * 16)
                nc.vector.tensor_reduce(y_slot[:, r, :], ps_yo.rearrange("p (i d) -> p d i", i=2), AX.X, ALU.add).then_inc(ys_ready, 1)

            low_x(0, 0)

            def slot(s, r, turn, at, first, last):
                if not first:
                    low_hidden(s - 1)
                multiply(s, r % 2)
                if not last:
                    low_x(s + 1, (r + 1) % 2)
                if not first:
                    evacuate_y(s - 1, (r - 1) % RING, turn - (1 if r == 0 else 0))

            all_slots(dve, slot)
            low_hidden(S - 1)
            evacuate_y(S - 1, (S - 1) % RING, S // RING - 1)

            dve.wait_ge(x1_loaded, 16)

            def mix(b):
                at = MIX * b
                dve.wait_ge(y_gathered[b], 16 * 2 * NT)
                if b:
                    dve.wait_ge(mix_ln, b)
                for k, gate in enumerate((gate1, gate2)):
                    for j in range(b * NT, (b + 1) * NT):
                        ins = nc.vector.scalar_tensor_tensor(out=x1[:, j, :], in0=y_got[k][:, j, :], scalar=gate[:, j:j + 1],
                                                             in1=x1[:, j, :], op0=ALU.mult, op1=ALU.add)
                    ins.then_inc(mix_step, 1)
                    dve.wait_ge(mix_step, at + k + 1)
                for j in range(NT):
                    ins = nc.vector.bn_stats(stats[:, j, :], x1[:, b * NT + j, :])
                ins.then_inc(mix_step, 1)

            def mix_statistics(b):
                at = MIX * b + 3
                dve.wait_ge(mix_step, at)
                wait(dve, mix_ready, b)
                nc.vector.tensor_tensor(mean[:], stats[:, :, 1], stats[:, :, 4], ALU.add)
                nc.vector.tensor_tensor(dif[:], stats[:, :, 1], stats[:, :, 4], ALU.subtract)
                nc.vector.tensor_tensor(sq[:], stats[:, :, 2], stats[:, :, 5], ALU.add).then_inc(mix_step, 1)
                dve.wait_ge(mix_step, at + 1)
                nc.vector.tensor_scalar(mean[:], mean[:], 0.5, None, ALU.mult)
                nc.vector.tensor_tensor(dif[:], dif[:], dif[:], ALU.mult).then_inc(mix_step, 1)
                dve.wait_ge(mix_step, at + 2)
                nc.vector.scalar_tensor_tensor(out=var[:], in0=dif[:], scalar=P / 4.0, in1=sq[:],
                                               op0=ALU.mult, op1=ALU.add).then_inc(mix_step, 1)

            def mix_normalise(b):
                dve.wait_ge(mix_rstd, b + 1)
                for j in range(NT):
                    ins = nc.vector.tensor_scalar(x1[:, b * NT + j, :], x1[:, b * NT + j, :], mean[:, j:j + 1], rstd[:, j:j + 1],
                                                  ALU.subtract, ALU.mult)
                ins.then_inc(mix_ready, 1)

            for b in range(B):
                mix(b)
                if b:
                    mix_normalise(b - 1)
                mix_statistics(b)
            mix_normalise(B - 1)


_INS = ['L0_attn_u', 'L0_attn_Win', 'L0_attn_b_in', 'L0_attn_Wg', 'L0_attn_bg', 'L0_attn_Wout', 'L0_attn_bout',
        'L0_attn_convw', 'L0_attn_convb', 'L0_attn_A', 'L0_attn_Wb', 'L0_attn_bb', 'L0_attn_Wc', 'L0_attn_bc',
        'L0_attn_Wdt', 'L0_attn_bdt', 'L0_ffn_Wg', 'L0_ffn_W1', 'L0_ffn_W2', 'L0_ffn_W3']


def kernel(**inputs):
    import numpy as _np
    import concourse.bacc as _bacc
    from concourse import mybir as _mybir
    from concourse.bass_utils import run_bass_kernel_spmd as _run

    nc = _bacc.Bacc("TRN2", target_bir_lowering=False, num_devices=1)
    arrays, args = {}, []
    for name in _INS:
        a = _np.ascontiguousarray(inputs[name])
        arrays[f"in_{name}_dram"] = a
        args.append(nc.dram_tensor(f"in_{name}_dram", a.shape, _mybir.dt.from_np(a.dtype), kind="ExternalInput").ap())
    args.append(nc.dram_tensor("out_0_dram", (8, 1024, 128), _mybir.dt.float32, kind="ExternalOutput").ap())
    build(nc, *args)
    r = _run(nc, [arrays], core_ids=[0])
    return r.results[0]["out_0_dram"]
```

```python
from contextlib import ExitStack

import concourse.bass as bass
from concourse import mybir

F32 = mybir.dt.float32
F32R = mybir.dt.float32r
ALU = mybir.AluOpType
ACT = mybir.ActivationFunctionType
AX = mybir.AxisListType

P = 128
EXP_LN = "natural_log_exp_and_others"
HALF = 512
I32 = mybir.dt.int32
U32 = mybir.dt.uint32
LAG = 4
RING = 4
TWO = 32
PAIR = 2


def wait(eng, sem, value):
    if not isinstance(value, int) or value > 0:
        eng.wait_ge(sem, value)


def build(nc, u, Win, b_in, Wg, bg, Wout, bout, convw, convb, A, Wb, bb, Wc, bc, Wdt, bdt,
          Wgate, W1, W2, W3, out):
    B, T, D = u.shape
    N = A.shape[1]
    NT = T // P
    E, H, _ = W1.shape
    HC = -(-H // P)
    HP = HC * P
    assert E == NT and E * H % 2 == 0

    group_of = [0] * (B - 2) + [1] * 2
    tokens = [group_of.count(g) * T for g in range(2)]
    region = [t + P for t in tokens]
    first_tile = [0, E * region[0] // P]
    tiles = first_tile[1] + E * region[1] // P
    slots = [-(-((2 * t + E * (P - 1)) // P) // RING) * RING for t in tokens]
    first_slot = [0, slots[0]]
    S = sum(slots)
    assert D == P and T == 2 * HALF and N == 16

    with ExitStack() as ctx:
        def sb(name, shape, dt=F32):
            return ctx.enter_context(nc.sbuf_tensor(name, shape, dt))

        def ps(name, shape, dt=F32):
            return ctx.enter_context(nc.psum_tensor(name, shape, dt))

        def sem(name):
            return ctx.enter_context(nc.semaphore(name))

        ident = sb("ident", [P, P])
        eps_c = sb("eps_c", [P, 1])
        zeros = sb("zeros", [P, P])
        RB = -(-E * H // P)
        raw = sb("raw", [P, 2 * RB + E * HC, D])
        raw1 = raw[:, 0:RB, :]
        raw2 = raw[:, RB:2 * RB, :]
        raw3 = raw[:, 2 * RB:, :].rearrange("p (e c) h -> p e (c h)", e=E)
        x1_row = [sb(f"x1_row{i}", [P, NT, D]) for i in range(2)]
        place = [sb(f"place{i}", [P, 2, NT], U32) for i in range(2)]
        places = sb("places", [P, 2, B * NT])
        gap = sb("gap", [P, B * NT])
        gate1 = sb("gate1", [P, B * NT])
        gate2 = sb("gate2", [P, B * NT])
        base_from = [sb(f"base_from{g}", [P, E]) for g in range(2)]
        base = [sb(f"base{g}", [P, E]) for g in range(2)]
        pad_place = [sb(f"pad_place{g}", [P, E], U32) for g in range(2)]
        slot_expert = sb("slot_expert", [1, S], I32)
        slot_from = sb("slot_from", [1, S], I32)
        skip = [sb(f"skip{g}", [P, E]) for g in range(2)]
        stats = sb("stats", [P, NT, 6])
        mean = sb("mean", [P, NT])
        dif = sb("dif", [P, NT])
        sq = sb("sq", [P, NT])
        var = sb("var", [P, NT])
        lnv = sb("lnv", [P, NT])
        rstd = sb("rstd", [P, NT])

        own = ctx.enter_context(ExitStack())

        def sb(name, shape, dt=F32):
            return own.enter_context(nc.sbuf_tensor(name, shape, dt))

        win = sb("win", [P, D])
        wg = sb("wg", [P, D])
        wdt = sb("wdt", [P, D])
        wout = sb("wout", [P, D])
        wbc = sb("wbc", [P, 4 * N])
        a_dn = sb("a_dn", [P, N])
        b_in_c = sb("b_in_c", [P, 1])
        bg_c = sb("bg_c", [P, 1])
        bdt_c = sb("bdt_c", [P, 1])
        cw = sb("cw", [P, 3])
        cb = sb("cb", [P, 1])
        bbc_c = sb("bbc_c", [4 * N, 1])
        bout_r = sb("bout_r", [2 * TWO, HALF], F32R)
        ones_r = sb("ones_r", [2 * TWO, P], F32R)
        pick = sb("pick", [4 * N, 2 * N, P], F32R)

        u_in = sb("u_in", [P, NT, D])
        u_res = sb("u_res", [P, NT, D])
        u_t = sb("u_t", [P, T])
        x_pad = sb("x_pad", [P, T + 2])
        xs = sb("xs", [P, T])
        z = [sb(f"z{i}", [P, T]) for i in range(2)]
        dt_abs = sb("dt_abs", [P, T])
        dt_relu = sb("dt_relu", [P, T])
        dt = [sb(f"dt{i}", [P, T]) for i in range(2)]
        dtx = [sb(f"dtx{i}", [P, T]) for i in range(2)]
        bc_val = sb("bc_val", [4 * N, T])
        bc_split = [sb(f"bc_split{i}", [4 * N, T], F32R) for i in range(2)]
        decay = sb("decay", [P, RING, T])
        state = sb("state", [P, RING, T])
        c_all = sb("c_all", [P, PAIR, T])
        prod = sb("prod", [P, RING, T])
        yz = sb("yz", [P, T])
        res = sb("res", [P, NT, D])
        x1_t = yz
        bout_v = state[0:2 * TWO, RING - 1, 0:HALF]
        wgate_t = sb("wgate_t", [P, E])
        wgate = sb("wgate", [E, D])
        before = sb("before", [P, P])
        ones = sb("ones", [P, P])
        first_high = sb("first_high", [P, E, NT])
        logit = sb("logit", [P, E, NT])
        logit2 = sb("logit2", [P, E, NT])
        top1 = sb("top1", [P, E, NT])
        top2 = sb("top2", [P, E, NT])
        chosen = sb("chosen", [P, E, NT])
        rank = sb("rank", [P, E, NT])
        part = sb("part", [P, E, NT])
        best = sb("best", [P, NT])
        place_f = sb("place_f", [P, 2, NT])
        best2 = sb("best2", [P, NT])
        index = sb("index", [P, NT])
        running = sb("running", [P, E * NT + 1])
        count = sb("count", [P, E])
        offset = sb("offset", [P, E])
        lane = sb("lane", [P, 1])
        SM = max(slots)
        slot_no = sb("slot_no", [1, SM])
        n_tiles = sb("n_tiles", [P, E])
        n_tiles_i = sb("n_tiles_i", [P, E], I32)
        done_at = sb("done_at", [P, E])
        passed = sb("passed", [1, SM, E])
        t_expert = sb("t_expert", [1, SM])
        t_tile = sb("t_tile", [1, SM])
        t_used = sb("t_used", [1, SM])
        ones_e = sb("ones_e", [P, E])
        own.close()

        def sb(name, shape, dt=F32):
            return ctx.enter_context(nc.sbuf_tensor(name, shape, dt))

        EH = E * H + 2
        w1 = [sb(f"w1_{i}", [P, EH], F32R) for i in ("hi", "lo")]
        w2 = [sb(f"w2_{i}", [P, EH], F32R) for i in ("hi", "lo")]
        w3 = sb("w3", [P, E * HC, 2, P], F32R)
        x1 = sb("x1", [P, B * NT, D])
        y_got = [sb("y_got", [P, B * NT, D]), raw[:, 0:B * NT, :]]
        x_slot = sb("x_slot", [P, RING, D])
        x_hi = sb("x_hi", [P, 2, P], F32R)
        x_lo = sb("x_lo", [P, 2, P], F32R)
        act1 = sb("act1", [P, 2, H])
        hid = sb("hid", [P, 2, HP])
        hid_hi = sb("hid_hi", [P, HP], F32R)
        hid_lo = sb("hid_lo", [P, HP], F32R)
        y_slot = sb("y_slot", [P, RING, D])
        y_place = sb("y_place", [P, 2, B * NT], U32)
        y_sum = y_slot[:, 0:2, 0:B * NT]

        mix_mean, mix_var, mix_lnv, mix_rs, mix_off = (
            sb(name, [P, 2, NT]) for name in ("mix_mean", "mix_var", "mix_lnv", "mix_rs", "mix_off"))

        x1_rows = nc.dram_tensor("x1_rows", (B * T, D), F32, kind="Internal").ap()
        x_sorted = nc.dram_tensor("x_sorted", (tiles * P, D), F32, kind="Internal").ap()
        y_sorted = nc.dram_tensor("y_sorted", (S * P, D), F32, kind="Internal").ap()

        ps_b = ps("ps_b", [P, T])
        ps_c = ps("ps_c", [P, T])
        ps_y = ps("ps_y", [P, T])
        ps_s = ps("ps_s", [P, T])

        w_loaded = sem("w_loaded")
        const_ready = sem("const_ready")
        pick_ready, bout_hi = sem("pick_ready"), sem("bout_hi")
        u_loaded, ures_loaded = sem("u_loaded"), sem("ures_loaded")
        raw_loaded = sem("raw_loaded")
        x1_saved = [sem("x1_saved0"), sem("x1_saved1")]
        x1t_in, x1t_ready = sem("x1t_in"), sem("x1t_ready")
        logit_in, logit_ready = sem("logit_in"), sem("logit_ready")
        count_ready, rank_in, rank_drained = sem("count_ready"), sem("rank_in"), sem("rank_drained")
        place_ready, route_step = sem("place_ready"), sem("route_step")
        scattered = [[sem(f"scattered{g}{i}") for i in range(2)] for g in range(2)]
        padded = [sem(f"padded{g}") for g in range(2)]
        table_step, table_ready = sem("table_step"), sem("table_ready")
        wgate_in, wgate_ready = sem("wgate_in"), sem("wgate_ready")
        prep_in, prep_hi, prep_lo = sem("prep_in"), sem("prep_hi"), sem("prep_lo")
        result_step, y_place_ready = sem("result_step"), sem("y_place_ready")
        gap_exp, gate_step = sem("gap_exp"), sem("gate_step")
        xs_loaded = [sem(f"xs_loaded{i}") for i in range(RING)]
        xt_in, xhi_ready, xlo_ready = sem("xt_in"), sem("xhi_ready"), sem("xlo_ready")
        h1_in, h2_in, silu_ready, hid_ready = sem("h1_in"), sem("h2_in"), sem("silu_ready"), sem("hid_ready")
        ht_in, hthi_ready, htlo_ready = sem("ht_in"), sem("hthi_ready"), sem("htlo_ready")
        yo_in, ys_ready = sem("yo_in"), sem("ys_ready")
        y_saved = [sem(f"y_saved{i}") for i in range(RING)]
        x1_loaded = sem("x1_loaded")
        y_gathered = [sem(f"y_gathered{i}") for i in range(B)]
        mix_scaled, mix_off_ready = sem("mix_scaled"), sem("mix_off_ready")
        mix_step, mix_ln, mix_rstd, mix_ready = sem("mix_step"), sem("mix_ln"), sem("mix_rstd"), sem("mix_ready")
        ut_in, ut_ready = sem("ut_in"), sem("ut_ready")
        x_in, xpad_ready = sem("x_in"), sem("xpad_ready")
        conv_part, conv_ready, xs_ready = sem("conv_part"), sem("conv_ready"), sem("xs_ready")
        z_in, z_ready = sem("z_in"), sem("z_ready")
        dt_in, dtabs_ready, dtrelu_ready = sem("dt_in"), sem("dtabs_ready"), sem("dtrelu_ready")
        dtexp_ready, dtln_ready, dt_ready, dtx_ready = sem("dtexp_ready"), sem("dtln_ready"), sem("dt_ready"), sem("dtx_ready")
        bc_in, bcval_ready, bchi_ready, bclo_ready = sem("bc_in"), sem("bcval_ready"), sem("bchi_ready"), sem("bclo_ready")
        bB_ready, bC_ready = sem("bB_ready"), sem("bC_ready")
        decay_ready, drive_ready, state_ready = sem("decay_ready"), sem("drive_ready"), sem("state_ready")
        c_ready, prod_ready, y_added = sem("c_ready"), sem("prod_ready"), sem("y_added")
        yz_ready, out_in, res_ready = sem("yz_ready"), sem("out_in"), sem("res_ready")
        stats_ready, agg_part, lnv_ready, rstd_ready, x1_ready = sem("stats_ready"), sem("agg_part"), sem("lnv_ready"), sem("rstd_ready"), sem("x1_ready")
        out_stored = sem("out_stored")

        u_v = u.rearrange("b (n p) d -> b p n d", p=P)
        out_v = out.rearrange("b (n p) d -> b p n d", p=P)
        x1_v = x1_rows.rearrange("(b n p) d -> b p n d", p=P, n=NT)
        col = lambda v: v.rearrange("(p o) -> p o", o=1)
        row = lambda v: v.rearrange("(o p) -> o p", o=1)
        weight_loads = (
            [(win[:], Win), (b_in_c[:], col(b_in)), (wg[:], Wg), (bg_c[:], col(bg)), (cw[:], convw), (cb[:], col(convb)),
             (wdt[:], Wdt), (bdt_c[:], col(bdt)), (a_dn[:], A), (wout[:], Wout)]
            + [(wbc[:, k * N:(k + 1) * N], (Wb, Wc)[k % 2]) for k in range(4)]
            + [(bbc_c[k * N:(k + 1) * N, :], col((bb, bc)[k % 2])) for k in range(4)]
            + [(wgate[:], Wgate)]
            + [(bout_v[q:q + 1, k * D:(k + 1) * D], row(bout)) for k in range(HALF // D) for q in (0, TWO)])
        CONSTANTS = 22
        ROUTE = 21
        TABLE = 16
        MIX = 6
        WEIGHTS = 16 * len(weight_loads)

        block = ctx.enter_context(nc.Block())

        HALVES = [slice(h * HALF, (h + 1) * HALF) for h in range(2)]

        def rows(eng, body):
            body(0, 0, first=True, last=False)
            body(1, 1, first=False, last=False)
            with eng.Fori(0, 2) as pair:
                body(pair * 2 + 2, 0, first=False, last=False)
                body(pair * 2 + 3, 1, first=False, last=False)
            body(6, 0, first=False, last=False)
            body(7, 1, first=False, last=True)

        def all_slots(eng, slot, begin=lambda first, count: None):
            begin(0, RING + 1)
            for s in range(RING + 1):
                slot(s, s % RING, s // RING, s, first=s == 0, last=False)
            with eng.Fori(0, S // RING - 2) as i:
                begin(i * RING + RING, RING + 1)
                for k in range(1, RING + 1):
                    slot(i * RING + (RING + k), k % RING, i + (1 + k // RING), k, first=False, last=False)
            begin(S - RING, RING)
            for s in range(S - RING + 1, S):
                slot(s, s % RING, s // RING, s - (S - RING), first=False, last=s == S - 1)

        preps = ([(1, c, min(HALF, E * H - c), w1) for c in range(0, E * H, HALF)]
                 + [(2, c, min(HALF, E * H - c), w2) for c in range(0, E * H, HALF)]
                 + [(3, c, HALF, None) for c in range(0, E * HP, HALF)])

        def prep_part(i, part):
            kind, cols, width, dst = preps[i]
            if kind == 3:
                return w3[:, cols // P:(cols + width) // P, part, :]
            return dst[part][:, cols:cols + width]

        def prep_shape(i, t):
            return t.rearrange("p (k m) -> p k m", m=P) if preps[i][0] == 3 else t

        def prep_bank(i):
            return ps_y[:, (i % 2) * HALF:(i % 2 + 1) * HALF]

        HE = H + H % 2
        ps_h1 = ps_b[:, 0:HE]
        ps_h2 = ps_b[:, HALF:HALF + HE]
        ps_ht = ps_c[:, 0:HP]
        ps_xt = ps_s[:, 0:P]
        ps_yo = ps_s[:, HALF:HALF + 2 * D]

        def group(b):
            return group_of[b] if isinstance(b, int) else 0

        @block.sync
        def _(sp):
            sp.dma_start(u_in[:], u_v[0]).then_inc(u_loaded, 16)
            sp.wait_ge(const_ready, 11)
            for dst, src in weight_loads:
                sp.dma_start(dst, src).then_inc(w_loaded, 16)

            def body(b, par, first, last):
                if not last:
                    wait(sp, ut_in, b + 1)
                    sp.dma_start(u_in[:], u_v[b + 1]).then_inc(u_loaded, 16)
                wait(sp, res_ready, b)
                sp.dma_start(u_res[:], u_v[b]).then_inc(ures_loaded, 16)
                if first:
                    for raw, w in ((raw1, W1), (raw2, W2)):
                        flat = w.rearrange("e h d -> (e h) d")
                        full = E * H // P
                        sp.dma_start(raw[:, 0:full, :], flat[0:full * P].rearrange("(k p) d -> p k d", p=P)).then_inc(raw_loaded, 16)
                        sp.dma_start(raw[0:E * H - full * P, full, :], flat[full * P:]).then_inc(raw_loaded, 16)
                    sp.dma_start(raw3[:, :, 0:H], W3.rearrange("e d h -> d e h")).then_inc(raw_loaded, 16)
                else:
                    if not isinstance(b, int) or b >= 2:
                        wait(sp, x1_saved[par], (b - par) * 8)
                    wait(sp, x1_ready, b)
                    sp.dma_start(x1_v[b - 1], x1_row[1 - par][:]).then_inc(x1_saved[1 - par], 16)

            rows(sp, body)
            sp.wait_ge(x1_ready, B)
            sp.dma_start(x1_v[B - 1], x1_row[1][:]).then_inc(x1_saved[1], 16)

            def load_slot(s, r):
                if not isinstance(s, int) or s >= RING:
                    wait(sp, xt_in, s - RING + 1)
                tile = sp.value_load(slot_from[0:1, bass.ds(s, 1)], min_val=0, max_val=tiles - 1)
                sp.dma_start(x_slot[:, r, :], x_sorted[bass.ds(tile * P, P)]).then_inc(xs_loaded[r], 16)

            sp.wait_ge(table_ready, 1)
            sp.wait_ge(padded[0], 16 * E)
            for i in range(2):
                sp.wait_ge(scattered[0][i], 16 * 2 * NT * (B - 2) // 2)
            sp.wait_ge(prep_lo, 1)
            for r in range(RING):
                load_slot(r, r)
            for i in range(2):
                sp.wait_ge(x1_saved[i], 16 * B // 2)
            sp.dma_start(x1[:], x1_rows.rearrange("(n p) d -> p n d", p=P)).then_inc(x1_loaded, 16)
            with sp.Fori(1, slots[0] // RING) as i:
                for r in range(RING):
                    load_slot(i * RING + r, r)
            sp.wait_ge(table_ready, 2)
            sp.wait_ge(padded[1], 16 * E)
            for i in range(2):
                sp.wait_ge(scattered[1][i], 16 * 2 * NT)
            with sp.Fori(slots[0] // RING, S // RING) as i:
                for r in range(RING):
                    load_slot(i * RING + r, r)
            for b in range(B):
                sp.wait_ge(mix_ready, b + 1)
                sp.dma_start(out_v[b], x1[:, b * NT:(b + 1) * NT, :]).then_inc(out_stored, 16)
            sp.wait_ge(out_stored, 16 * B)

        @block.gpsimd
        def _(pool):
            stage = prod[0:4 * N, :, :].rearrange("q a (r m) -> q (a r) m", m=P)
            nc.gpsimd.memset(stage, 0.0).then_inc(const_ready, 1)
            nc.gpsimd.memset(ident[:], 0.0).then_inc(const_ready, 1)
            nc.gpsimd.memset(ones[:], 1.0).then_inc(const_ready, 1)
            nc.gpsimd.memset(before[:], 1.0).then_inc(const_ready, 1)
            nc.gpsimd.memset(zeros[:], 0.0).then_inc(const_ready, 1)
            nc.gpsimd.memset(running[:, 0:1], 0.0).then_inc(const_ready, 1)
            nc.gpsimd.memset(ones_e[:], 1.0).then_inc(const_ready, 1)
            nc.gpsimd.memset(raw3[:, :, H:HP], 0.0).then_inc(const_ready, 1)
            nc.gpsimd.memset(x_pad[:], 0.0).then_inc(const_ready, 1)
            nc.gpsimd.memset(bout_v, 0.0).then_inc(const_ready, 1)
            nc.gpsimd.memset(eps_c[:], 1e-5).then_inc(const_ready, 1)
            pool.wait_ge(const_ready, 11)
            nc.gpsimd.affine_select(out=ident[:], in_=ident[:], compare_op=ALU.not_equal, fill=1.0, base=0,
                                    pattern=[[-1, P]], channel_multiplier=1).then_inc(const_ready, 1)
            for part in range(2):
                nc.gpsimd.affine_select(out=stage, in_=stage, compare_op=ALU.not_equal, fill=1.0,
                                        base=-2 * N * part, pattern=[[-1, 2 * N], [0, P]],
                                        channel_multiplier=1).then_inc(const_ready, 1)
                pool.wait_ge(const_ready, 13 + part)
            nc.gpsimd.affine_select(out=before[:], in_=before[:], compare_op=ALU.is_gt, fill=0.0, base=0,
                                    pattern=[[1, P]], channel_multiplier=-1).then_inc(const_ready, 1)
            exact = dict(allow_small_or_imprecise_dtypes=True)
            nc.gpsimd.iota(first_high[:], pattern=[[-1, E], [0, NT]], base=E, channel_multiplier=0, **exact).then_inc(const_ready, 1)
            nc.gpsimd.iota(lane[:], pattern=[[0, 1]], base=0, channel_multiplier=1, **exact).then_inc(const_ready, 1)
            nc.gpsimd.iota(slot_no[:], pattern=[[1, SM]], base=0, channel_multiplier=0, **exact).then_inc(const_ready, 1)
            for g in range(2):
                for t in (base_from[g], base[g]):
                    nc.gpsimd.iota(t[:], pattern=[[region[g], E]], base=first_tile[g] * P, channel_multiplier=0,
                                   **exact).then_inc(const_ready, 1)

            def scatter(b, par, j, choices=(0, 1)):
                for k in choices:
                    nc.gpsimd.indirect_dma_start(x_sorted[:, :], bass.IndirectOffsetOnAxis(place[par][:, k, j:j + 1], 0),
                                                 x1_row[par][:, j, :], None).then_inc(scattered[group(b)][par], 16)

            def pad(g, e):
                if e == 0:
                    pool.wait_ge(table_ready, g + 1)
                nc.gpsimd.indirect_dma_start(x_sorted[:, :], bass.IndirectOffsetOnAxis(pad_place[g][:, e:e + 1], 0),
                                             zeros[:], None).then_inc(padded[g], 16)

            def body(b, par, first, last):
                past = not isinstance(b, int) or b >= 2
                for n in range(N):
                    g = b * N + n
                    if past and n == 0:
                        wait(pool, place_ready, b - 1)
                    if n == 2 and (not isinstance(b, int) or b >= 3):
                        wait(pool, scattered[0][1 - par], (b - 1 - (1 - par)) * (8 * 2 * NT))
                    wait(pool, state_ready, g + 1)
                    wait(pool, c_ready, b * (2 * N) + (2 * n + 2))
                    if first and n == 0:
                        pool.wait_ge(pick_ready, 1)
                    if not first or n >= RING:
                        wait(pool, y_added, g - RING + 1)
                    nc.gpsimd.tensor_tensor(prod[:, n % RING, :], state[:, n % RING, :], c_all[:, n % PAIR, :],
                                            ALU.mult).then_inc(prod_ready, 1)
                    if past:
                        scatter(b - 2, par, n // 2, (n % 2,))

            rows(pool, body)
            for e in range(E):
                pad(0, e)
            for b in (B - 2, B - 1):
                pool.wait_ge(place_ready, b + 1)
                for j in range(NT):
                    scatter(b, b % 2, j)
            for e in range(E):
                pad(1, e)

            for b in range(B):
                if b == 0:
                    pool.wait_ge(y_place_ready, 2)
                    pool.wait_ge(ys_ready, slots[0] + RING)
                if b == group_of.count(0):
                    for r in range(RING):
                        pool.wait_ge(y_saved[r], 16 * S // RING)
                done = y_sorted[0:slots[0] * P, :] if group_of[b] == 0 else y_sorted[:, :]
                for j in range(b * NT, (b + 1) * NT):
                    for k in range(2):
                        nc.gpsimd.indirect_dma_start(y_got[k][:, j, :], None, done,
                                                     bass.IndirectOffsetOnAxis(y_place[:, k, j:j + 1], 0)).then_inc(y_gathered[b], 16)

        @block.tensor
        def _(pe):
            def transpose_u(b):
                wait(pe, u_loaded, (b + 1) * 16)
                for j in range(NT):
                    ins = nc.tensor.transpose(ps_s[:, j * P:(j + 1) * P], u_in[:, j, :], ident[:])
                ins.then_inc(ut_in, 1)

            def project(dst, lhs, rhs, done, part):
                for h in (0, 1) if part is None else (part,):
                    ins = nc.tensor.matmul(dst[:, HALVES[h]], lhs, rhs[:, HALVES[h]], start=True, stop=True)
                if part != 0:
                    ins.then_inc(done, 1)

            def project_x(b, part=None):
                wait(pe, ut_ready, b + 1)
                project(ps_s, win[:], u_t, x_in, part)

            def project_z(b, part=None):
                wait(pe, xpad_ready, b + 1)
                project(ps_s, wg[:], u_t, z_in, part)

            def project_dt(b, part=None):
                wait(pe, xs_ready, b + 1)
                wait(pe, z_ready, b + 1)
                project(ps_s, wdt[:], xs, dt_in, part)

            def project_bc(b, part=None):
                wait(pe, dtabs_ready, b + 1)
                wait(pe, dtrelu_ready, b + 1)
                project(ps_s[0:4 * N], wbc[:], xs, bc_in, part)

            def project_out(b, part=None):
                wait(pe, yz_ready, (b + 1) * 2)
                for h in (0, 1) if part is None else (part,):
                    nc.tensor.matmul(ps_s[:, HALVES[h]], ones_r[:], bout_r[:], start=True, stop=True)
                    for j in range(h * NT // 2, (h + 1) * NT // 2):
                        ins = nc.tensor.matmul(ps_s[:, j * P:(j + 1) * P], yz[:, j * P:(j + 1) * P], wout[:],
                                               start=False, stop=True, skip_group_check=True)
                if part != 0:
                    ins.then_inc(out_in, 1)

            def add_state(b, n):
                wait(pe, prod_ready, b * N + n + 1)
                for h, s in enumerate(HALVES):
                    if n == 0 and (not isinstance(b, int) or b):
                        wait(pe, yz_ready, (b - 1) * 2 + (h + 1))
                    ins = nc.tensor.matmul(ps_y[:, s], ident[:], prod[:, n % RING, s], start=n == 0, stop=n == N - 1)
                ins.then_inc(y_added, 1)

            def broadcast(b, par, n):
                if n == 0:
                    wait(pe, bchi_ready, b + 1)
                    wait(pe, bclo_ready, b + 1)
                for bank, rows_, left, done in ((ps_b, n, drive_ready, bB_ready), (ps_c, N + n, c_ready, bC_ready)):
                    for h, s in enumerate(HALVES):
                        if not isinstance(b, int) or b * N + n >= 1:
                            wait(pe, left, b * (2 * N) + (2 * n + h - 1))
                        nc.tensor.matmul(bank[:, s], pick[:, rows_, :], bc_split[par][:, s], start=True, stop=True).then_inc(done, 1)

            def transpose_x1(b, par):
                wait(pe, x1_ready, b + 1)
                for j in range(NT):
                    ins = nc.tensor.transpose(ps_s[:, j * P:(j + 1) * P], x1_row[par][:, j, :], ident[:])
                ins.then_inc(x1t_in, 1)

            def route_logits(b):
                wait(pe, x1t_ready, b + 1)
                for j in range(NT):
                    ins = nc.tensor.matmul(ps_s[:, j * E:(j + 1) * E], x1_t[:, j * P:(j + 1) * P], wgate_t[:],
                                           start=True, stop=True)
                ins.then_inc(logit_in, 1)

            def rank_tokens(b):
                wait(pe, count_ready, b + 1)
                nc.tensor.matmul(ps_s[:, 0:E], before[:], count[:], start=True, stop=True)
                nc.tensor.matmul(ps_s[:, E:2 * E], ones[:], count[:], start=True, stop=True).then_inc(rank_in, 1)

            pe.wait_ge(const_ready, CONSTANTS)
            transpose_u(0)
            pe.wait_ge(w_loaded, WEIGHTS)
            nc.tensor.transpose(ps_y[:, 0:E], wgate[:], ident[0:E, 0:E]).then_inc(wgate_in, 1)
            project_x(0)
            project_z(0)
            project_dt(0)
            project_bc(0)
            pe.wait_ge(pick_ready, 1)

            def body(b, par, first, last):
                for n in range(N):
                    broadcast(b, par, n)
                    if n >= LAG:
                        add_state(b, n - LAG)
                    elif not first:
                        add_state(b - 1, n - LAG + N)
                    if not last:
                        if n == 0:
                            if first:
                                wait(pe, bcval_ready, 1)
                            elif isinstance(b, int) and b == 1:
                                wait(pe, bcval_ready, 2)
                            else:
                                wait(pe, rank_drained, b - 1)
                            transpose_u(b + 1)
                        if n in (1, 2):
                            project_x(b + 1, n - 1)
                        if n == 3:
                            project_z(b + 1)
                        if n in (7, 8):
                            if not first:
                                wait(pe, res_ready, b)
                            project_dt(b + 1, n - 7)
                        if n == 9:
                            project_bc(b + 1)
                    if not first:
                        if n == 5:
                            if last:
                                wait(pe, rank_drained, b - 1)
                            else:
                                wait(pe, z_ready, b + 2)
                            project_out(b - 1)
                        if n == 10:
                            if last:
                                wait(pe, res_ready, b)
                            else:
                                wait(pe, bcval_ready, b + 2)
                            transpose_x1(b - 1, 1 - par)
                        if n == 11:
                            route_logits(b - 1)
                        if n == 14:
                            wait(pe, logit_ready, b)
                            rank_tokens(b - 1)

            rows(pe, body)
            for n in range(N - LAG, N):
                add_state(B - 1, n)
            pe.wait_ge(rank_drained, B - 1)
            project_out(B - 1)
            pe.wait_ge(res_ready, B)
            transpose_x1(B - 1, 1)
            route_logits(B - 1)
            pe.wait_ge(logit_ready, B)
            rank_tokens(B - 1)

            pe.wait_ge(raw_loaded, 16 * 5)
            for i, (kind, cols, width, _) in enumerate(preps):
                if i >= 2:
                    pe.wait_ge(prep_lo, i - 1)
                for c in range(0, width, P):
                    if kind == 3:
                        src, n = raw3.rearrange("d e h -> d (e h)")[:, cols + c:cols + c + P], P
                    else:
                        n = min(P, width - c)
                        src = (raw1, raw2)[kind - 1][0:n, (cols + c) // P, :]
                    ins = nc.tensor.transpose(prep_bank(i)[:, c:c + n], src, ident[0:src.shape[0], 0:src.shape[0]])
                ins.then_inc(prep_in, 1)

            expert = []

            def load_experts(first, count):
                expert[:] = nc.values_load_multi_w_load_instructions(
                    slot_expert[0:1, bass.ds(first, count)], [mybir.EngineType.PE], min_val=0, max_val=E - 1,
                    skip_runtime_bounds_check_because="tables() takes an expert below E or the first")[1]

            def three(dst, a_hi, a_lo, b_hi, b_lo, start=True, stop=True):
                nc.tensor.matmul(dst, a_hi, b_hi, start=start, stop=False)
                nc.tensor.matmul(dst, a_hi, b_lo, start=False, stop=False)
                return nc.tensor.matmul(dst, a_lo, b_hi, start=False, stop=stop)

            def turn_x(s, r, turn):
                wait(pe, xs_loaded[r], (turn + 1) * 16)
                nc.tensor.transpose(ps_xt, x_slot[:, r, :], ident[:]).then_inc(xt_in, 1)

            def hidden(s, p, e, nxt):
                wait(pe, xlo_ready, s + 1)
                cut = bass.ds(e * H, H + H % 2)
                three(ps_h1, x_hi[:, p, :], x_lo[:, p, :], w1[0][:, cut], w1[1][:, cut]).then_inc(h1_in, 1)
                if nxt is not None:
                    turn_x(*nxt)
                three(ps_h2, x_hi[:, p, :], x_lo[:, p, :], w2[0][:, cut], w2[1][:, cut]).then_inc(h2_in, 1)

            def turn_hidden(s, p):
                wait(pe, hid_ready, s + 1)
                for c in range(HC):
                    ins = nc.tensor.transpose(ps_ht[:, c * P:(c + 1) * P], hid[:, p, c * P:(c + 1) * P], ident[:])
                ins.then_inc(ht_in, 1)

            def out_rows(s, e):
                wait(pe, hthi_ready, s + 1)
                wait(pe, ys_ready, s)
                chunk = lambda c, both: w3.rearrange("p k i m -> p (k i m)")[:, bass.ds(e * (2 * HP) + 2 * P * c, P * (1 + both))]
                for c in range(HC):
                    nc.tensor.matmul(ps_yo, hid_hi[:, c * P:(c + 1) * P], chunk(c, True), start=c == 0, stop=c == HC - 1)
                wait(pe, htlo_ready, s + 1)
                for c in range(HC):
                    ins = nc.tensor.matmul(ps_yo[:, 0:D], hid_lo[:, c * P:(c + 1) * P], chunk(c, False), start=False,
                                           stop=c == HC - 1, skip_group_check=True)
                ins.then_inc(yo_in, 1)

            pe.wait_ge(prep_lo, len(preps))
            pe.wait_ge(gate_step, 0 + 3)
            pe.wait_ge(table_ready, 2)
            turn_x(0, 0, 0)

            def slot(s, r, turn, at, first, last):
                if not first:
                    turn_hidden(s - 1, (r - 1) % 2)
                hidden(s, r % 2, expert[at], None if last else (s + 1, (r + 1) % RING, turn + (r + 1) // RING))
                if not first:
                    out_rows(s - 1, expert[at - 1])

            all_slots(pe, slot, load_experts)
            turn_hidden(S - 1, (S - 1) % 2)
            out_rows(S - 1, expert[RING - 1])

        @block.scalar
        def _(act):
            def evacuate_u(b):
                wait(act, ut_in, b + 1)
                wait(act, z_in, b)
                nc.scalar.copy(u_t[:], ps_s[:]).then_inc(ut_ready, 1)

            def evacuate_x(b):
                wait(act, x_in, b + 1)
                wait(act, conv_ready, b)
                nc.scalar.activation(x_pad[:, 1:T + 1], ps_s[:], ACT.Identity, bias=b_in_c[:]).then_inc(xpad_ready, 1)

            def silu_z(b, par):
                wait(act, z_in, b + 1)
                wait(act, yz_ready, (b - 1) * 2)
                nc.scalar.activation(z[par][:], ps_s[:], ACT.Silu, bias=bg_c[:]).then_inc(z_ready, 1)

            def silu_x(b):
                wait(act, conv_ready, b + 1)
                nc.scalar.activation(xs[:], xs[:], ACT.Silu).then_inc(xs_ready, 1)
                act.preload_act_table_set(EXP_LN)

            def abs_dt(b):
                wait(act, dt_in, b + 1)
                wait(act, dt_ready, b)
                nc.scalar.activation(dt_abs[:], ps_s[:], ACT.Abs, bias=bdt_c[:]).then_inc(dtabs_ready, 1)

            def relu_dt(b):
                wait(act, dt_ready, b)
                nc.scalar.activation(dt_relu[:], ps_s[:], ACT.Relu, bias=bdt_c[:]).then_inc(dtrelu_ready, 1)

            def exp_dt(b):
                wait(act, dtabs_ready, b + 1)
                nc.scalar.activation(dt_abs[:], dt_abs[:], ACT.Exp, scale=-1.0).then_inc(dtexp_ready, 1)

            def ln_dt(b):
                wait(act, dtexp_ready, b + 1)
                nc.scalar.activation(dt_abs[:], dt_abs[:], ACT.Ln, bias=1.0).then_inc(dtln_ready, 1)

            def evacuate_bc(b):
                wait(act, bc_in, b + 1)
                wait(act, bclo_ready, b)
                nc.scalar.activation(bc_val[:], ps_s[0:4 * N, :], ACT.Identity, bias=bbc_c[:]).then_inc(bcval_ready, 1)

            def round_bc(b, par):
                wait(act, bcval_ready, b + 1)
                wait(act, bC_ready, (b - 1) * (2 * N))
                nc.scalar.copy(bc_split[par][:], bc_val[:]).then_inc(bchi_ready, 1)

            def row_ln(b):
                wait(act, agg_part, 3 * b + 3)
                nc.scalar.activation(lnv[:], var[:], ACT.Ln, bias=eps_c[:], scale=1.0 / P).then_inc(lnv_ready, 1)

            def row_rstd(b):
                wait(act, lnv_ready, b + 1)
                nc.scalar.activation(rstd[:], lnv[:], ACT.Exp, scale=-0.5).then_inc(rstd_ready, 1)

            def evacuate_x1(b):
                wait(act, x1t_in, b + 1)
                wait(act, logit_in, b)
                nc.scalar.copy(x1_t[:], ps_s[:]).then_inc(x1t_ready, 1)

            act.preload_act_table_set(EXP_LN)
            act.wait_ge(const_ready, CONSTANTS)
            act.wait_ge(w_loaded, WEIGHTS)
            act.wait_ge(wgate_in, 1)
            nc.scalar.copy(wgate_t[:], ps_y[:, 0:E]).then_inc(wgate_ready, 1)
            nc.scalar.copy(ones_r[:], ones[0:2 * TWO, :])
            nc.scalar.copy(bout_r[:], bout_v).then_inc(bout_hi, 1)
            evacuate_u(0)
            evacuate_x(0)
            silu_z(0, 0)
            silu_x(0)
            nc.scalar.copy(pick[:], prod[0:4 * N, :, :].rearrange("q a (r m) -> q (a r) m", m=P)).then_inc(pick_ready, 1)
            abs_dt(0)
            relu_dt(0)
            evacuate_bc(0)
            exp_dt(0)
            round_bc(0, 0)
            ln_dt(0)

            def body(b, par, first, last):
                for n in range(N):
                    g = b * N + n
                    if n == 0:
                        wait(act, dt_ready, b + 1)
                    if not first or n >= RING:
                        wait(act, state_ready, g - RING + 1)
                    nc.scalar.activation(decay[:, n % RING, :], dt[par][:], ACT.Exp,
                                         scale=a_dn[:, n:n + 1]).then_inc(decay_ready, 1)
                    if not first or n >= PAIR:
                        wait(act, prod_ready, g - PAIR + 1)
                    for h, s in enumerate(HALVES):
                        wait(act, bC_ready, b * (2 * N) + (2 * n + h + 1))
                        nc.scalar.copy(c_all[:, n % PAIR, s], ps_c[:, s]).then_inc(c_ready, 1)
                    if not first:
                        if n == 8:
                            row_ln(b - 1)
                            row_rstd(b - 1)
                        if n == 10:
                            evacuate_x1(b - 1)
                    if not last:
                        if n == 0:
                            evacuate_u(b + 1)
                        if n == 2:
                            evacuate_x(b + 1)
                        if n == 4:
                            silu_z(b + 1, 1 - par)
                            silu_x(b + 1)
                        if n == 8:
                            abs_dt(b + 1)
                            relu_dt(b + 1)
                        if n == 9:
                            evacuate_bc(b + 1)
                            exp_dt(b + 1)
                        if n == 10:
                            ln_dt(b + 1)
                        if n == 11:
                            round_bc(b + 1, 1 - par)

            rows(act, body)
            row_ln(B - 1)
            row_rstd(B - 1)
            evacuate_x1(B - 1)
            act.wait_ge(route_step, B * ROUTE)
            nc.scalar.activation(gate2[:], gap[:], ACT.Exp).then_inc(gap_exp, 1)

            for i, (kind, cols, width, dst) in enumerate(preps):
                act.wait_ge(prep_in, i + 1)
                nc.scalar.copy(prep_part(i, 0), prep_shape(i, prep_bank(i)[:, 0:width])).then_inc(prep_hi, 1)

            def round_x(s, p):
                wait(act, xt_in, s + 1)
                nc.scalar.copy(x_hi[:, p, :], ps_xt).then_inc(xhi_ready, 1)

            def silu_hidden(s, p):
                wait(act, h1_in, s + 1)
                nc.scalar.activation(act1[:, p, :], ps_h1[:, 0:H], ACT.Silu).then_inc(silu_ready, 1)

            def round_hidden(s):
                wait(act, ht_in, s + 1)
                nc.scalar.copy(hid_hi[:], ps_ht).then_inc(hthi_ready, 1)

            def save_slot(s, r):
                wait(act, ys_ready, s + 1)
                act.dma_start(y_sorted[bass.ds(s * P, P)], y_slot[:, r, :]).then_inc(y_saved[r], 16)

            act.wait_ge(table_ready, 2)
            act.preload_act_table(ACT.Silu)
            round_x(0, 0)

            def slot(s, r, turn, at, first, last):
                if not first:
                    round_hidden(s - 1)
                silu_hidden(s, r % 2)
                if not last:
                    round_x(s + 1, (r + 1) % 2)
                if not isinstance(s, int) or s >= 2:
                    save_slot(s - 2, (r - 2) % RING)

            all_slots(act, slot)
            round_hidden(S - 1)
            for s in (S - 2, S - 1):
                save_slot(s, s % RING)

            act.preload_act_table_set(EXP_LN)
            def scale_first(b):
                act.wait_ge(y_gathered[b], 16 * 2 * NT)
                for j in range(b * NT, (b + 1) * NT):
                    ins = nc.scalar.activation(y_got[0][:, j, :], y_got[0][:, j, :], ACT.Copy, scale=gate1[:, j:j + 1])
                ins.then_inc(mix_scaled, 1)

            def mix_deviation(b):
                p = b % 2
                act.wait_ge(mix_step, MIX * (b + 1))
                nc.scalar.activation(mix_lnv[:, p, :], mix_var[:, p, :], ACT.Ln, bias=eps_c[:], scale=1.0 / P).then_inc(mix_ln, 1)
                act.wait_ge(mix_ln, b + 1)
                nc.scalar.activation(mix_rs[:, p, :], mix_lnv[:, p, :], ACT.Exp, scale=-0.5).then_inc(mix_rstd, 1)

            def mix_normalise(b):
                act.wait_ge(mix_off_ready, b + 1)
                for j in range(NT):
                    ins = nc.scalar.activation(x1[:, b * NT + j, :], x1[:, b * NT + j, :], ACT.Identity,
                                               bias=mix_off[:, b % 2, j:j + 1], scale=mix_rs[:, b % 2, j:j + 1])
                ins.then_inc(mix_ready, 1)

            for b in range(B):
                scale_first(b)
                if b:
                    mix_normalise(b - 1)
                mix_deviation(b)
            mix_normalise(B - 1)

        @block.vector
        def _(dve):
            def conv(b, part=None):
                if part != 1:
                    conv_two(b)
                if part != 0:
                    conv_last(b)

            def conv_two(b):
                wait(dve, xpad_ready, b + 1)
                wait(dve, dtx_ready, b)
                wait(dve, bc_in, b)
                nc.vector.tensor_scalar(xs[:], x_pad[:, 0:T], cw[:, 0:1], cb[:], ALU.mult, ALU.add).then_inc(conv_part, 1)
                wait(dve, conv_part, 2 * b + 1)
                nc.vector.scalar_tensor_tensor(out=xs[:], in0=x_pad[:, 1:T + 1], scalar=cw[:, 1:2], in1=xs[:],
                                               op0=ALU.mult, op1=ALU.add).then_inc(conv_part, 1)

            def conv_last(b):
                wait(dve, conv_part, 2 * b + 2)
                nc.vector.scalar_tensor_tensor(out=xs[:], in0=x_pad[:, 2:T + 2], scalar=cw[:, 2:3], in1=xs[:],
                                               op0=ALU.mult, op1=ALU.add).then_inc(conv_ready, 1)

            def sum_dt(b, par):
                wait(dve, dtln_ready, b + 1)
                wait(dve, dtrelu_ready, b + 1)
                wait(dve, dtx_ready, b - 1)
                wait(dve, decay_ready, (b - 1) * N)
                nc.vector.tensor_tensor(dt[par][:], dt_relu[:], dt_abs[:], ALU.add).then_inc(dt_ready, 1)

            def mul_dtx(b, par):
                wait(dve, dt_ready, b + 1)
                wait(dve, drive_ready, (b - 1) * (2 * N))
                nc.vector.tensor_tensor(dtx[par][:], dt[par][:], xs[:], ALU.mult).then_inc(dtx_ready, 1)

            def low_bc(b, par):
                wait(dve, bchi_ready, b + 1)
                lo = slice(2 * N, 4 * N)
                nc.vector.tensor_tensor(bc_split[par][lo, :], bc_val[lo, :], bc_split[par][lo, :].bitcast(F32),
                                        ALU.subtract).then_inc(bclo_ready, 1)

            def drive_of(b, par, n):
                g = b * N + n
                if n == 0:
                    wait(dve, dtx_ready, b + 1)
                if not isinstance(g, int) or g >= RING:
                    wait(dve, prod_ready, g - RING + 1)
                for h, s in enumerate(HALVES):
                    wait(dve, bB_ready, b * (2 * N) + (2 * n + h + 1))
                    nc.vector.tensor_tensor(state[:, n % RING, s], dtx[par][:, s], ps_b[:, s], ALU.mult).then_inc(drive_ready, 1)

            def scan(b, n):
                g = b * N + n
                wait(dve, drive_ready, b * (2 * N) + (2 * n + 2))
                wait(dve, decay_ready, g + 1)
                nc.vector.tensor_tensor_scan(state[:, n % RING, :], decay[:, n % RING, :], state[:, n % RING, :], 0.0,
                                             ALU.mult, ALU.add).then_inc(state_ready, 1)

            def gate_y(b, par):
                wait(dve, y_added, (b + 1) * N)
                wait(dve, z_ready, b + 1)
                wait(dve, logit_in, b)
                for s in HALVES:
                    nc.vector.tensor_tensor(yz[:, s], ps_y[:, s], z[par][:, s], ALU.mult).then_inc(yz_ready, 1)

            def residual(b, par):
                wait(dve, out_in, b + 1)
                wait(dve, ures_loaded, (b + 1) * 16)
                nc.vector.tensor_tensor(res[:].rearrange("p n d -> p (n d)"), ps_s[:],
                                        u_res[:].rearrange("p n d -> p (n d)"), ALU.add).then_inc(res_ready, 1)

            def statistics(b):
                wait(dve, res_ready, b + 1)
                for j in range(NT):
                    ins = nc.vector.bn_stats(stats[:, j, :], res[:, j, :])
                ins.then_inc(stats_ready, 1)

            def aggregate(b):
                wait(dve, stats_ready, b + 1)
                nc.vector.tensor_tensor(mean[:], stats[:, :, 1], stats[:, :, 4], ALU.add)
                nc.vector.tensor_tensor(dif[:], stats[:, :, 1], stats[:, :, 4], ALU.subtract)
                nc.vector.tensor_tensor(sq[:], stats[:, :, 2], stats[:, :, 5], ALU.add).then_inc(agg_part, 1)
                wait(dve, agg_part, 3 * b + 1)
                nc.vector.tensor_scalar(mean[:], mean[:], 0.5, None, ALU.mult)
                nc.vector.tensor_tensor(dif[:], dif[:], dif[:], ALU.mult).then_inc(agg_part, 1)
                wait(dve, agg_part, 3 * b + 2)
                nc.vector.scalar_tensor_tensor(out=var[:], in0=dif[:], scalar=P / 4.0, in1=sq[:],
                                               op0=ALU.mult, op1=ALU.add).then_inc(agg_part, 1)

            def normalise(b, par, part=None):
                wait(dve, rstd_ready, b + 1)
                if isinstance(b, int) and b == B - 1:
                    dve.wait_ge(scattered[0][par], 16 * 2 * NT * (B - 2) // 2)
                else:
                    wait(dve, prod_ready, (b + 1) * N + 3)
                for j in range(NT) if part is None else range(part * NT // 2, (part + 1) * NT // 2):
                    ins = nc.vector.tensor_scalar(x1_row[par][:, j, :], res[:, j, :], mean[:, j:j + 1], rstd[:, j:j + 1],
                                                  ALU.subtract, ALU.mult)
                if part != 0:
                    ins.then_inc(x1_ready, 1)

            by_tile = lambda t: t[:].rearrange("p e j -> p j e")
            each_expert = lambda t: t[:].unsqueeze(1).broadcast_to([P, E, NT])
            each_tile = lambda t: t[:].unsqueeze(2).broadcast_to([P, E, NT])
            flat = lambda t: t[:].rearrange("p e j -> p (e j)")

            def choose(b, part=None):
                k = [6 if part == 1 else 0]

                def link(ins):
                    k[0] += 1
                    ins.then_inc(route_step, 1)
                    wait(dve, route_step, b * ROUTE + k[0])

                def pick_top(values, top, dst):
                    link(nc.vector.tensor_reduce(dst[:], by_tile(values), AX.X, ALU.max))
                    link(nc.vector.tensor_tensor(top[:], values[:], each_expert(dst), ALU.is_equal))
                    link(nc.vector.tensor_tensor(top[:], top[:], first_high[:], ALU.mult))
                    link(nc.vector.tensor_reduce(index[:], by_tile(top), AX.X, ALU.max))
                    link(nc.vector.tensor_tensor(top[:], first_high[:], each_expert(index), ALU.is_equal))

                if part != 1:
                    wait(dve, logit_in, b + 1)
                    ins = nc.vector.tensor_copy(logit[:], ps_s[:, 0:E * NT].rearrange("p (j e) -> p e j", e=E))
                    ins.then_inc(logit_ready, 1)
                    wait(dve, logit_ready, b + 1)
                    pick_top(logit, top1, best)
                    link(nc.vector.scalar_tensor_tensor(out=flat(logit2), in0=flat(top1), scalar=-3.0e38, in1=flat(logit),
                                                        op0=ALU.mult, op1=ALU.add))
                if part == 0:
                    return
                pick_top(logit2, top2, best2)
                nc.vector.tensor_tensor(gap[:, bass.ds(b * NT, NT)], best2[:], best[:], ALU.subtract)
                link(nc.vector.tensor_tensor(chosen[:], top1[:], top2[:], ALU.add))
                link(nc.vector.tensor_tensor_scan(running[:, 1:], ones[:, 0:E * NT], flat(chosen), 0.0, ALU.mult, ALU.add))
                nc.vector.tensor_tensor(count[:], running[:, NT::NT], running[:, 0:E * NT:NT], ALU.subtract).then_inc(count_ready, 1)
                assert k[0] == ROUTE - 8

            def locate(b, par):
                g = group(b)
                k = [ROUTE - 8]

                def link(ins):
                    k[0] += 1
                    ins.then_inc(route_step, 1)
                    wait(dve, route_step, b * ROUTE + k[0])

                wait(dve, count_ready, b + 1)
                link(nc.vector.tensor_tensor(offset[:], base[g][:], running[:, 0:E * NT:NT], ALU.subtract))
                wait(dve, rank_in, b + 1)
                link(nc.vector.tensor_tensor(offset[:], offset[:], ps_s[:, 0:E], ALU.add))
                nc.vector.tensor_tensor(base[g][:], base[g][:], ps_s[:, E:2 * E], ALU.add).then_inc(rank_drained, 1)
                link(nc.vector.tensor_tensor(flat(rank), running[:, 1:], flat(chosen), ALU.subtract))
                link(nc.vector.tensor_tensor(rank[:], rank[:], each_tile(offset), ALU.add))
                for i, top in enumerate((top1, top2)):
                    link(nc.vector.tensor_tensor(part[:], top[:], rank[:], ALU.mult))
                    link(nc.vector.tensor_reduce(place_f[:, i, :], by_tile(part), AX.X, ALU.add))
                nc.vector.tensor_copy(place[par][:], place_f[:])
                nc.vector.tensor_copy(places[:, :, bass.ds(b * NT, NT)], place_f[:]).then_inc(place_ready, 1)
                assert k[0] == ROUTE

            def tables(g):
                n, o, k = slots[g], first_slot[g], [g * TABLE]

                def link(ins):
                    k[0] += 1
                    ins.then_inc(table_step, 1)
                    dve.wait_ge(table_step, k[0])

                number, one = slot_no[:, 0:n], slice(0, 1)
                by_slot = lambda t: t[one, :].unsqueeze(1).broadcast_to([1, n, E])
                dve.wait_ge(rank_drained, B - 2 if g == 0 else B)
                link(nc.vector.tensor_tensor(pad_place[g][:], base[g][:], lane[:].broadcast_to([P, E]), ALU.add))
                link(nc.vector.tensor_tensor(n_tiles[:], base[g][:], base_from[g][:], ALU.subtract))
                link(nc.vector.tensor_scalar(n_tiles_i[:], n_tiles[:], float(P - 1), None, ALU.add))
                link(nc.vector.tensor_scalar(n_tiles_i[:], n_tiles_i[:], 7, None, ALU.logical_shift_right))
                link(nc.vector.tensor_copy(n_tiles[:], n_tiles_i[:]))
                link(nc.vector.tensor_tensor_scan(done_at[:], ones_e[:], n_tiles[:], 0.0, ALU.mult, ALU.add))
                link(nc.vector.tensor_scalar(skip[g][:], n_tiles[:], -1.0, float(region[g] // P), ALU.mult, ALU.add))
                link(nc.vector.tensor_tensor(passed[:, 0:n, :], number.unsqueeze(2).broadcast_to([1, n, E]), by_slot(done_at), ALU.is_ge))
                link(nc.vector.tensor_reduce(t_expert[:, 0:n], passed[:, 0:n, :], AX.X, ALU.add))
                link(nc.vector.tensor_tensor(passed[:, 0:n, :], passed[:, 0:n, :], by_slot(skip[g]), ALU.mult))
                link(nc.vector.tensor_reduce(t_tile[:, 0:n], passed[:, 0:n, :], AX.X, ALU.add))
                link(nc.vector.tensor_scalar(t_used[:, 0:n], number, done_at[one, E - 1:E], None, ALU.is_lt))
                link(nc.vector.tensor_tensor(slot_expert[:, o:o + n], t_expert[:, 0:n], t_used[:, 0:n], ALU.mult))
                link(nc.vector.scalar_tensor_tensor(out=t_tile[:, 0:n], in0=t_tile[:, 0:n], scalar=float(first_tile[g]), in1=number,
                                                    op0=ALU.add, op1=ALU.add))
                link(nc.vector.scalar_tensor_tensor(out=t_tile[:, 0:n], in0=t_tile[:, 0:n], scalar=-float(first_tile[g]),
                                                    in1=t_used[:, 0:n], op0=ALU.add, op1=ALU.mult))
                link(nc.vector.tensor_scalar(slot_from[:, o:o + n], t_tile[:, 0:n], float(first_tile[g]), None, ALU.add))
                assert k[0] == (g + 1) * TABLE
                nc.vector.tensor_copy(t_tile[:, 0:1], number[:, 0:1]).then_inc(table_ready, 1)

            def find_results():
                step = [0]

                def link(ins):
                    step[0] += 1
                    ins.then_inc(result_step, 1)
                    dve.wait_ge(result_step, step[0])

                dve.wait_ge(table_ready, 2)
                for g in range(2):
                    first = group_of.index(g) * NT
                    n = 2 * tokens[g] // P
                    gaps = hid[:].rearrange("p a h -> p (a h)")[:, 0:n * E].rearrange("p (i t e) -> p i t e", i=2, e=E)
                    total = y_sum[:, :, first:first + n // 2]
                    mine = places[:, :, first:first + n // 2]
                    spread = lambda t: t[:].unsqueeze(1).unsqueeze(1).broadcast_to([P, 2, n // 2, E])
                    link(nc.vector.tensor_scalar(total, mine, -float(region[g]), None, ALU.add))
                    link(nc.vector.tensor_tensor(gaps, total.unsqueeze(3).broadcast_to([P, 2, n // 2, E]), spread(base_from[g]), ALU.is_ge))
                    link(nc.vector.tensor_tensor(gaps, gaps, spread(skip[g]), ALU.mult))
                    link(nc.vector.tensor_reduce(total, gaps, AX.X, ALU.add))
                    link(nc.vector.scalar_tensor_tensor(out=total, in0=total, scalar=-float(P), in1=mine, op0=ALU.mult, op1=ALU.add))
                    nc.vector.tensor_scalar(y_place[:, :, first:first + n // 2], total,
                                            float((first_slot[g] - first_tile[g]) * P), None, ALU.add).then_inc(y_place_ready, 1)

            dve.wait_ge(w_loaded, WEIGHTS)
            dve.wait_ge(const_ready, CONSTANTS)
            dve.wait_ge(bout_hi, 1)
            nc.vector.tensor_tensor(bout_r[TWO:, :], bout_v[TWO:, :], bout_r[TWO:, :].bitcast(F32), ALU.subtract)
            conv(0)
            sum_dt(0, 0)
            mul_dtx(0, 0)
            low_bc(0, 0)

            def body(b, par, first, last):
                for n in range(N):
                    drive_of(b, par, n)
                    if n == LAG and not first:
                        gate_y(b - 1, 1 - par)
                    if n:
                        scan(b, n - 1)
                    elif not first:
                        scan(b - 1, N - 1)
                    if not first:
                        if n == 6:
                            residual(b - 1, 1 - par)
                        if n == 7:
                            statistics(b - 1)
                            aggregate(b - 1)
                        if n == 9:
                            normalise(b - 1, 1 - par)
                        if n == 12:
                            choose(b - 1, 0)
                        if n == 13:
                            choose(b - 1, 1)
                        if n == 15:
                            locate(b - 1, 1 - par)
                    if last and n == 1:
                        tables(0)
                    if not last:
                        if n == 3:
                            conv(b + 1)
                        if n == 11:
                            sum_dt(b + 1, 1 - par)
                        if n == 14:
                            low_bc(b + 1, 1 - par)
                            mul_dtx(b + 1, 1 - par)

            rows(dve, body)
            scan(B - 1, N - 1)
            gate_y(B - 1, 1)
            residual(B - 1, 1)
            statistics(B - 1)
            aggregate(B - 1)
            normalise(B - 1, 1)
            choose(B - 1)
            locate(B - 1, 1)
            tables(1)
            find_results()
            dve.wait_ge(gap_exp, 1)
            nc.vector.tensor_scalar(gate1[:], gate2[:], 1.0, None, ALU.add).then_inc(gate_step, 1)
            dve.wait_ge(gate_step, 1)
            nc.vector.reciprocal(gate1[:], gate1[:]).then_inc(gate_step, 1)
            dve.wait_ge(gate_step, 2)
            nc.vector.tensor_tensor(gate2[:], gate2[:], gate1[:], ALU.mult)
            nc.vector.memset(hid[:, :, H:HP], 0.0).then_inc(gate_step, 1)

            for i, (kind, cols, width, dst) in enumerate(preps):
                dve.wait_ge(prep_hi, i + 1)
                nc.vector.tensor_tensor(prep_part(i, 1), prep_shape(i, prep_bank(i)[:, 0:width]), prep_part(i, 0).bitcast(F32),
                                        ALU.subtract).then_inc(prep_lo, 1)
            for w in w1 + w2:
                nc.vector.memset(w[:, E * H:].bitcast(F32), 0.0)

            def low_x(s, p):
                wait(dve, xhi_ready, s + 1)
                nc.vector.tensor_tensor(x_lo[:, p, :], ps_xt, x_hi[:, p, :].bitcast(F32), ALU.subtract).then_inc(xlo_ready, 1)

            def multiply(s, p):
                wait(dve, silu_ready, s + 1)
                wait(dve, h2_in, s + 1)
                nc.vector.tensor_tensor(hid[:, p, 0:H], act1[:, p, :], ps_h2[:, 0:H], ALU.mult).then_inc(hid_ready, 1)

            def low_hidden(s):
                wait(dve, hthi_ready, s + 1)
                nc.vector.tensor_tensor(hid_lo[:], ps_ht, hid_hi[:].bitcast(F32), ALU.subtract).then_inc(htlo_ready, 1)

            def evacuate_y(s, r, turn):
                wait(dve, yo_in, s + 1)
                wait(dve, y_saved[r], turn * 16)
                nc.vector.tensor_reduce(y_slot[:, r, :], ps_yo.rearrange("p (i d) -> p d i", i=2), AX.X, ALU.add).then_inc(ys_ready, 1)

            low_x(0, 0)

            def slot(s, r, turn, at, first, last):
                if not first:
                    low_hidden(s - 1)
                multiply(s, r % 2)
                if not last:
                    low_x(s + 1, (r + 1) % 2)
                if not first:
                    evacuate_y(s - 1, (r - 1) % RING, turn - (1 if r == 0 else 0))

            all_slots(dve, slot)
            low_hidden(S - 1)
            evacuate_y(S - 1, (S - 1) % RING, S // RING - 1)

            dve.wait_ge(x1_loaded, 16)

            def weigh(b):
                wait(dve, y_gathered[b], 16 * 2 * NT)
                for j in range(b * NT, (b + 1) * NT):
                    ins = nc.vector.scalar_tensor_tensor(out=x1[:, j, :], in0=y_got[1][:, j, :], scalar=gate2[:, j:j + 1],
                                                         in1=x1[:, j, :], op0=ALU.mult, op1=ALU.add)
                ins.then_inc(mix_step, 1)

            def mix(b):
                at, rows_ = MIX * b, slice(b * NT, (b + 1) * NT)
                dve.wait_ge(mix_step, at + 1)
                dve.wait_ge(mix_scaled, b + 1)
                nc.vector.tensor_tensor(x1[:, rows_, :], x1[:, rows_, :], y_got[0][:, rows_, :], ALU.add).then_inc(mix_step, 1)
                dve.wait_ge(mix_step, at + 2)
                for j in range(NT):
                    ins = nc.vector.bn_stats(stats[:, j, :], x1[:, b * NT + j, :])
                ins.then_inc(mix_step, 1)

            def mix_statistics(b):
                at, p = MIX * b + 3, b % 2
                dve.wait_ge(mix_step, at)
                wait(dve, mix_ln, b - 1)
                nc.vector.tensor_tensor(mix_mean[:, p, :], stats[:, :, 1], stats[:, :, 4], ALU.add)
                nc.vector.tensor_tensor(dif[:], stats[:, :, 1], stats[:, :, 4], ALU.subtract)
                nc.vector.tensor_tensor(sq[:], stats[:, :, 2], stats[:, :, 5], ALU.add).then_inc(mix_step, 1)
                dve.wait_ge(mix_step, at + 1)
                nc.vector.tensor_tensor(dif[:], dif[:], dif[:], ALU.mult).then_inc(mix_step, 1)
                dve.wait_ge(mix_step, at + 2)
                nc.vector.scalar_tensor_tensor(out=mix_var[:, p, :], in0=dif[:], scalar=P / 4.0, in1=sq[:],
                                               op0=ALU.mult, op1=ALU.add).then_inc(mix_step, 1)

            def mix_offset(b):
                wait(dve, mix_rstd, b + 1)
                wait(dve, mix_ready, b - 1)
                nc.vector.scalar_tensor_tensor(out=mix_off[:, b % 2, :], in0=mix_mean[:, b % 2, :], scalar=-0.5,
                                               in1=mix_rs[:, b % 2, :], op0=ALU.mult, op1=ALU.mult).then_inc(mix_off_ready, 1)

            for b in range(B):
                weigh(b)
                if b:
                    mix_offset(b - 1)
                mix(b)
                mix_statistics(b)
            mix_offset(B - 1)


_INS = ['L0_attn_u', 'L0_attn_Win', 'L0_attn_b_in', 'L0_attn_Wg', 'L0_attn_bg', 'L0_attn_Wout', 'L0_attn_bout',
        'L0_attn_convw', 'L0_attn_convb', 'L0_attn_A', 'L0_attn_Wb', 'L0_attn_bb', 'L0_attn_Wc', 'L0_attn_bc',
        'L0_attn_Wdt', 'L0_attn_bdt', 'L0_ffn_Wg', 'L0_ffn_W1', 'L0_ffn_W2', 'L0_ffn_W3']


def kernel(**inputs):
    import numpy as _np
    import concourse.bacc as _bacc
    from concourse import mybir as _mybir
    from concourse.bass_utils import run_bass_kernel_spmd as _run

    nc = _bacc.Bacc("TRN2", target_bir_lowering=False, num_devices=1)
    arrays, args = {}, []
    for name in _INS:
        a = _np.ascontiguousarray(inputs[name])
        arrays[f"in_{name}_dram"] = a
        args.append(nc.dram_tensor(f"in_{name}_dram", a.shape, _mybir.dt.from_np(a.dtype), kind="ExternalInput").ap())
    args.append(nc.dram_tensor("out_0_dram", (8, 1024, 128), _mybir.dt.float32, kind="ExternalOutput").ap())
    build(nc, *args)
    r = _run(nc, [arrays], core_ids=[0])
    return r.results[0]["out_0_dram"]
```

```python
from contextlib import ExitStack

import concourse.bass as bass
from concourse import mybir

F32 = mybir.dt.float32
F32R = mybir.dt.float32r
ALU = mybir.AluOpType
ACT = mybir.ActivationFunctionType
AX = mybir.AxisListType

P = 128
EXP_LN = "natural_log_exp_and_others"
HALF = 512
I32 = mybir.dt.int32
U32 = mybir.dt.uint32
LAG = 4
RING = 4
TWO = 32
PAIR = 2


def wait(eng, sem, value):
    if not isinstance(value, int) or value > 0:
        eng.wait_ge(sem, value)


def build(nc, u, Win, b_in, Wg, bg, Wout, bout, convw, convb, A, Wb, bb, Wc, bc, Wdt, bdt,
          Wgate, W1, W2, W3, out):
    B, T, D = u.shape
    N = A.shape[1]
    NT = T // P
    E, H, _ = W1.shape
    HC = -(-H // P)
    HP = HC * P
    assert E == NT and E * H % 2 == 0

    group_of = [0] * (B - 3) + [1] * 3
    G = group_of[-1] + 1
    tokens = [group_of.count(g) * T for g in range(G)]
    region = [t + P for t in tokens]
    first_tile = [E * sum(region[0:g]) // P for g in range(G)]
    tiles = E * sum(region) // P
    slots = [-(-((2 * t + E * (P - 1)) // P) // RING) * RING for t in tokens]
    first_slot = [sum(slots[0:g]) for g in range(G)]
    S = sum(slots)
    scatters = [[16 * 2 * NT * sum(group_of[b] == g for b in range(i, B, 2)) for i in range(2)] for g in range(G)]
    assert D == P and T == 2 * HALF and N == 16

    with ExitStack() as ctx:
        def sb(name, shape, dt=F32):
            return ctx.enter_context(nc.sbuf_tensor(name, shape, dt))

        def ps(name, shape, dt=F32):
            return ctx.enter_context(nc.psum_tensor(name, shape, dt))

        def sem(name):
            return ctx.enter_context(nc.semaphore(name))

        ident = sb("ident", [P, P])
        eps_c = sb("eps_c", [P, 1])
        zeros = sb("zeros", [P, P])
        RB = -(-E * H // P)
        raw = sb("raw", [P, 2 * RB + E * HC, D])
        raw1 = raw[:, 0:RB, :]
        raw2 = raw[:, RB:2 * RB, :]
        raw3 = raw[:, 2 * RB:, :].rearrange("p (e c) h -> p e (c h)", e=E)
        x1_row = [sb(f"x1_row{i}", [P, NT, D]) for i in range(2)]
        place = [sb(f"place{i}", [P, 2, NT], U32) for i in range(2)]
        places = sb("places", [P, 2, B * NT])
        gap = sb("gap", [P, B * NT])
        gate1 = sb("gate1", [P, B * NT])
        gate2 = sb("gate2", [P, B * NT])
        base_from = [sb(f"base_from{g}", [P, E]) for g in range(G)]
        base = [sb(f"base{g}", [P, E]) for g in range(G)]
        pad_place = [sb(f"pad_place{g}", [P, E], U32) for g in range(G)]
        slot_expert = sb("slot_expert", [1, S], I32)
        slot_from = sb("slot_from", [1, S], I32)
        skip = [sb(f"skip{g}", [P, E]) for g in range(G)]
        stats = sb("stats", [P, NT, 6])
        mean = sb("mean", [P, NT])
        dif = sb("dif", [P, NT])
        sq = sb("sq", [P, NT])
        var = sb("var", [P, NT])
        lnv = sb("lnv", [P, NT])
        rstd = sb("rstd", [P, NT])

        own = ctx.enter_context(ExitStack())

        def sb(name, shape, dt=F32):
            return own.enter_context(nc.sbuf_tensor(name, shape, dt))

        win = sb("win", [P, D])
        wg = sb("wg", [P, D])
        wdt = sb("wdt", [P, D])
        wbc = sb("wbc", [P, 4 * N])
        a_dn = sb("a_dn", [P, N])
        b_in_c = sb("b_in_c", [P, 1])
        bg_c = sb("bg_c", [P, 1])
        bdt_c = sb("bdt_c", [P, 1])
        cw = sb("cw", [P, 3])
        cb = sb("cb", [P, 1])
        bbc_c = sb("bbc_c", [4 * N, 1])
        pick = sb("pick", [4 * N, 2 * N, P], F32R)
        u_in = sb("u_in", [P, NT, D])
        u_t = sb("u_t", [P, T])
        x_pad = sb("x_pad", [P, T + 2])
        xs = sb("xs", [P, T])
        dt_abs = sb("dt_abs", [P, T])
        dt_relu = sb("dt_relu", [P, T])
        dt = [sb(f"dt{i}", [P, T]) for i in range(2)]
        dtx = [sb(f"dtx{i}", [P, T]) for i in range(2)]
        bc_val = sb("bc_val", [4 * N, T])
        bc_split = [sb(f"bc_split{i}", [4 * N, T], F32R) for i in range(2)]
        decay = sb("decay", [P, RING, T])

        z = [sb(f"z{i}", [P, T]) for i in range(2)]
        state = sb("state", [P, RING, T])
        c_all = sb("c_all", [P, PAIR, T])
        prod = sb("prod", [P, RING, T])
        yz = sb("yz", [P, T])
        res = sb("res", [P, NT, D])
        u_res = sb("u_res", [P, NT, D])
        wout = sb("wout", [P, D])
        bout_r = sb("bout_r", [2 * TWO, HALF], F32R)
        ones_r = sb("ones_r", [2 * TWO, P], F32R)
        x1_t = yz
        bout_v = state[0:2 * TWO, RING - 1, 0:HALF]
        wgate_t = sb("wgate_t", [P, E])
        wgate = sb("wgate", [E, D])
        before = sb("before", [P, P])
        ones = sb("ones", [P, P])
        first_high = sb("first_high", [P, E, NT])
        logit = sb("logit", [P, E, NT])
        logit2 = sb("logit2", [P, E, NT])
        top1 = sb("top1", [P, E, NT])
        top2 = sb("top2", [P, E, NT])
        chosen = sb("chosen", [P, E, NT])
        rank = sb("rank", [P, E, NT])
        part = sb("part", [P, E, NT])
        best = sb("best", [P, NT])
        place_f = sb("place_f", [P, 2, NT])
        best2 = sb("best2", [P, NT])
        index = sb("index", [P, NT])
        running = sb("running", [P, E * NT + 1])
        count = sb("count", [P, E])
        offset = sb("offset", [P, E])
        lane = sb("lane", [P, 1])
        SM = max(slots)
        slot_no = sb("slot_no", [1, SM])
        n_tiles = sb("n_tiles", [P, E])
        n_tiles_i = sb("n_tiles_i", [P, E], I32)
        done_at = sb("done_at", [P, E])
        passed = sb("passed", [1, SM, E])
        t_expert = sb("t_expert", [1, SM])
        t_tile = sb("t_tile", [1, SM])
        t_used = sb("t_used", [1, SM])
        ones_e = sb("ones_e", [P, E])
        own.close()

        def sb(name, shape, dt=F32):
            return ctx.enter_context(nc.sbuf_tensor(name, shape, dt))

        EH = E * H + 2
        w1 = [sb(f"w1_{i}", [P, EH], F32R) for i in ("hi", "lo")]
        w2 = [sb(f"w2_{i}", [P, EH], F32R) for i in ("hi", "lo")]
        w3 = sb("w3", [P, E * HC, 2, P], F32R)
        x_slot = sb("x_slot", [P, RING, D])
        x_hi = sb("x_hi", [P, 2, P], F32R)
        x_lo = sb("x_lo", [P, 2, P], F32R)
        act1 = sb("act1", [P, 2, H])
        hid = sb("hid", [P, 2, HP])
        hid_hi = sb("hid_hi", [P, 2, HP], F32R)
        hid_lo = sb("hid_lo", [P, 2, HP], F32R)
        y_slot = sb("y_slot", [P, RING, D])
        x1 = sb("x1", [P, B * NT, D])
        y_got = [sb("y_got", [P, B * NT, D]), raw[:, 0:B * NT, :]]
        y_place = sb("y_place", [P, 2, B * NT], U32)
        mix_mean, mix_var, mix_lnv, mix_rs, mix_off = (
            sb(name, [P, 2, NT]) for name in ("mix_mean", "mix_var", "mix_lnv", "mix_rs", "mix_off"))

        x1_rows = nc.dram_tensor("x1_rows", (B * T, D), F32, kind="Internal").ap()
        x_sorted = nc.dram_tensor("x_sorted", (tiles * P, D), F32, kind="Internal").ap()
        y_sorted = nc.dram_tensor("y_sorted", (S * P, D), F32, kind="Internal").ap()

        ps_b = ps("ps_b", [P, T])
        ps_c = ps("ps_c", [P, T])
        ps_y = ps("ps_y", [P, T])
        ps_s = ps("ps_s", [P, T])

        first_loaded, w_loaded = sem("first_loaded"), sem("w_loaded")
        const_ready = sem("const_ready")
        pick_ready, bout_hi = sem("pick_ready"), sem("bout_hi")
        u_loaded, ures_loaded = sem("u_loaded"), sem("ures_loaded")
        raw_loaded = sem("raw_loaded")
        x1_saved = [sem("x1_saved0"), sem("x1_saved1")]
        x1t_in, x1t_ready = sem("x1t_in"), sem("x1t_ready")
        logit_in, logit_ready = sem("logit_in"), sem("logit_ready")
        count_ready, rank_in, rank_drained = sem("count_ready"), sem("rank_in"), sem("rank_drained")
        place_ready, route_step = sem("place_ready"), sem("route_step")
        scattered = [[sem(f"scattered{g}{i}") for i in range(2)] for g in range(G)]
        padded = [sem(f"padded{g}") for g in range(G)]
        table_step, table_ready = sem("table_step"), sem("table_ready")
        wgate_in, wgate_ready = sem("wgate_in"), sem("wgate_ready")
        prep_in, prep_hi, prep_lo = sem("prep_in"), sem("prep_hi"), sem("prep_lo")
        result_step, y_place_ready = sem("result_step"), sem("y_place_ready")
        gate_step = sem("gate_step")
        xs_loaded = [sem(f"xs_loaded{i}") for i in range(RING)]
        xt_in, xhi_ready, xlo_ready = sem("xt_in"), sem("xhi_ready"), sem("xlo_ready")
        h1_in, h2_in, silu_ready, hid_ready = sem("h1_in"), sem("h2_in"), sem("silu_ready"), sem("hid_ready")
        ht_in, hthi_ready, htlo_ready = sem("ht_in"), sem("hthi_ready"), sem("htlo_ready")
        yo_in, ys_ready = sem("yo_in"), sem("ys_ready")
        y_saved = [sem(f"y_saved{i}") for i in range(RING)]
        x1_loaded = sem("x1_loaded")
        y_gathered = [sem(f"y_gathered{i}") for i in range(B)]
        mix_scaled, mix_off_ready = sem("mix_scaled"), sem("mix_off_ready")
        mix_step, mix_ln, mix_rstd, mix_ready = sem("mix_step"), sem("mix_ln"), sem("mix_rstd"), sem("mix_ready")
        ut_in, ut_ready = sem("ut_in"), sem("ut_ready")
        x_in, xpad_ready = sem("x_in"), sem("xpad_ready")
        conv_part, conv_ready, xs_ready = sem("conv_part"), sem("conv_ready"), sem("xs_ready")
        z_in, z_ready = sem("z_in"), sem("z_ready")
        dt_in, dtabs_ready, dtrelu_ready = sem("dt_in"), sem("dtabs_ready"), sem("dtrelu_ready")
        dtexp_ready, dtln_ready, dt_ready, dtx_ready = sem("dtexp_ready"), sem("dtln_ready"), sem("dt_ready"), sem("dtx_ready")
        bc_in, bcval_ready, bchi_ready, bclo_ready = sem("bc_in"), sem("bcval_ready"), sem("bchi_ready"), sem("bclo_ready")
        bB_ready, bC_ready = sem("bB_ready"), sem("bC_ready")
        decay_ready, drive_ready, state_ready = sem("decay_ready"), sem("drive_ready"), sem("state_ready")
        c_ready, prod_ready, y_added = sem("c_ready"), sem("prod_ready"), sem("y_added")
        yz_ready, out_in, res_ready = sem("yz_ready"), sem("out_in"), sem("res_ready")
        stats_ready, agg_part, lnv_ready, rstd_ready, x1_ready = sem("stats_ready"), sem("agg_part"), sem("lnv_ready"), sem("rstd_ready"), sem("x1_ready")
        out_stored = sem("out_stored")

        u_v = u.rearrange("b (n p) d -> b p n d", p=P)
        out_v = out.rearrange("b (n p) d -> b p n d", p=P)
        x1_v = x1_rows.rearrange("(b n p) d -> b p n d", p=P, n=NT)
        col = lambda v: v.rearrange("(p o) -> p o", o=1)
        row = lambda v: v.rearrange("(o p) -> o p", o=1)
        first_loads = [(win[:], Win), (b_in_c[:], col(b_in)), (wg[:], Wg), (bg_c[:], col(bg)), (cw[:], convw), (cb[:], col(convb))]
        act_loads = ([(wdt[:], Wdt), (bdt_c[:], col(bdt))]
                     + [(wbc[:, k * N:(k + 1) * N], (Wb, Wc)[k % 2]) for k in range(4)]
                     + [(bbc_c[k * N:(k + 1) * N, :], col((bb, bc)[k % 2])) for k in range(4)])
        sp_loads = ([(a_dn[:], A), (wout[:], Wout), (wgate[:], Wgate)]
                    + [(bout_v[q:q + 1, :].rearrange("o (k d) -> o k d", d=D), row(bout).unsqueeze(1).broadcast_to([1, HALF // D, D]))
                       for q in (0, TWO)])
        IDENT = 2
        CLEARED = 6
        PICKED = CLEARED + 3
        CONSTANTS = PICKED + 9 + 2 * G
        ROUTE = 21
        TABLE = 16
        MIX = 6
        FIRST = 16 * len(first_loads)
        WEIGHTS = 16 * (len(act_loads) + len(sp_loads))

        block = ctx.enter_context(nc.Block())

        HALVES = [slice(h * HALF, (h + 1) * HALF) for h in range(2)]

        def rows(eng, body):
            body(0, 0, first=True, last=False)
            body(1, 1, first=False, last=False)
            with eng.Fori(0, 2) as pair:
                body(pair * 2 + 2, 0, first=False, last=False)
                body(pair * 2 + 3, 1, first=False, last=False)
            body(6, 0, first=False, last=False)
            body(7, 1, first=False, last=True)

        ROUNDS = 2
        assert (S // RING - 2) % ROUNDS == 0

        def all_slots(eng, slot, begin=lambda first, count: None):
            begin(0, RING + 1)
            for s in range(RING + 1):
                slot(s, s % RING, s // RING, s, first=s == 0, last=False)
            with eng.Fori(0, (S // RING - 2) // ROUNDS) as i:
                begin(i * (ROUNDS * RING) + (RING - 1), ROUNDS * RING + 2)
                for k in range(1, ROUNDS * RING + 1):
                    slot(i * (ROUNDS * RING) + (RING + k), k % RING, i * ROUNDS + (1 + k // RING), k + 1, first=False, last=False)
            begin(S - RING - 1, RING + 1)
            for s in range(S - RING + 1, S):
                slot(s, s % RING, s // RING, s - (S - RING - 1), first=False, last=s == S - 1)

        preps = ([(1, c, min(HALF, E * H - c), w1) for c in range(0, E * H, HALF)]
                 + [(2, c, min(HALF, E * H - c), w2) for c in range(0, E * H, HALF)]
                 + [(3, c, HALF, None) for c in range(0, E * HP, HALF)])

        def prep_part(i, part):
            kind, cols, width, dst = preps[i]
            if kind == 3:
                return w3[:, cols // P:(cols + width) // P, part, :]
            return dst[part][:, cols:cols + width]

        def prep_shape(i, t):
            return t.rearrange("p (k m) -> p k m", m=P) if preps[i][0] == 3 else t

        def prep_bank(i):
            return (ps_b, ps_c)[i % 4 // 2][:, HALVES[i % 2]]

        stages = [range(0, 6), range(6, 8), range(8, 10), range(10, 14), range(14, len(preps))]

        HE = H + H % 2
        ps_h1 = ps_b[:, 0:HE]
        ps_h2 = ps_b[:, HALF:HALF + HE]
        ps_ht = [ps_c[:, i * HALF:i * HALF + HP] for i in range(2)]
        ps_xt = ps_s[:, 0:P]
        ps_yo = ps_s[:, HALF:HALF + 2 * D]

        def group(b):
            return group_of[b] if isinstance(b, int) else 0

        @block.sync
        def _(sp):
            sp.dma_start(u_in[:], u_v[0]).then_inc(u_loaded, 16)
            for dst, src in first_loads:
                sp.dma_start(dst, src).then_inc(first_loaded, 16)
            sp.wait_ge(const_ready, CLEARED)
            for dst, src in sp_loads:
                sp.dma_start(dst, src).then_inc(w_loaded, 16)

            def body(b, par, first, last):
                if not last:
                    wait(sp, ut_in, b + 1)
                    sp.dma_start(u_in[:], u_v[b + 1]).then_inc(u_loaded, 16)
                wait(sp, res_ready, b)
                sp.dma_start(u_res[:], u_v[b]).then_inc(ures_loaded, 16)
                if first:
                    for raw, w in ((raw1, W1), (raw2, W2)):
                        flat = w.rearrange("e h d -> (e h) d")
                        full = E * H // P
                        sp.dma_start(raw[:, 0:full, :], flat[0:full * P].rearrange("(k p) d -> p k d", p=P)).then_inc(raw_loaded, 16)
                        sp.dma_start(raw[0:E * H - full * P, full, :], flat[full * P:]).then_inc(raw_loaded, 16)
                    sp.dma_start(raw3[:, :, 0:H], W3.rearrange("e d h -> d e h")).then_inc(raw_loaded, 16)
                else:
                    if not isinstance(b, int) or b >= 2:
                        wait(sp, x1_saved[par], (b - par) * 8)
                    wait(sp, x1_ready, b)
                    sp.dma_start(x1_v[b - 1], x1_row[1 - par][:]).then_inc(x1_saved[1 - par], 16)

            rows(sp, body)
            sp.wait_ge(x1_ready, B)
            sp.dma_start(x1_v[B - 1], x1_row[1][:]).then_inc(x1_saved[1], 16)

            def load_slot(s, r):
                if not isinstance(s, int) or s >= RING:
                    wait(sp, xt_in, s - RING + 1)
                tile = sp.value_load(slot_from[0:1, bass.ds(s, 1)], min_val=0, max_val=tiles - 1)
                sp.dma_start(x_slot[:, r, :], x_sorted[bass.ds(tile * P, P)]).then_inc(xs_loaded[r], 16)

            def group_sorted(g):
                sp.wait_ge(table_ready, g + 1)
                sp.wait_ge(padded[g], 16 * E)
                for i in range(2):
                    if scatters[g][i]:
                        sp.wait_ge(scattered[g][i], scatters[g][i])

            group_sorted(0)
            sp.wait_ge(prep_lo, 1)
            for r in range(RING):
                load_slot(r, r)
            with sp.Fori(1, slots[0] // RING) as i:
                for r in range(RING):
                    load_slot(i * RING + r, r)
            for g in range(1, G):
                group_sorted(g)
                if g == G - 1:
                    for i in range(2):
                        sp.wait_ge(x1_saved[i], 16 * B // 2)
                    sp.dma_start(x1[:], x1_rows.rearrange("(n p) d -> p n d", p=P)).then_inc(x1_loaded, 16)
                with sp.Fori(first_slot[g] // RING, (first_slot[g] + slots[g]) // RING) as i:
                    for r in range(RING):
                        load_slot(i * RING + r, r)
            for b in range(B):
                sp.wait_ge(mix_ready, b + 1 if b < B - 1 else B + 1)
                sp.dma_start(out_v[b], x1[:, b * NT:(b + 1) * NT, :]).then_inc(out_stored, 16)
            sp.wait_ge(out_stored, 16 * B)

        @block.gpsimd
        def _(pool):
            stage = prod[0:4 * N, :, :].rearrange("q a (r m) -> q (a r) m", m=P)
            nc.gpsimd.memset(ident[:], 0.0).then_inc(const_ready, 1)
            pool.wait_ge(const_ready, 1)
            nc.gpsimd.affine_select(out=ident[:], in_=ident[:], compare_op=ALU.not_equal, fill=1.0, base=0,
                                    pattern=[[-1, P]], channel_multiplier=1).then_inc(const_ready, 1)
            nc.gpsimd.memset(x_pad[:], 0.0).then_inc(const_ready, 1)
            nc.gpsimd.memset(bout_v, 0.0).then_inc(const_ready, 1)
            nc.gpsimd.memset(ones[:], 1.0).then_inc(const_ready, 1)
            nc.gpsimd.memset(eps_c[:], 1e-5).then_inc(const_ready, 1)
            pool.wait_ge(const_ready, CLEARED)
            nc.gpsimd.memset(stage, 0.0).then_inc(const_ready, 1)
            for part in range(2):
                pool.wait_ge(const_ready, CLEARED + 1 + part)
                nc.gpsimd.affine_select(out=stage, in_=stage, compare_op=ALU.not_equal, fill=1.0,
                                        base=-2 * N * part, pattern=[[-1, 2 * N], [0, P]],
                                        channel_multiplier=1).then_inc(const_ready, 1)
            nc.gpsimd.memset(before[:], 1.0).then_inc(const_ready, 1)
            pool.wait_ge(const_ready, CLEARED + 4)
            nc.gpsimd.affine_select(out=before[:], in_=before[:], compare_op=ALU.is_gt, fill=0.0, base=0,
                                    pattern=[[1, P]], channel_multiplier=-1).then_inc(const_ready, 1)
            nc.gpsimd.memset(zeros[:], 0.0).then_inc(const_ready, 1)
            nc.gpsimd.memset(running[:, 0:1], 0.0).then_inc(const_ready, 1)
            nc.gpsimd.memset(ones_e[:], 1.0).then_inc(const_ready, 1)
            nc.gpsimd.memset(raw3[:, :, H:HP], 0.0).then_inc(const_ready, 1)
            exact = dict(allow_small_or_imprecise_dtypes=True)
            nc.gpsimd.iota(first_high[:], pattern=[[-1, E], [0, NT]], base=E, channel_multiplier=0, **exact).then_inc(const_ready, 1)
            nc.gpsimd.iota(lane[:], pattern=[[0, 1]], base=0, channel_multiplier=1, **exact).then_inc(const_ready, 1)
            nc.gpsimd.iota(slot_no[:], pattern=[[1, SM]], base=0, channel_multiplier=0, **exact).then_inc(const_ready, 1)
            for g in range(G):
                for t in (base_from[g], base[g]):
                    nc.gpsimd.iota(t[:], pattern=[[region[g], E]], base=first_tile[g] * P, channel_multiplier=0,
                                   **exact).then_inc(const_ready, 1)

            def scatter(b, par, j, choices=(0, 1)):
                for k in choices:
                    nc.gpsimd.indirect_dma_start(x_sorted[:, :], bass.IndirectOffsetOnAxis(place[par][:, k, j:j + 1], 0),
                                                 x1_row[par][:, j, :], None).then_inc(scattered[group(b)][par], 16)

            def pad(g, e):
                if e == 0:
                    pool.wait_ge(table_ready, g + 1)
                nc.gpsimd.indirect_dma_start(x_sorted[:, :], bass.IndirectOffsetOnAxis(pad_place[g][:, e:e + 1], 0),
                                             zeros[:], None).then_inc(padded[g], 16)

            def body(b, par, first, last):
                past = not isinstance(b, int) or b >= 2
                for n in range(N):
                    g = b * N + n
                    if past and n == 0:
                        wait(pool, place_ready, b - 1)
                    if n == 2 and (not isinstance(b, int) or b >= 3):
                        wait(pool, scattered[0][1 - par], (b - 1 - (1 - par)) * (8 * 2 * NT))
                    wait(pool, state_ready, g + 1)
                    wait(pool, c_ready, b * (2 * N) + (2 * n + 2))
                    if first and n == 0:
                        pool.wait_ge(pick_ready, 1)
                    if not first or n >= RING:
                        wait(pool, y_added, g - RING + 1)
                    nc.gpsimd.tensor_tensor(prod[:, n % RING, :], state[:, n % RING, :], c_all[:, n % PAIR, :],
                                            ALU.mult).then_inc(prod_ready, 1)
                    if past:
                        scatter(b - 2, par, n // 2, (n % 2,))

            rows(pool, body)
            for e in range(E):
                pad(0, e)
            for b in (B - 2, B - 1):
                pool.wait_ge(place_ready, b + 1)
                for j in range(NT):
                    scatter(b, b % 2, j)
            for e in range(E):
                pad(G - 1, e)

            def find_results():
                step = [0]

                def link(ins):
                    step[0] += 1
                    ins.then_inc(result_step, 1)
                    pool.wait_ge(result_step, step[0])

                pool.wait_ge(table_ready, G)
                for g in range(G):
                    first, n = group_of.index(g) * NT, tokens[g] // P
                    mine = places[:, :, first:first + n]
                    last, unused, total = (y_got[0][:, t:t + 2, 0:n] for t in (0, 2, 4))
                    link(nc.gpsimd.memset(total, 0.0))
                    link(nc.gpsimd.tensor_scalar(last, mine, -float(region[g]), None, ALU.add))
                    for e in range(E - 1):
                        link(nc.gpsimd.tensor_scalar(unused, last, base_from[g][:, e:e + 1], skip[g][:, e:e + 1], ALU.is_ge, ALU.mult))
                        link(nc.gpsimd.tensor_tensor(total, total, unused, ALU.add))
                    link(nc.gpsimd.tensor_scalar(total, total, -float(P), None, ALU.mult))
                    link(nc.gpsimd.tensor_tensor(total, total, mine, ALU.add))
                    nc.gpsimd.tensor_scalar(y_place[:, :, first:first + n], total,
                                            float((first_slot[g] - first_tile[g]) * P), None, ALU.add).then_inc(y_place_ready, 1)
                    pool.wait_ge(y_place_ready, g + 1)

            find_results()

            for b in range(B):
                g = group_of[b]
                if b == 0:
                    pool.wait_ge(y_place_ready, G)
                if g < G - 1 and b == group_of.index(g):
                    pool.wait_ge(ys_ready, first_slot[g] + slots[g] + RING)
                if b == group_of.index(G - 1):
                    for r in range(RING):
                        pool.wait_ge(y_saved[r], 16 * S // RING)
                done = y_sorted[0:(first_slot[g] + slots[g]) * P, :]
                for j in range(b * NT, (b + 1) * NT):
                    for k in range(2):
                        nc.gpsimd.indirect_dma_start(y_got[k][:, j, :], None, done,
                                                     bass.IndirectOffsetOnAxis(y_place[:, k, j:j + 1], 0)).then_inc(y_gathered[b], 16)

        @block.tensor
        def _(pe):
            def transpose_u(b):
                wait(pe, u_loaded, (b + 1) * 16)
                for j in range(NT):
                    ins = nc.tensor.transpose(ps_s[:, j * P:(j + 1) * P], u_in[:, j, :], ident[:])
                ins.then_inc(ut_in, 1)

            def project(dst, lhs, rhs, done, part):
                for h in (0, 1) if part is None else (part,):
                    ins = nc.tensor.matmul(dst[:, HALVES[h]], lhs, rhs[:, HALVES[h]], start=True, stop=True)
                if part != 0:
                    ins.then_inc(done, 1)

            def project_x(b, part=None):
                wait(pe, ut_ready, b + 1)
                project(ps_s, win[:], u_t, x_in, part)

            def project_z(b, part=None):
                wait(pe, xpad_ready, b + 1)
                project(ps_s, wg[:], u_t, z_in, part)

            def project_dt(b, part=None):
                wait(pe, xs_ready, b + 1)
                wait(pe, z_ready, b + 1)
                project(ps_s, wdt[:], xs, dt_in, part)

            def project_bc(b, part=None):
                wait(pe, dtabs_ready, b + 1)
                wait(pe, dtrelu_ready, b + 1)
                project(ps_s[0:4 * N], wbc[:], xs, bc_in, part)

            def project_out(b, part=None):
                wait(pe, yz_ready, (b + 1) * 2)
                for h in (0, 1) if part is None else (part,):
                    nc.tensor.matmul(ps_s[:, HALVES[h]], ones_r[:], bout_r[:], start=True, stop=True)
                    for j in range(h * NT // 2, (h + 1) * NT // 2):
                        ins = nc.tensor.matmul(ps_s[:, j * P:(j + 1) * P], yz[:, j * P:(j + 1) * P], wout[:],
                                               start=False, stop=True, skip_group_check=True)
                if part != 0:
                    ins.then_inc(out_in, 1)

            def add_state(b, n):
                wait(pe, prod_ready, b * N + n + 1)
                for h, s in enumerate(HALVES):
                    if n == 0 and (not isinstance(b, int) or b):
                        wait(pe, yz_ready, (b - 1) * 2 + (h + 1))
                    ins = nc.tensor.matmul(ps_y[:, s], ident[:], prod[:, n % RING, s], start=n == 0, stop=n == N - 1)
                ins.then_inc(y_added, 1)

            def broadcast_b(b, par, n):
                if n == 0:
                    wait(pe, bchi_ready, b + 1)
                    wait(pe, bclo_ready, b + 1)
                for h, s in enumerate(HALVES):
                    if not isinstance(b, int) or b * N + n >= 1:
                        wait(pe, drive_ready, b * (2 * N) + (2 * n + h - 1))
                    nc.tensor.matmul(ps_b[:, s], pick[:, n, :], bc_split[par][:, s], start=True, stop=True).then_inc(bB_ready, 1)

            def broadcast_c(b, par, n):
                for h, s in enumerate(HALVES):
                    if not isinstance(b, int) or b * N + n >= 1:
                        wait(pe, c_ready, b * (2 * N) + (2 * n + h - 1))
                    nc.tensor.matmul(ps_c[:, s], pick[:, N + n, :], bc_split[par][:, s], start=True, stop=True).then_inc(bC_ready, 1)

            def transpose_x1(b, par):
                wait(pe, x1_ready, b + 1)
                for j in range(NT):
                    ins = nc.tensor.transpose(ps_s[:, j * P:(j + 1) * P], x1_row[par][:, j, :], ident[:])
                ins.then_inc(x1t_in, 1)

            def route_logits(b):
                wait(pe, x1t_ready, b + 1)
                for j in range(NT):
                    ins = nc.tensor.matmul(ps_s[:, j * E:(j + 1) * E], x1_t[:, j * P:(j + 1) * P], wgate_t[:],
                                           start=True, stop=True)
                ins.then_inc(logit_in, 1)

            def rank_tokens(b):
                wait(pe, count_ready, b + 1)
                nc.tensor.matmul(ps_s[:, 0:E], before[:], count[:], start=True, stop=True)
                nc.tensor.matmul(ps_s[:, E:2 * E], ones[:], count[:], start=True, stop=True).then_inc(rank_in, 1)

            pe.wait_ge(const_ready, IDENT)
            transpose_u(0)
            pe.wait_ge(first_loaded, FIRST)
            project_x(0)
            project_z(0)
            pe.wait_ge(w_loaded, WEIGHTS)
            nc.tensor.transpose(ps_y[:, 0:E], wgate[:], ident[0:E, 0:E]).then_inc(wgate_in, 1)
            project_dt(0)
            project_bc(0)
            pe.wait_ge(pick_ready, 1)

            def body(b, par, first, last):
                for n in range(N):
                    broadcast_b(b, par, n)
                    if n == LAG:
                        broadcast_c(b, par, n)
                    if n >= LAG:
                        add_state(b, n - LAG)
                    elif not first:
                        add_state(b - 1, n - LAG + N)
                    if n != LAG:
                        broadcast_c(b, par, n)
                    if not last:
                        if n == 0:
                            if first:
                                wait(pe, bcval_ready, 1)
                            elif isinstance(b, int) and b == 1:
                                wait(pe, bcval_ready, 2)
                            else:
                                wait(pe, rank_drained, b - 1)
                            transpose_u(b + 1)
                        if n in (1, 2):
                            project_x(b + 1, n - 1)
                        if n == 3:
                            project_z(b + 1)
                        if n == 7:
                            if not first:
                                wait(pe, res_ready, b)
                            project_dt(b + 1)
                        if n == 9:
                            project_bc(b + 1)
                    if not first:
                        if n == 5:
                            if last:
                                wait(pe, rank_drained, b - 1)
                            else:
                                wait(pe, z_ready, b + 2)
                            project_out(b - 1)
                        if n == 10:
                            if last:
                                wait(pe, res_ready, b)
                            else:
                                wait(pe, bcval_ready, b + 2)
                            transpose_x1(b - 1, 1 - par)
                        if n == 11:
                            route_logits(b - 1)
                        if n == 14:
                            wait(pe, logit_ready, b)
                            rank_tokens(b - 1)

            rows(pe, body)

            def turn_weights(pieces):
                for i in pieces:
                    if i >= 4:
                        pe.wait_ge(prep_lo, i - 3)
                    kind, cols, width, _ = preps[i]
                    for c in range(0, width, P):
                        if kind == 3:
                            src, n = raw3.rearrange("d e h -> d (e h)")[:, cols + c:cols + c + P], P
                        else:
                            n = min(P, width - c)
                            src = (raw1, raw2)[kind - 1][0:n, (cols + c) // P, :]
                        ins = nc.tensor.transpose(prep_bank(i)[:, c:c + n], src, ident[0:src.shape[0], 0:src.shape[0]])
                    ins.then_inc(prep_in, 1)

            pe.wait_ge(drive_ready, 2 * B * N)
            pe.wait_ge(raw_loaded, 16 * 5)
            add_state(B - 1, N - 4)
            turn_weights(range(0, 2))
            add_state(B - 1, N - 3)
            pe.wait_ge(c_ready, 2 * B * N)
            turn_weights(range(2, 4))
            add_state(B - 1, N - 2)
            turn_weights(range(4, 6))
            add_state(B - 1, N - 1)
            turn_weights(stages[1])
            pe.wait_ge(rank_drained, B - 1)
            project_out(B - 1)
            turn_weights(stages[2])
            turn_weights(stages[3])
            pe.wait_ge(res_ready, B)
            transpose_x1(B - 1, 1)
            turn_weights(stages[4])
            route_logits(B - 1)
            pe.wait_ge(logit_ready, B)
            rank_tokens(B - 1)

            expert = []

            def load_experts(first, count):
                if not isinstance(first, int):
                    pe.wait_ge(table_ready, G)
                expert[:] = nc.values_load_multi_w_load_instructions(
                    slot_expert[0:1, bass.ds(first, count)], [mybir.EngineType.PE], min_val=0, max_val=E - 1,
                    skip_runtime_bounds_check_because="tables() takes an expert below E or the first")[1]

            def three(dst, a_hi, a_lo, b_hi, b_lo, start=True, stop=True):
                nc.tensor.matmul(dst, a_hi, b_hi, start=start, stop=False)
                nc.tensor.matmul(dst, a_hi, b_lo, start=False, stop=False)
                return nc.tensor.matmul(dst, a_lo, b_hi, start=False, stop=stop)

            def turn_x(s, r, turn):
                wait(pe, xs_loaded[r], (turn + 1) * 16)
                nc.tensor.transpose(ps_xt, x_slot[:, r, :], ident[:]).then_inc(xt_in, 1)

            def hidden_one(s, p, e):
                wait(pe, xlo_ready, s + 1)
                wait(pe, silu_ready, s)
                cut = bass.ds(e * H, H + H % 2)
                three(ps_h1, x_hi[:, p, :], x_lo[:, p, :], w1[0][:, cut], w1[1][:, cut]).then_inc(h1_in, 1)

            def hidden_two(s, p, e):
                cut = bass.ds(e * H, H + H % 2)
                three(ps_h2, x_hi[:, p, :], x_lo[:, p, :], w2[0][:, cut], w2[1][:, cut]).then_inc(h2_in, 1)

            def turn_hidden(s, p):
                wait(pe, hid_ready, s + 1)
                for c in range(HC):
                    ins = nc.tensor.transpose(ps_ht[p][:, c * P:(c + 1) * P], hid[:, p, c * P:(c + 1) * P], ident[:])
                ins.then_inc(ht_in, 1)

            def out_rows(s, p, e):
                wait(pe, htlo_ready, s + 1)
                wait(pe, ys_ready, s)
                chunk = lambda c, both: w3.rearrange("p k i m -> p (k i m)")[:, bass.ds(e * (2 * HP) + 2 * P * c, P * (1 + both))]
                for c in range(HC):
                    nc.tensor.matmul(ps_yo, hid_hi[:, p, c * P:(c + 1) * P], chunk(c, True), start=c == 0, stop=c == HC - 1)
                for c in range(HC):
                    ins = nc.tensor.matmul(ps_yo[:, 0:D], hid_lo[:, p, c * P:(c + 1) * P], chunk(c, False), start=False,
                                           stop=c == HC - 1, skip_group_check=True)
                ins.then_inc(yo_in, 1)

            pe.wait_ge(prep_lo, len(preps))
            pe.wait_ge(rank_drained, B)
            turn_x(0, 0, 0)

            def slot(s, r, turn, at, first, last):
                hidden_one(s, r % 2, expert[at])
                if not first:
                    turn_hidden(s - 1, (r - 1) % 2)
                if not last:
                    turn_x(s + 1, (r + 1) % RING, turn + (r + 1) // RING)
                hidden_two(s, r % 2, expert[at])
                if not isinstance(s, int) or s >= 2:
                    out_rows(s - 2, r % 2, expert[at - 2])

            all_slots(pe, slot, load_experts)
            turn_hidden(S - 1, (S - 1) % 2)
            for s in (S - 2, S - 1):
                out_rows(s, s % 2, expert[s - (S - RING - 1)])

        @block.scalar
        def _(act):
            def evacuate_u(b):
                wait(act, ut_in, b + 1)
                wait(act, z_in, b)
                nc.scalar.copy(u_t[:], ps_s[:]).then_inc(ut_ready, 1)

            def evacuate_x(b):
                wait(act, x_in, b + 1)
                wait(act, conv_ready, b)
                nc.scalar.activation(x_pad[:, 1:T + 1], ps_s[:], ACT.Identity, bias=b_in_c[:]).then_inc(xpad_ready, 1)

            def silu_z(b, par):
                wait(act, z_in, b + 1)
                wait(act, yz_ready, (b - 1) * 2)
                nc.scalar.activation(z[par][:], ps_s[:], ACT.Silu, bias=bg_c[:]).then_inc(z_ready, 1)

            def silu_x(b):
                wait(act, conv_ready, b + 1)
                nc.scalar.activation(xs[:], xs[:], ACT.Silu).then_inc(xs_ready, 1)
                act.preload_act_table_set(EXP_LN)

            def abs_dt(b):
                wait(act, dt_in, b + 1)
                wait(act, dt_ready, b)
                nc.scalar.activation(dt_abs[:], ps_s[:], ACT.Abs, bias=bdt_c[:]).then_inc(dtabs_ready, 1)

            def relu_dt(b):
                wait(act, dt_ready, b)
                nc.scalar.activation(dt_relu[:], ps_s[:], ACT.Relu, bias=bdt_c[:]).then_inc(dtrelu_ready, 1)

            def exp_dt(b):
                wait(act, dtabs_ready, b + 1)
                nc.scalar.activation(dt_abs[:], dt_abs[:], ACT.Exp, scale=-1.0).then_inc(dtexp_ready, 1)

            def ln_dt(b):
                wait(act, dtexp_ready, b + 1)
                nc.scalar.activation(dt_abs[:], dt_abs[:], ACT.Ln, bias=1.0).then_inc(dtln_ready, 1)

            def evacuate_bc(b):
                wait(act, bc_in, b + 1)
                wait(act, bclo_ready, b)
                nc.scalar.activation(bc_val[:], ps_s[0:4 * N, :], ACT.Identity, bias=bbc_c[:]).then_inc(bcval_ready, 1)

            def round_bc(b, par):
                wait(act, bcval_ready, b + 1)
                wait(act, bC_ready, (b - 1) * (2 * N))
                nc.scalar.copy(bc_split[par][:], bc_val[:]).then_inc(bchi_ready, 1)

            def decay_of(b, par, n):
                g = b * N + n
                if n == 0:
                    wait(act, dt_ready, b + 1)
                if not isinstance(g, int) or g >= RING:
                    wait(act, state_ready, g - RING + 1)
                nc.scalar.activation(decay[:, n % RING, :], dt[par][:], ACT.Exp, scale=a_dn[:, n:n + 1]).then_inc(decay_ready, 1)

            def row_ln(b):
                wait(act, agg_part, 3 * b + 3)
                nc.scalar.activation(lnv[:], var[:], ACT.Ln, bias=eps_c[:], scale=1.0 / P).then_inc(lnv_ready, 1)

            def row_rstd(b):
                wait(act, lnv_ready, b + 1)
                nc.scalar.activation(rstd[:], lnv[:], ACT.Exp, scale=-0.5).then_inc(rstd_ready, 1)

            def evacuate_x1(b):
                wait(act, x1t_in, b + 1)
                wait(act, logit_in, b)
                nc.scalar.copy(x1_t[:], ps_s[:]).then_inc(x1t_ready, 1)

            act.preload_act_table_set(EXP_LN)
            for dst, src in act_loads:
                act.dma_start(dst, src).then_inc(w_loaded, 16)
            act.wait_ge(const_ready, CLEARED)
            evacuate_u(0)
            act.wait_ge(first_loaded, FIRST)
            evacuate_x(0)
            silu_z(0, 0)
            silu_x(0)
            act.wait_ge(w_loaded, WEIGHTS)
            act.wait_ge(wgate_in, 1)
            nc.scalar.copy(wgate_t[:], ps_y[:, 0:E]).then_inc(wgate_ready, 1)
            nc.scalar.copy(ones_r[:], ones[0:2 * TWO, :])
            nc.scalar.copy(bout_r[:], bout_v).then_inc(bout_hi, 1)
            abs_dt(0)
            relu_dt(0)
            evacuate_bc(0)
            round_bc(0, 0)
            exp_dt(0)
            ln_dt(0)
            decay_of(0, 0, 0)

            def body(b, par, first, last):
                for n in range(N):
                    g = b * N + n
                    if n < N - 1:
                        decay_of(b, par, n + 1)
                    elif not last:
                        decay_of(b + 1, 1 - par, 0)
                    if not first or n >= PAIR:
                        wait(act, prod_ready, g - PAIR + 1)
                    for h, s in enumerate(HALVES):
                        wait(act, bC_ready, b * (2 * N) + (2 * n + h + 1))
                        nc.scalar.copy(c_all[:, n % PAIR, s], ps_c[:, s]).then_inc(c_ready, 1)
                    if not first:
                        if n == 8:
                            row_ln(b - 1)
                            row_rstd(b - 1)
                        if n == 10:
                            evacuate_x1(b - 1)
                    if not last:
                        if n == 0:
                            evacuate_u(b + 1)
                        if n == 2:
                            evacuate_x(b + 1)
                        if n == 4:
                            silu_z(b + 1, 1 - par)
                            silu_x(b + 1)
                        if n == 8:
                            abs_dt(b + 1)
                            relu_dt(b + 1)
                        if n == 9:
                            evacuate_bc(b + 1)
                            exp_dt(b + 1)
                            ln_dt(b + 1)
                        if n == 10:
                            round_bc(b + 1, 1 - par)

            rows(act, body)

            def round_weights(pieces):
                for i in pieces:
                    act.wait_ge(prep_in, i + 1)
                    width = preps[i][2]
                    nc.scalar.copy(prep_part(i, 0), prep_shape(i, prep_bank(i)[:, 0:width])).then_inc(prep_hi, 1)

            act.wait_ge(state_ready, B * N)
            for pieces in stages[0:3]:
                round_weights(pieces)
            row_ln(B - 1)
            row_rstd(B - 1)
            round_weights(stages[3])
            evacuate_x1(B - 1)
            round_weights(stages[4])

            def round_x(s, p):
                wait(act, xt_in, s + 1)
                nc.scalar.copy(x_hi[:, p, :], ps_xt).then_inc(xhi_ready, 1)

            def silu_hidden(s, p):
                wait(act, h1_in, s + 1)
                nc.scalar.activation(act1[:, p, :], ps_h1[:, 0:H], ACT.Silu).then_inc(silu_ready, 1)

            def round_hidden(s, p):
                wait(act, ht_in, s + 1)
                nc.scalar.copy(hid_hi[:, p, :], ps_ht[p]).then_inc(hthi_ready, 1)

            def save_slot(s, r):
                wait(act, ys_ready, s + 1)
                act.dma_start(y_sorted[bass.ds(s * P, P)], y_slot[:, r, :]).then_inc(y_saved[r], 16)

            act.preload_act_table(ACT.Silu)
            round_x(0, 0)

            def slot(s, r, turn, at, first, last):
                silu_hidden(s, r % 2)
                if not last:
                    round_x(s + 1, (r + 1) % 2)
                if not first:
                    round_hidden(s - 1, (r - 1) % 2)
                if not isinstance(s, int) or s >= 3:
                    save_slot(s - 3, (r - 3) % RING)

            all_slots(act, slot)
            round_hidden(S - 1, (S - 1) % 2)
            for s in (S - 3, S - 2, S - 1):
                save_slot(s, s % RING)

            act.preload_act_table_set(EXP_LN)
            nc.scalar.activation(gate2[:], gap[:], ACT.Exp).then_inc(gate_step, 1)

            def scale_first(b):
                if b == 0:
                    act.wait_ge(gate_step, 3)
                act.wait_ge(y_gathered[b], 16 * 2 * NT)
                for j in range(b * NT, (b + 1) * NT):
                    ins = nc.scalar.activation(y_got[0][:, j, :], y_got[0][:, j, :], ACT.Copy, scale=gate1[:, j:j + 1])
                ins.then_inc(mix_scaled, 1)

            def mix_deviation(b):
                p = b % 2
                act.wait_ge(mix_step, MIX * (b + 1))
                nc.scalar.activation(mix_lnv[:, p, :], mix_var[:, p, :], ACT.Ln, bias=eps_c[:], scale=1.0 / P).then_inc(mix_ln, 1)
                act.wait_ge(mix_ln, b + 1)
                nc.scalar.activation(mix_rs[:, p, :], mix_lnv[:, p, :], ACT.Exp, scale=-0.5).then_inc(mix_rstd, 1)

            def mix_normalise(b):
                act.wait_ge(mix_off_ready, b + 1)
                for j in range(NT if b < B - 1 else NT // 2):
                    ins = nc.scalar.activation(x1[:, b * NT + j, :], x1[:, b * NT + j, :], ACT.Identity,
                                               bias=mix_off[:, b % 2, j:j + 1], scale=mix_rs[:, b % 2, j:j + 1])
                ins.then_inc(mix_ready, 1)

            scale_first(0)
            for b in range(B):
                if b + 1 < B - 1:
                    scale_first(b + 1)
                if b:
                    mix_normalise(b - 1)
                mix_deviation(b)
                if b + 1 == B - 1:
                    scale_first(b + 1)
            mix_normalise(B - 1)

        @block.vector
        def _(dve):
            def conv(b, part=None):
                if part != 1:
                    conv_two(b)
                if part != 0:
                    conv_last(b)

            def conv_two(b):
                wait(dve, xpad_ready, b + 1)
                wait(dve, dtx_ready, b)
                wait(dve, bc_in, b)
                nc.vector.tensor_scalar(xs[:], x_pad[:, 0:T], cw[:, 0:1], cb[:], ALU.mult, ALU.add).then_inc(conv_part, 1)
                wait(dve, conv_part, 2 * b + 1)
                nc.vector.scalar_tensor_tensor(out=xs[:], in0=x_pad[:, 1:T + 1], scalar=cw[:, 1:2], in1=xs[:],
                                               op0=ALU.mult, op1=ALU.add).then_inc(conv_part, 1)

            def conv_last(b):
                wait(dve, conv_part, 2 * b + 2)
                nc.vector.scalar_tensor_tensor(out=xs[:], in0=x_pad[:, 2:T + 2], scalar=cw[:, 2:3], in1=xs[:],
                                               op0=ALU.mult, op1=ALU.add).then_inc(conv_ready, 1)

            def sum_dt(b, par):
                wait(dve, dtln_ready, b + 1)
                wait(dve, dtrelu_ready, b + 1)
                wait(dve, dtx_ready, b - 1)
                wait(dve, decay_ready, (b - 1) * N)
                nc.vector.tensor_tensor(dt[par][:], dt_relu[:], dt_abs[:], ALU.add).then_inc(dt_ready, 1)

            def mul_dtx(b, par):
                wait(dve, dt_ready, b + 1)
                wait(dve, drive_ready, (b - 1) * (2 * N))
                nc.vector.tensor_tensor(dtx[par][:], dt[par][:], xs[:], ALU.mult).then_inc(dtx_ready, 1)

            def low_bc(b, par):
                wait(dve, bchi_ready, b + 1)
                lo = slice(2 * N, 4 * N)
                nc.vector.tensor_tensor(bc_split[par][lo, :], bc_val[lo, :], bc_split[par][lo, :].bitcast(F32),
                                        ALU.subtract).then_inc(bclo_ready, 1)

            def drive_of(b, par, n):
                g = b * N + n
                if n == 0:
                    wait(dve, dtx_ready, b + 1)
                if not isinstance(g, int) or g >= RING:
                    wait(dve, prod_ready, g - RING + 1)
                for h, s in enumerate(HALVES):
                    wait(dve, bB_ready, b * (2 * N) + (2 * n + h + 1))
                    nc.vector.tensor_tensor(state[:, n % RING, s], dtx[par][:, s], ps_b[:, s], ALU.mult).then_inc(drive_ready, 1)

            def scan(b, n):
                g = b * N + n
                wait(dve, drive_ready, b * (2 * N) + (2 * n + 2))
                wait(dve, decay_ready, g + 1)
                nc.vector.tensor_tensor_scan(state[:, n % RING, :], decay[:, n % RING, :], state[:, n % RING, :], 0.0,
                                             ALU.mult, ALU.add).then_inc(state_ready, 1)

            def gate_y(b, par):
                wait(dve, y_added, (b + 1) * N)
                wait(dve, z_ready, b + 1)
                wait(dve, logit_in, b)
                for s in HALVES:
                    nc.vector.tensor_tensor(yz[:, s], ps_y[:, s], z[par][:, s], ALU.mult).then_inc(yz_ready, 1)

            def residual(b, par):
                wait(dve, out_in, b + 1)
                wait(dve, ures_loaded, (b + 1) * 16)
                nc.vector.tensor_tensor(res[:].rearrange("p n d -> p (n d)"), ps_s[:],
                                        u_res[:].rearrange("p n d -> p (n d)"), ALU.add).then_inc(res_ready, 1)

            def statistics(b):
                wait(dve, res_ready, b + 1)
                for j in range(NT):
                    ins = nc.vector.bn_stats(stats[:, j, :], res[:, j, :])
                ins.then_inc(stats_ready, 1)

            def aggregate(b):
                wait(dve, stats_ready, b + 1)
                nc.vector.tensor_tensor(mean[:], stats[:, :, 1], stats[:, :, 4], ALU.add)
                nc.vector.tensor_tensor(dif[:], stats[:, :, 1], stats[:, :, 4], ALU.subtract)
                nc.vector.tensor_tensor(sq[:], stats[:, :, 2], stats[:, :, 5], ALU.add).then_inc(agg_part, 1)
                wait(dve, agg_part, 3 * b + 1)
                nc.vector.tensor_scalar(mean[:], mean[:], 0.5, None, ALU.mult)
                nc.vector.tensor_tensor(dif[:], dif[:], dif[:], ALU.mult).then_inc(agg_part, 1)
                wait(dve, agg_part, 3 * b + 2)
                nc.vector.scalar_tensor_tensor(out=var[:], in0=dif[:], scalar=P / 4.0, in1=sq[:],
                                               op0=ALU.mult, op1=ALU.add).then_inc(agg_part, 1)

            def normalise(b, par, part=None):
                wait(dve, rstd_ready, b + 1)
                if isinstance(b, int) and b == B - 1:
                    g = group_of[b - 2]
                    dve.wait_ge(scattered[g][par], 16 * 2 * NT * sum(group_of[k] == g for k in range(par, b, 2)))
                else:
                    wait(dve, prod_ready, (b + 1) * N + 3)
                for j in range(NT) if part is None else range(part * NT // 2, (part + 1) * NT // 2):
                    ins = nc.vector.tensor_scalar(x1_row[par][:, j, :], res[:, j, :], mean[:, j:j + 1], rstd[:, j:j + 1],
                                                  ALU.subtract, ALU.mult)
                if part != 0:
                    ins.then_inc(x1_ready, 1)

            by_tile = lambda t: t[:].rearrange("p e j -> p j e")
            each_expert = lambda t: t[:].unsqueeze(1).broadcast_to([P, E, NT])
            each_tile = lambda t: t[:].unsqueeze(2).broadcast_to([P, E, NT])
            flat = lambda t: t[:].rearrange("p e j -> p (e j)")

            def choose(b, part=None):
                k = [6 if part == 1 else 0]

                def link(ins):
                    k[0] += 1
                    ins.then_inc(route_step, 1)
                    wait(dve, route_step, b * ROUTE + k[0])

                def pick_top(values, top, dst):
                    link(nc.vector.tensor_reduce(dst[:], by_tile(values), AX.X, ALU.max))
                    link(nc.vector.tensor_tensor(top[:], values[:], each_expert(dst), ALU.is_equal))
                    link(nc.vector.tensor_tensor(top[:], top[:], first_high[:], ALU.mult))
                    link(nc.vector.tensor_reduce(index[:], by_tile(top), AX.X, ALU.max))
                    link(nc.vector.tensor_tensor(top[:], first_high[:], each_expert(index), ALU.is_equal))

                if part != 1:
                    wait(dve, logit_in, b + 1)
                    ins = nc.vector.tensor_copy(logit[:], ps_s[:, 0:E * NT].rearrange("p (j e) -> p e j", e=E))
                    ins.then_inc(logit_ready, 1)
                    wait(dve, logit_ready, b + 1)
                    pick_top(logit, top1, best)
                    link(nc.vector.scalar_tensor_tensor(out=flat(logit2), in0=flat(top1), scalar=-3.0e38, in1=flat(logit),
                                                        op0=ALU.mult, op1=ALU.add))
                if part == 0:
                    return
                pick_top(logit2, top2, best2)
                nc.vector.tensor_tensor(gap[:, bass.ds(b * NT, NT)], best2[:], best[:], ALU.subtract)
                link(nc.vector.tensor_tensor(chosen[:], top1[:], top2[:], ALU.add))
                link(nc.vector.tensor_tensor_scan(running[:, 1:], ones[:, 0:E * NT], flat(chosen), 0.0, ALU.mult, ALU.add))
                nc.vector.tensor_tensor(count[:], running[:, NT::NT], running[:, 0:E * NT:NT], ALU.subtract).then_inc(count_ready, 1)
                assert k[0] == ROUTE - 8

            def locate(b, par):
                g = group(b)
                k = [ROUTE - 8]

                def link(ins):
                    k[0] += 1
                    ins.then_inc(route_step, 1)
                    wait(dve, route_step, b * ROUTE + k[0])

                wait(dve, count_ready, b + 1)
                link(nc.vector.tensor_tensor(offset[:], base[g][:], running[:, 0:E * NT:NT], ALU.subtract))
                wait(dve, rank_in, b + 1)
                link(nc.vector.tensor_tensor(offset[:], offset[:], ps_s[:, 0:E], ALU.add))
                nc.vector.tensor_tensor(base[g][:], base[g][:], ps_s[:, E:2 * E], ALU.add).then_inc(rank_drained, 1)
                link(nc.vector.tensor_tensor(flat(rank), running[:, 1:], flat(chosen), ALU.subtract))
                link(nc.vector.tensor_tensor(rank[:], rank[:], each_tile(offset), ALU.add))
                for i, top in enumerate((top1, top2)):
                    link(nc.vector.tensor_tensor(part[:], top[:], rank[:], ALU.mult))
                    link(nc.vector.tensor_reduce(place_f[:, i, :], by_tile(part), AX.X, ALU.add))
                nc.vector.tensor_copy(place[par][:], place_f[:])
                nc.vector.tensor_copy(places[:, :, bass.ds(b * NT, NT)], place_f[:]).then_inc(place_ready, 1)
                assert k[0] == ROUTE

            def tables(g, part=None):
                n, o, k = slots[g], first_slot[g], [g * TABLE + (0, 7, 11)[part or 0]]

                def link(ins):
                    k[0] += 1
                    ins.then_inc(table_step, 1)
                    dve.wait_ge(table_step, k[0])

                number, one = slot_no[:, 0:n], slice(0, 1)
                by_slot = lambda t: t[one, :].unsqueeze(1).broadcast_to([1, n, E])
                if part in (None, 0):
                    dve.wait_ge(rank_drained, sum(k <= g for k in group_of))
                    link(nc.vector.tensor_tensor(pad_place[g][:], base[g][:], lane[:].broadcast_to([P, E]), ALU.add))
                    link(nc.vector.tensor_tensor(n_tiles[:], base[g][:], base_from[g][:], ALU.subtract))
                    link(nc.vector.tensor_scalar(n_tiles_i[:], n_tiles[:], float(P - 1), None, ALU.add))
                    link(nc.vector.tensor_scalar(n_tiles_i[:], n_tiles_i[:], 7, None, ALU.logical_shift_right))
                    link(nc.vector.tensor_copy(n_tiles[:], n_tiles_i[:]))
                    link(nc.vector.tensor_tensor_scan(done_at[:], ones_e[:], n_tiles[:], 0.0, ALU.mult, ALU.add))
                    link(nc.vector.tensor_scalar(skip[g][:], n_tiles[:], -1.0, float(region[g] // P), ALU.mult, ALU.add))
                if part in (None, 1):
                    link(nc.vector.tensor_tensor(passed[:, 0:n, :], number.unsqueeze(2).broadcast_to([1, n, E]), by_slot(done_at), ALU.is_ge))
                    link(nc.vector.tensor_reduce(t_expert[:, 0:n], passed[:, 0:n, :], AX.X, ALU.add))
                    link(nc.vector.tensor_tensor(passed[:, 0:n, :], passed[:, 0:n, :], by_slot(skip[g]), ALU.mult))
                    link(nc.vector.tensor_reduce(t_tile[:, 0:n], passed[:, 0:n, :], AX.X, ALU.add))
                if part in (None, 2):
                    link(nc.vector.tensor_scalar(t_used[:, 0:n], number, done_at[one, E - 1:E], None, ALU.is_lt))
                    link(nc.vector.tensor_tensor(slot_expert[:, o:o + n], t_expert[:, 0:n], t_used[:, 0:n], ALU.mult))
                    link(nc.vector.scalar_tensor_tensor(out=t_tile[:, 0:n], in0=t_tile[:, 0:n], scalar=float(first_tile[g]), in1=number,
                                                        op0=ALU.add, op1=ALU.add))
                    link(nc.vector.scalar_tensor_tensor(out=t_tile[:, 0:n], in0=t_tile[:, 0:n], scalar=-float(first_tile[g]),
                                                        in1=t_used[:, 0:n], op0=ALU.add, op1=ALU.mult))
                    link(nc.vector.tensor_scalar(slot_from[:, o:o + n], t_tile[:, 0:n], float(first_tile[g]), None, ALU.add))
                    assert k[0] == (g + 1) * TABLE
                    nc.vector.tensor_copy(t_tile[:, 0:1], number[:, 0:1]).then_inc(table_ready, 1)

            dve.wait_ge(first_loaded, FIRST)
            conv(0)
            dve.wait_ge(const_ready, PICKED)
            nc.vector.tensor_copy(pick[:], prod[0:4 * N, :, :].rearrange("q a (r m) -> q (a r) m", m=P)).then_inc(pick_ready, 1)
            dve.wait_ge(w_loaded, WEIGHTS)
            dve.wait_ge(const_ready, CONSTANTS)
            dve.wait_ge(bout_hi, 1)
            nc.vector.tensor_tensor(bout_r[TWO:, :], bout_v[TWO:, :], bout_r[TWO:, :].bitcast(F32), ALU.subtract)
            low_bc(0, 0)
            sum_dt(0, 0)
            mul_dtx(0, 0)

            def body(b, par, first, last):
                for n in range(N):
                    drive_of(b, par, n)
                    if n == LAG and not first:
                        gate_y(b - 1, 1 - par)
                    if n:
                        scan(b, n - 1)
                    elif not first:
                        scan(b - 1, N - 1)
                    if not first:
                        if n == 6:
                            residual(b - 1, 1 - par)
                        if n == 7:
                            statistics(b - 1)
                            aggregate(b - 1)
                        if n == 9:
                            normalise(b - 1, 1 - par)
                        if n == 12:
                            choose(b - 1, 0)
                        if n == 13:
                            choose(b - 1, 1)
                        if n == 15:
                            locate(b - 1, 1 - par)
                    if last and n == 1:
                        tables(0)
                    if not last:
                        if n in (3, 4):
                            conv(b + 1, n - 3)
                        if n == 10:
                            sum_dt(b + 1, 1 - par)
                        if n == 11:
                            low_bc(b + 1, 1 - par)
                        if n == 14:
                            mul_dtx(b + 1, 1 - par)

            rows(dve, body)

            def low_weights(pieces):
                for i in pieces:
                    dve.wait_ge(prep_hi, i + 1)
                    width = preps[i][2]
                    nc.vector.tensor_tensor(prep_part(i, 1), prep_shape(i, prep_bank(i)[:, 0:width]), prep_part(i, 0).bitcast(F32),
                                            ALU.subtract).then_inc(prep_lo, 1)

            scan(B - 1, N - 1)
            low_weights(stages[0])
            gate_y(B - 1, 1)
            low_weights(stages[1])
            residual(B - 1, 1)
            statistics(B - 1)
            aggregate(B - 1)
            low_weights(stages[2])
            normalise(B - 1, 1)
            low_weights(stages[3])
            for w in w1 + w2:
                nc.vector.memset(w[:, E * H:].bitcast(F32), 0.0)
            nc.vector.memset(hid[:, :, H:HP], 0.0)
            low_weights(stages[4])
            choose(B - 1)
            locate(B - 1, 1)

            def low_x(s, p):
                wait(dve, xhi_ready, s + 1)
                nc.vector.tensor_tensor(x_lo[:, p, :], ps_xt, x_hi[:, p, :].bitcast(F32), ALU.subtract).then_inc(xlo_ready, 1)

            def multiply(s, p):
                wait(dve, silu_ready, s + 1)
                wait(dve, h2_in, s + 1)
                nc.vector.tensor_tensor(hid[:, p, 0:H], act1[:, p, :], ps_h2[:, 0:H], ALU.mult).then_inc(hid_ready, 1)

            def low_hidden(s, p):
                wait(dve, hthi_ready, s + 1)
                nc.vector.tensor_tensor(hid_lo[:, p, :], ps_ht[p], hid_hi[:, p, :].bitcast(F32), ALU.subtract).then_inc(htlo_ready, 1)

            def evacuate_y(s, r, turn):
                wait(dve, yo_in, s + 1)
                wait(dve, y_saved[r], turn * 16)
                nc.vector.tensor_reduce(y_slot[:, r, :], ps_yo.rearrange("p (i d) -> p d i", i=2), AX.X, ALU.add).then_inc(ys_ready, 1)

            low_x(0, 0)

            def slot(s, r, turn, at, first, last):
                if not last:
                    low_x(s + 1, (r + 1) % 2)
                multiply(s, r % 2)
                if isinstance(s, int) and s < 3:
                    tables(G - 1, s)
                if not first:
                    low_hidden(s - 1, (r - 1) % 2)
                if not isinstance(s, int) or s >= 2:
                    evacuate_y(s - 2, (r - 2) % RING, turn - (1 if r < 2 else 0))

            all_slots(dve, slot)
            low_hidden(S - 1, (S - 1) % 2)
            for s in (S - 2, S - 1):
                evacuate_y(s, s % RING, s // RING)

            dve.wait_ge(x1_loaded, 16)

            dve.wait_ge(gate_step, 1)
            nc.vector.tensor_scalar(gate1[:], gate2[:], 1.0, None, ALU.add).then_inc(gate_step, 1)
            dve.wait_ge(gate_step, 2)
            nc.vector.reciprocal(gate1[:], gate1[:]).then_inc(gate_step, 1)
            dve.wait_ge(gate_step, 3)
            nc.vector.tensor_tensor(gate2[:], gate2[:], gate1[:], ALU.mult).then_inc(gate_step, 1)
            dve.wait_ge(gate_step, 4)

            def weigh(b):
                wait(dve, y_gathered[b], 16 * 2 * NT)
                for j in range(b * NT, (b + 1) * NT):
                    ins = nc.vector.scalar_tensor_tensor(out=x1[:, j, :], in0=y_got[1][:, j, :], scalar=gate2[:, j:j + 1],
                                                         in1=x1[:, j, :], op0=ALU.mult, op1=ALU.add)
                ins.then_inc(mix_step, 1)

            def mix(b):
                at, rows_ = MIX * b, slice(b * NT, (b + 1) * NT)
                dve.wait_ge(mix_step, at + 1)
                dve.wait_ge(mix_scaled, b + 1)
                nc.vector.tensor_tensor(x1[:, rows_, :], x1[:, rows_, :], y_got[0][:, rows_, :], ALU.add).then_inc(mix_step, 1)
                dve.wait_ge(mix_step, at + 2)
                for j in range(NT):
                    ins = nc.vector.bn_stats(stats[:, j, :], x1[:, b * NT + j, :])
                ins.then_inc(mix_step, 1)

            def mix_statistics(b):
                at, p = MIX * b + 3, b % 2
                dve.wait_ge(mix_step, at)
                wait(dve, mix_ln, b - 1)
                nc.vector.tensor_tensor(mix_mean[:, p, :], stats[:, :, 1], stats[:, :, 4], ALU.add)
                nc.vector.tensor_tensor(dif[:], stats[:, :, 1], stats[:, :, 4], ALU.subtract)
                nc.vector.tensor_tensor(sq[:], stats[:, :, 2], stats[:, :, 5], ALU.add).then_inc(mix_step, 1)
                dve.wait_ge(mix_step, at + 1)
                nc.vector.tensor_tensor(dif[:], dif[:], dif[:], ALU.mult).then_inc(mix_step, 1)
                dve.wait_ge(mix_step, at + 2)
                nc.vector.scalar_tensor_tensor(out=mix_var[:, p, :], in0=dif[:], scalar=P / 4.0, in1=sq[:],
                                               op0=ALU.mult, op1=ALU.add).then_inc(mix_step, 1)

            def mix_offset(b):
                wait(dve, mix_rstd, b + 1)
                wait(dve, mix_ready, b - 1)
                nc.vector.scalar_tensor_tensor(out=mix_off[:, b % 2, :], in0=mix_mean[:, b % 2, :], scalar=-0.5,
                                               in1=mix_rs[:, b % 2, :], op0=ALU.mult, op1=ALU.mult).then_inc(mix_off_ready, 1)

            for b in range(B):
                if b == B - 1:
                    mix_offset(b - 1)
                weigh(b)
                if 0 < b < B - 1:
                    mix_offset(b - 1)
                mix(b)
                mix_statistics(b)
            mix_offset(B - 1)
            dve.wait_ge(mix_off_ready, B)
            p = (B - 1) % 2
            for j in range(NT // 2, NT):
                tile = x1[:, (B - 1) * NT + j, :]
                ins = nc.vector.tensor_scalar(tile, tile, mix_rs[:, p, j:j + 1], mix_off[:, p, j:j + 1], ALU.mult, ALU.add)
            ins.then_inc(mix_ready, 1)


_INS = ['L0_attn_u', 'L0_attn_Win', 'L0_attn_b_in', 'L0_attn_Wg', 'L0_attn_bg', 'L0_attn_Wout', 'L0_attn_bout',
        'L0_attn_convw', 'L0_attn_convb', 'L0_attn_A', 'L0_attn_Wb', 'L0_attn_bb', 'L0_attn_Wc', 'L0_attn_bc',
        'L0_attn_Wdt', 'L0_attn_bdt', 'L0_ffn_Wg', 'L0_ffn_W1', 'L0_ffn_W2', 'L0_ffn_W3']


def kernel(**inputs):
    import numpy as _np
    import concourse.bacc as _bacc
    from concourse import mybir as _mybir
    from concourse.bass_utils import run_bass_kernel_spmd as _run

    nc = _bacc.Bacc("TRN2", target_bir_lowering=False, num_devices=1)
    arrays, args = {}, []
    for name in _INS:
        a = _np.ascontiguousarray(inputs[name])
        arrays[f"in_{name}_dram"] = a
        args.append(nc.dram_tensor(f"in_{name}_dram", a.shape, _mybir.dt.from_np(a.dtype), kind="ExternalInput").ap())
    args.append(nc.dram_tensor("out_0_dram", (8, 1024, 128), _mybir.dt.float32, kind="ExternalOutput").ap())
    build(nc, *args)
    r = _run(nc, [arrays], core_ids=[0])
    return r.results[0]["out_0_dram"]
```
